# Optimizing a Trainium2 kernel written in Bass

```python
import numpy as np
import jax
import jax.numpy as jnp

def _softmax(x, axis=-1):
    return jax.nn.softmax(x, axis=axis)

def _gelu(x):
    return jax.nn.gelu(x, approximate=True)

def _silu(x):
    return jax.nn.silu(x)

def _sigmoid(x):
    return jax.nn.sigmoid(x)

def _layernorm(x, axis=-1, eps=1e-05):
    m = jnp.mean(x, axis=axis, keepdims=True)
    v = jnp.var(x, axis=axis, keepdims=True)
    return (x - m) / jnp.sqrt(v + eps)

def _scatter_add(tgt, idx, src, axis=0):
    return tgt.at[idx].add(src)

def _segment_sum(src, seg, n):
    return jax.ops.segment_sum(src, seg, n)
kernel_name = 'mk_seq_preln_d2_jaxref_r4_a160ed'

def setup_inputs(seed: int=0):
    np.random.seed(seed)
    _w = jnp.asarray

    def _L0_attn_setup():
        import jax, jax.numpy as jnp
        import numpy as np
        B, T, C = (4, 1024, 256)
        H = 16
        D = C // H
        EPS = 1e-06

        def _phi(x):
            return jax.nn.elu(x) + 1.0
        key = jax.random.key(seed)
        k1, k2, k3 = jax.random.split(key, 3)
        x = jax.random.normal(k1, (B, T, C), dtype=jnp.float32)
        Wqkv = jax.random.normal(k2, (3 * C, C), dtype=jnp.float32) * (1.0 / np.sqrt(C))
        Wproj = jax.random.normal(k3, (C, C), dtype=jnp.float32) * (1.0 / np.sqrt(C))
        bproj = jnp.zeros((C,), dtype=jnp.float32)
        return {'x': x, 'Wqkv': Wqkv, 'Wproj': Wproj, 'bproj': bproj}
    _L0_attn_in = _L0_attn_setup()

    def _L0_ffn_setup():
        import jax, jax.numpy as jnp
        import numpy as np
        B, S, D, F, E, K = (2, 512, 256, 256, 8, 2)
        key = jax.random.key(seed)
        kx, kg, k1, k3, k2 = jax.random.split(key, 5)
        x = jax.random.normal(kx, (B, S, D), dtype=jnp.float32)
        gate_w = jax.random.uniform(kg, (E, D), jnp.float32, -1.0, 1.0) / np.sqrt(D)
        w1 = jax.random.uniform(k1, (E, F, D), jnp.float32, -1.0, 1.0) / np.sqrt(D)
        w3 = jax.random.uniform(k3, (E, F, D), jnp.float32, -1.0, 1.0) / np.sqrt(D)
        w2 = jax.random.uniform(k2, (E, D, F), jnp.float32, -1.0, 1.0) / np.sqrt(F)
        return {'x': x, 'gate_w': gate_w, 'w1': w1, 'w3': w3, 'w2': w2}
    _L0_ffn_in = _L0_ffn_setup()

    def _L1_attn_setup():
        import jax, jax.numpy as jnp
        import numpy as np
        EPS = 1e-06
        N_HEADS = 16

        def _inner(x, y):
            return -x[..., 0] * y[..., 0] + jnp.sum(x[..., 1:] * y[..., 1:], axis=-1)

        def _project(x):
            sp = jnp.clip(x[..., 1:], -8.0, 8.0)
            x0 = jnp.sqrt(1.0 + jnp.sum(sp ** 2, axis=-1, keepdims=True) + EPS)
            return jnp.concatenate([x0, sp], axis=-1)

        def _exp_map(x, v):
            vx = _inner(v, x)[..., None]
            v_tan = v + vx * x
            v_ns = jnp.maximum(_inner(v_tan, v_tan), 0.0)
            v_n = jnp.minimum(jnp.sqrt(v_ns + EPS)[..., None], 5.0)
            res = jnp.cosh(v_n) * x + jnp.sinh(v_n) * v_tan / (v_n + EPS)
            return _project(res)

        def _log_map(x, y):
            y = _project(y)
            xy = jnp.minimum(_inner(x, y)[..., None], -(1.0 + EPS))
            d = jnp.maximum(jnp.arccosh(jnp.maximum(-xy, 1.0 + EPS)), 0.001)
            direc = y + xy * x
            dn = jnp.sqrt(jnp.maximum(_inner(direc, direc), EPS))[..., None]
            return d * direc / (dn + EPS)
        key = jax.random.key(seed)
        ks = jax.random.split(key, 5)
        B, T, d = (2, 256, 256)
        x = jax.random.normal(ks[0], (B, T, d), dtype=jnp.float32)
        s = 0.02
        Wq = jax.random.normal(ks[1], (d, d), dtype=jnp.float32) * s
        Wk = jax.random.normal(ks[2], (d, d), dtype=jnp.float32) * s
        Wv = jax.random.normal(ks[3], (d, d), dtype=jnp.float32) * s
        Wo = jax.random.normal(ks[4], (d, d), dtype=jnp.float32) * s
        return {'x': x, 'Wq': Wq, 'Wk': Wk, 'Wv': Wv, 'Wo': Wo}
    _L1_attn_in = _L1_attn_setup()

    def _L1_ffn_setup():
        import jax, jax.numpy as jnp
        import numpy as np
        E = 8
        K = 2
        D = 256
        H = 684
        B, S = (2, 512)

        def _moe_forward(x, centroid, Wg, bg, W1, b1, W2, b2):
            T = x.shape[0] * x.shape[1]
            xs = x.reshape(T, D)
            d2 = jnp.sum(xs * xs, axis=-1, keepdims=True) + jnp.sum(centroid * centroid, axis=-1)[None, :] - 2.0 * (xs @ centroid.T)
            dist = jnp.sqrt(jnp.maximum(d2, 1e-12))
            w, sel = jax.lax.top_k(dist, K)
            w = jax.nn.softmax(w.astype(jnp.float32), axis=1).astype(x.dtype)
            we = jnp.zeros((T, E), dtype=x.dtype).at[jnp.arange(T)[:, None], sel].add(w)
            out = jnp.zeros_like(xs)
            for e in range(E):
                h = jax.nn.silu(xs @ Wg[e] + bg[e]) * (xs @ W1[e] + b1[e])
                out = out + we[:, e:e + 1] * (h @ W2[e] + b2[e])
            return out.reshape(x.shape)
        key = jax.random.key(seed)
        ks = jax.random.split(key, 9)
        scale = 0.02
        return {'x': jax.random.normal(ks[0], (B, S, D), dtype=jnp.float32), 'centroid': jax.random.normal(ks[1], (E, D), dtype=jnp.float32), 'Wg': jax.random.normal(ks[2], (E, D, H), dtype=jnp.float32) * scale, 'bg': jnp.zeros((E, H), dtype=jnp.float32), 'W1': jax.random.normal(ks[3], (E, D, H), dtype=jnp.float32) * scale, 'b1': jnp.zeros((E, H), dtype=jnp.float32), 'W2': jax.random.normal(ks[4], (E, H, D), dtype=jnp.float32) * scale, 'b2': jnp.zeros((E, D), dtype=jnp.float32)}
    _L1_ffn_in = _L1_ffn_setup()
    _d = {'L0_attn_x': _L0_attn_in['x'], 'L0_attn_Wqkv': _L0_attn_in['Wqkv'], 'L0_attn_Wproj': _L0_attn_in['Wproj'], 'L0_attn_bproj': _L0_attn_in['bproj'], 'L0_ffn_gate_w': _L0_ffn_in['gate_w'], 'L0_ffn_w1': _L0_ffn_in['w1'], 'L0_ffn_w3': _L0_ffn_in['w3'], 'L0_ffn_w2': _L0_ffn_in['w2'], 'L1_attn_Wq': _L1_attn_in['Wq'], 'L1_attn_Wk': _L1_attn_in['Wk'], 'L1_attn_Wv': _L1_attn_in['Wv'], 'L1_attn_Wo': _L1_attn_in['Wo'], 'L1_ffn_centroid': _L1_ffn_in['centroid'], 'L1_ffn_Wg': _L1_ffn_in['Wg'], 'L1_ffn_bg': _L1_ffn_in['bg'], 'L1_ffn_W1': _L1_ffn_in['W1'], 'L1_ffn_b1': _L1_ffn_in['b1'], 'L1_ffn_W2': _L1_ffn_in['W2'], 'L1_ffn_b2': _L1_ffn_in['b2']}
    _x0 = _d['L0_attn_x']
    _d['L0_attn_x'] = jax.random.normal(jax.random.fold_in(jax.random.key(seed), 1), (2, 2048, 256), dtype=_x0.dtype)
    del _x0
    return _d

def reference(L0_attn_x, L0_attn_Wqkv, L0_attn_Wproj, L0_attn_bproj, L0_ffn_gate_w, L0_ffn_w1, L0_ffn_w3, L0_ffn_w2, L1_attn_Wq, L1_attn_Wk, L1_attn_Wv, L1_attn_Wo, L1_ffn_centroid, L1_ffn_Wg, L1_ffn_bg, L1_ffn_W1, L1_ffn_b1, L1_ffn_W2, L1_ffn_b2):

    def _L0_attn_ref(x, Wqkv, Wproj, bproj):
        import jax, jax.numpy as jnp
        import numpy as np
        B, T, C = (4, 1024, 256)
        H = 16
        D = C // H
        EPS = 1e-06

        def _phi(x):
            return jax.nn.elu(x) + 1.0
        b, t, c = x.shape
        qkv = jnp.einsum('btc,ec->bte', x, Wqkv)
        qkv = qkv.reshape(b, t, 3, H, D)
        q, k, v = (qkv[:, :, 0], qkv[:, :, 1], qkv[:, :, 2])
        q = _phi(q)
        k = _phi(k)
        kv = jnp.einsum('bnhd,bnhm->bhdm', k, v)
        k_sum = k.sum(axis=1)
        out = jnp.einsum('bnhd,bhdm->bnhm', q, kv)
        normalizer = jnp.einsum('bnhd,bhd->bnh', q, k_sum) + EPS
        out = out / normalizer[..., None]
        out = out.reshape(b, t, c)
        out = jnp.einsum('btc,oc->bto', out, Wproj) + bproj
        return out

    def _L0_ffn_ref(x, gate_w, w1, w3, w2):
        import jax, jax.numpy as jnp
        import numpy as np
        B, S, D, F, E, K = (2, 512, 256, 256, 8, 2)
        b, s, d = x.shape
        T = b * s
        xf = x.reshape(T, d)
        logits = xf @ gate_w.T
        probs = jax.nn.softmax(logits, axis=-1)
        topk_w, topk_idx = jax.lax.top_k(probs, K)
        topk_w = topk_w / jnp.sum(topk_w, axis=-1, keepdims=True)
        gate_full = jnp.zeros((T, E), x.dtype).at[jnp.arange(T)[:, None], topk_idx].add(topk_w)
        out = jnp.zeros_like(xf)
        for e in range(E):
            h = jax.nn.silu(xf @ w1[e].T) * (xf @ w3[e].T)
            out = out + gate_full[:, e:e + 1] * (h @ w2[e].T)
        return out.reshape(b, s, d)

    def _L1_attn_ref(x, Wq, Wk, Wv, Wo):
        import jax, jax.numpy as jnp
        import numpy as np
        EPS = 1e-06
        N_HEADS = 16

        def _inner(x, y):
            return -x[..., 0] * y[..., 0] + jnp.sum(x[..., 1:] * y[..., 1:], axis=-1)

        def _project(x):
            sp = jnp.clip(x[..., 1:], -8.0, 8.0)
            x0 = jnp.sqrt(1.0 + jnp.sum(sp ** 2, axis=-1, keepdims=True) + EPS)
            return jnp.concatenate([x0, sp], axis=-1)

        def _exp_map(x, v):
            vx = _inner(v, x)[..., None]
            v_tan = v + vx * x
            v_ns = jnp.maximum(_inner(v_tan, v_tan), 0.0)
            v_n = jnp.minimum(jnp.sqrt(v_ns + EPS)[..., None], 5.0)
            res = jnp.cosh(v_n) * x + jnp.sinh(v_n) * v_tan / (v_n + EPS)
            return _project(res)

        def _log_map(x, y):
            y = _project(y)
            xy = jnp.minimum(_inner(x, y)[..., None], -(1.0 + EPS))
            d = jnp.maximum(jnp.arccosh(jnp.maximum(-xy, 1.0 + EPS)), 0.001)
            direc = y + xy * x
            dn = jnp.sqrt(jnp.maximum(_inner(direc, direc), EPS))[..., None]
            return d * direc / (dn + EPS)
        B, T, d = x.shape
        h = N_HEADS
        dh = d // h
        mu = jnp.zeros((d,), dtype=x.dtype).at[0].set(1.0)
        v = _log_map(mu, x)

        def proj_h(w):
            hh = w.reshape(B, T, h, dh)
            sp = jnp.clip(hh[..., 1:], -5.0, 5.0)
            x0 = jnp.sqrt(1.0 + jnp.sum(sp ** 2, axis=-1, keepdims=True) + EPS)
            return jnp.transpose(jnp.concatenate([x0, sp], axis=-1), (0, 2, 1, 3))
        q = proj_h(v @ Wq.T)
        k = proj_h(v @ Wk.T)
        vv = jnp.transpose((v @ Wv.T).reshape(B, T, h, dh), (0, 2, 1, 3))
        sc = (-jnp.einsum('bhqi,bhki->bhqk', q[..., :1], k[..., :1]) + jnp.einsum('bhqc,bhkc->bhqk', q[..., 1:], k[..., 1:])) / dh ** 0.5
        at = jax.nn.softmax(sc, axis=-1)
        out = jnp.einsum('bhqk,bhkc->bhqc', at, vv)
        out = jnp.transpose(out, (0, 2, 1, 3)).reshape(B, T, d)
        return _project(_exp_map(mu, out @ Wo.T))

    def _L1_ffn_ref(x, centroid, Wg, bg, W1, b1, W2, b2):
        import jax, jax.numpy as jnp
        import numpy as np
        E = 8
        K = 2
        D = 256
        H = 684
        B, S = (2, 512)

        def _moe_forward(x, centroid, Wg, bg, W1, b1, W2, b2):
            T = x.shape[0] * x.shape[1]
            xs = x.reshape(T, D)
            d2 = jnp.sum(xs * xs, axis=-1, keepdims=True) + jnp.sum(centroid * centroid, axis=-1)[None, :] - 2.0 * (xs @ centroid.T)
            dist = jnp.sqrt(jnp.maximum(d2, 1e-12))
            w, sel = jax.lax.top_k(dist, K)
            w = jax.nn.softmax(w.astype(jnp.float32), axis=1).astype(x.dtype)
            we = jnp.zeros((T, E), dtype=x.dtype).at[jnp.arange(T)[:, None], sel].add(w)
            out = jnp.zeros_like(xs)
            for e in range(E):
                h = jax.nn.silu(xs @ Wg[e] + bg[e]) * (xs @ W1[e] + b1[e])
                out = out + we[:, e:e + 1] * (h @ W2[e] + b2[e])
            return out.reshape(x.shape)
        return _moe_forward(x, centroid, Wg, bg, W1, b1, W2, b2)
    x = L0_attn_x
    x = x + _L0_attn_ref(_layernorm(x, axis=-1), L0_attn_Wqkv, L0_attn_Wproj, L0_attn_bproj)
    x = x + _L0_ffn_ref(_layernorm(x, axis=-1), L0_ffn_gate_w, L0_ffn_w1, L0_ffn_w3, L0_ffn_w2)
    x = x + _L1_attn_ref(_layernorm(x, axis=-1), L1_attn_Wq, L1_attn_Wk, L1_attn_Wv, L1_attn_Wo)
    x = x + _L1_ffn_ref(_layernorm(x, axis=-1), L1_ffn_centroid, L1_ffn_Wg, L1_ffn_bg, L1_ffn_W1, L1_ffn_b1, L1_ffn_W2, L1_ffn_b2)
    return x

_drawn_inputs = setup_inputs


def setup_inputs(seed=0):
    import zlib

    import numpy as np

    out = dict(_drawn_inputs(seed))
    spreads = {'L0_attn_bproj': (0.0, 0.1),
     'L1_ffn_bg': (0.0, 0.8),
     'L1_ffn_b1': (0.0, 0.8),
     'L1_ffn_b2': (0.0, 0.1)}
    factors = {'L1_attn_Wq': 8.0,
     'L1_attn_Wk': 8.0,
     'L1_attn_Wv': 8.0,
     'L1_attn_Wo': 8.0,
     'L1_ffn_Wg': 2.693,
     'L1_ffn_W1': 2.677}
    for name, (base, spread) in spreads.items():
        noise = np.random.default_rng([zlib.crc32(name.encode()), seed]).standard_normal(out[name].shape)
        drawn = base * np.exp(spread * noise) if base else spread * noise
        out[name] = jnp.asarray(drawn.astype(out[name].dtype))
    for name, factor in factors.items():
        out[name] = (out[name] * factor).astype(out[name].dtype)
    return out
```

```python
from contextlib import ExitStack

import concourse.bass as bass
from concourse import mybir

ALU = mybir.AluOpType
ACT = mybir.ActivationFunctionType
AX = mybir.AxisListType
F32 = mybir.dt.float32
BF16 = mybir.dt.bfloat16
I32 = mybir.dt.int32
U32 = mybir.dt.uint32

P = 128
T, C = 4096, 256
KC = C // P
NT = T // P
NB = 2
TB = NT // NB
TS = T // NB
H, D = 16, 16
E = 8
F0 = 256
F1 = 684
HG, HW = 3, 228
HK, HP = 6, 114
NTILE = 2 * T // P + E
BANK = 512
LN_EPS = 1e-5
EPS = 1e-6
GR = 4
ds = bass.ds


class Serial:

    def __init__(self, eng, sem):
        self.eng, self.sem, self.n = eng, sem, 0

    def __call__(self, ins):
        ins.then_inc(self.sem, 1)
        self.n += 1
        self.eng.wait_ge(self.sem, self.n)


class Stage:

    def __init__(self, nc, name):
        self.nc, self.name, self.stack, self.held = nc, name, ExitStack(), []

    def __enter__(self):
        self.stack.__enter__()
        return self

    def __exit__(self, *a):
        if self.held and a[0] is None:
            self.nc.clear_and_free_semaphores(self.held)
            self.nc.all_engine_barrier()
        return self.stack.__exit__(*a)

    def sb(self, name, shape, dt=F32):
        return self.stack.enter_context(self.nc.sbuf_tensor(f"{self.name}_{name}", shape, dt))

    def ps(self, name, shape, dt=F32):
        return self.stack.enter_context(self.nc.psum_tensor(f"{self.name}_{name}", shape, dt))

    def sem(self, name):
        self.held.append(self.nc.alloc_semaphore(f"{self.name}_{name}"))
        return self.held[-1]

    def sems(self, name, n):
        return [self.sem(f"{name}{i}") for i in range(n)]


class Consts:
    pass


def bc(ap, shape):
    return ap.to_broadcast(shape)


def constants(nc, st, k):
    k.ident = st.sb("ident", [P, P])
    k.identb = st.sb("identb", [P, P], BF16)
    k.ones = st.sb("ones", [P, P])
    k.onesb = st.sb("onesb", [P, P], BF16)
    k.upperb = st.sb("upperb", [P, P], BF16)
    k.blockdiag = st.sb("blockdiag", [P, P])
    k.lane = st.sb("lane", [P, P])
    k.lane1 = st.sb("lane1", [P, 1])
    k.odd_rows = st.sb("odd_rows", [P, NTILE])
    with Stage(nc, "cst") as s:
        tmp = s.sb("tmp", [P, P], I32)
        tcol = s.sb("tcol", [P, 1], I32)
        todd = s.sb("todd", [P, NTILE], I32)
        filled, picked, turned = s.sem("filled"), s.sem("picked"), s.sem("turned")
        with nc.Block() as block:

            @block.gpsimd
            def _(pool):
                pool.memset(k.ident[:, :], 0.0).then_inc(filled, 1)
                pool.memset(k.ones[:, :], 1.0).then_inc(filled, 1)
                pool.memset(k.blockdiag[:, :], 1.0).then_inc(filled, 1)
                pool.iota(tmp[:, :], pattern=[[1, P]], base=0, channel_multiplier=0).then_inc(filled, 1)
                pool.iota(tcol[:, :], pattern=[[1, 1]], base=0, channel_multiplier=1).then_inc(filled, 1)
                pool.iota(todd[:, :].rearrange("p (a b) -> p a b", b=2), pattern=[[0, NTILE // 2], [P, 2]], base=0,
                          channel_multiplier=0).then_inc(filled, 1)
                pool.wait_ge(filled, 6)
                pool.affine_select(out=k.ident[:, :], in_=k.ident[:, :], compare_op=ALU.not_equal, fill=1.0,
                                   base=0, pattern=[[-1, P]], channel_multiplier=1).then_inc(picked, 1)
                pool.affine_select(out=k.upperb[:, :], in_=k.ones[:, :], compare_op=ALU.is_gt, fill=0.0,
                                   base=0, pattern=[[1, P]], channel_multiplier=-1).then_inc(picked, 1)
                bd = k.blockdiag[:, :].rearrange("p (h d) -> p h d", d=D)
                pool.affine_select(out=bd, in_=bd, compare_op=ALU.is_ge, fill=0.0,
                                   base=0, pattern=[[-D, P // D], [0, D]], channel_multiplier=1).then_inc(picked, 1)
                pool.wait_ge(picked, 3)
                pool.affine_select(out=bd, in_=bd, compare_op=ALU.is_ge, fill=0.0,
                                   base=D - 1, pattern=[[D, P // D], [0, D]], channel_multiplier=-1).then_inc(picked, 1)

            @block.vector
            def _(dve):
                dve.wait_ge(filled, 6)
                dve.tensor_copy(k.lane[:, :], tmp[:, :]).then_inc(turned, 1)
                dve.tensor_copy(k.odd_rows[:, :], todd[:, :]).then_inc(turned, 1)
                dve.tensor_copy(k.lane1[:, :], tcol[:, :]).then_inc(turned, 1)
                dve.tensor_copy(k.onesb[:, :], k.ones[:, :]).then_inc(turned, 1)
                dve.wait_ge(picked, 3)
                dve.tensor_copy(k.identb[:, :], k.ident[:, :]).then_inc(turned, 1)


def transpose_squares(nc, k, name, squares, small, looped=None):
    RING = 6
    with Stage(nc, name) as s:
        raw = s.sb("raw", [P, RING, KC, C])
        rawsm = s.sb("rawsm", [E, max(len(small), 1), C])
        ps = s.ps("ps", [P, RING, KC * C])
        pss = s.ps("pss", [P, BANK])
        loaded = s.sems("loaded", RING)
        sm_loaded = s.sem("sm_loaded")
        turned, out_dve, out_act, sm_turned, sm_out = (s.sem(x) for x in ("turned", "odve", "oact", "smt", "smo"))
        n0 = len(squares)
        per = len(looped[1]) if looped else 0
        steps = looped[0] * per // RING if looped else 0
        assert not looped or (looped[0] * per) % RING == 0 and RING % per == 0

        def rows(src):
            return src.rearrange("(b p) c -> p b c", p=P)

        def target(i, m, n):
            if m is None:
                return squares[n][1]
            e = i * (RING // per) + m // per
            return looped[2][m % per](e)

        def walk(eng, step):
            for n in range(n0):
                step(None, None, n, n % RING, n // RING)
            if looped:
                with eng.Fori(0, steps) as i:
                    for m in range(RING):
                        n = n0 + m
                        step(i, m, n, n % RING, i + n // RING)

        def again(eng, sem, per_lap, lap, n, extra=0):
            eng.wait_ge(sem, per_lap)

        with nc.Block() as block:

            @block.sync
            def _(sp):
                for j, (src, _) in enumerate(small):
                    sp.dma_start(rawsm[:, j, :], src).then_inc(sm_loaded, 16)

                def load(i, m, n, slot, lap):
                    if m is None:
                        src = squares[n][0]
                    else:
                        src = looped[1][m % per](i * (RING // per) + m // per)
                    if m is not None or n >= RING:
                        sp.wait_ge(turned, (i * RING if m is not None else 0) + n + 1)
                    sp.dma_start(raw[:, slot, :, :], rows(src)).then_inc(loaded[slot], 16)

                walk(sp, load)

            @block.tensor
            def _(pe):
                pe.sem_inc(turned, RING)

                def turn(i, m, n, slot, lap):
                    pe.wait_ge(loaded[slot], lap * 16 + 16)
                    if m is not None or n >= RING:
                        par = out_dve if n % 2 == 0 else out_act
                        pe.wait_ge(par, (i * (RING // 2) if m is not None else 0) + n // 2 + 1)
                    for kk in range(KC):
                        for b in range(KC):
                            mm = pe.transpose(ps[:, slot, kk * C + b * P:kk * C + (b + 1) * P],
                                              raw[:, slot, b, kk * P:(kk + 1) * P], k.ident[:, :])
                    mm.then_inc(turned, 1)

                walk(pe, turn)
                if small:
                    pe.wait_ge(sm_loaded, 16 * len(small))
                    for j in range(len(small)):
                        for kk in range(KC):
                            mm = pe.transpose(pss[:, (j * KC + kk) * E:(j * KC + kk + 1) * E],
                                              rawsm[:, j, kk * P:(kk + 1) * P], k.ident[0:E, 0:E])
                    mm.then_inc(sm_turned, 1)

            def copier(which, sem):
                def copy_out(eng, copy):
                    eng.sem_inc(sem, RING // 2)

                    def out(i, m, n, slot, lap):
                        if n % 2 != which:
                            return
                        eng.wait_ge(turned, (i * RING if m is not None else 0) + n + 1 + RING)
                        copy(target(i, m, n), ps[:, slot, :].rearrange("p (k c) -> p k c", k=KC)).then_inc(sem, 1)

                    walk(eng, out)
                return copy_out

            @block.vector
            def _(dve):
                copier(0, out_dve)(dve, dve.tensor_copy)
                if small:
                    dve.wait_ge(sm_turned, 1)
                    for j, (_, dst) in enumerate(small):
                        dve.tensor_copy(dst, pss[:, j * KC * E:(j + 1) * KC * E].rearrange("p (k e) -> p k e", k=KC))

            @block.scalar
            def _(act):
                copier(1, out_act)(act, lambda o, i: act.activation(o, i, ACT.Copy))


def ln_stats(nc, k, name, x):
    with Stage(nc, name) as s:
        st6 = s.sb("st6", [P, NT, 6])
        mv = s.sb("mv", [P, NT, 2])
        std = s.sb("std", [P, NT])
        stats, aggr, rooted, done = (s.sem(v) for v in ("stats", "aggr", "rooted", "done"))
        with nc.Block() as block:

            @block.vector
            def _(dve):
                with dve.Fori(0, NT) as t:
                    dve.bn_stats(st6[:, ds(t, 1), :].rearrange("p a s -> p (a s)"),
                                 x[:, ds(t, 1), :].rearrange("p a c -> p (a c)")).then_inc(stats, 1)
                dve.wait_ge(stats, NT)
                for t in range(NT):
                    dve.bn_aggr(mv[:, t, :], st6[:, t, :]).then_inc(aggr, 1)
                dve.wait_ge(aggr, NT)
                dve.tensor_scalar(std[:, :], mv[:, :, 1], LN_EPS, None, ALU.add).then_inc(aggr, 1)
                dve.tensor_copy(k.mean[:, :], mv[:, :, 0]).then_inc(aggr, 1)
                dve.wait_ge(rooted, 1)
                dve.reciprocal(k.rstd[:, :], std[:, :]).then_inc(done, 1)

            @block.scalar
            def _(act):
                act.wait_ge(aggr, NT + 1)
                act.activation(std[:, :], std[:, :], ACT.Sqrt).then_inc(rooted, 1)


def load_x(nc, k, x):
    G = 4
    with Stage(nc, "ldx") as s:
        in_ = s.sem("in")
        with nc.Block() as block:

            @block.sync
            def _(sp):
                xd = x.rearrange("b (t p) c -> p (b t) c", p=P)
                for g in range(NT // G):
                    sp.dma_start(k.x[:, g * G:(g + 1) * G, :], xd[:, g * G:(g + 1) * G, :]).then_inc(in_, 16)
                sp.wait_ge(in_, 16 * (NT // G))


def tile(ap, t):
    return ap[:, ds(t, 1), :].rearrange("p a c -> p (a c)")


def linear_attention_in(nc, k, s_out):
    with Stage(nc, "lai") as s:
        xn = s.sb("xn", [P, 2, C])
        xnT = s.sb("xnT", [P, 2, KC, P])
        low = s.sb("low", [P, 2, 2 * C])
        phi = s.sb("phi", [P, 2, 2 * C])
        va = s.sb("va", [P, 2, KC, P + 1])
        zero = s.sb("zero", [1, P + 1])
        psT = s.ps("psT", [P, 2, BANK])
        psQK = s.ps("psQK", [P, 2, BANK])
        psV = s.ps("psV", [P, BANK])
        psQT = s.ps("psQT", [P, BANK])
        psKV = s.ps("psKV", [P, KC, BANK])
        (normed, x_turned, x_out, qk_ready, v_ready, clipped, raised, phi_ready, v_out, kv_added, q_turned, q_out,
         seq_done, kv_out, start, act_in) = (
            s.sem(v) for v in ("normed", "xturned", "xout", "qk", "v", "clipped", "raised", "phi", "vout", "kvadd",
                               "qturned", "qout", "seqdone", "kvout", "start", "actin"))
        with nc.Block() as block:

            @block.vector
            def _(dve):
                dve.memset(zero[:, :], 0.0).then_inc(start, 1)
                for j in range(2):
                    dve.memset(va[:, j, :, P:P + 1], 1.0).then_inc(start, 1)
                dve.sem_inc(clipped, 2)
                dve.sem_inc(phi_ready, 1)

                def norm(t, j):
                    dve.wait_ge(x_turned, t)
                    dve.tensor_scalar(xn[:, j, :], tile(k.x, t), k.mean[:, ds(t, 1)], k.rstd[:, ds(t, 1)],
                                      ALU.subtract, ALU.mult).then_inc(normed, 1)

                def elementwise(t, j):
                    dve.wait_ge(qk_ready, t + 1)
                    dve.wait_ge(raised, t)
                    dve.tensor_scalar(low[:, j, :], psQK[:, j, :], 0.0, None, ALU.min).then_inc(clipped, 1)
                    dve.wait_ge(raised, t + 2)
                    dve.wait_ge(kv_added, t)
                    dve.scalar_tensor_tensor(phi[:, j, :], psQK[:, j, :], 0.0, low[:, j, :],
                                             ALU.max, ALU.add).then_inc(phi_ready, 1)

                for b in range(NB):
                    norm(b * TB, 0)
                    with dve.Fori(0, TB // 2 - 1) as i:
                        for j in range(2):
                            norm(b * TB + i * 2 + j + 1, (j + 1) % 2)
                            elementwise(b * TB + i * 2 + j, j)
                    norm(b * TB + TB - 1, 1)
                    elementwise(b * TB + TB - 2, 0)
                    elementwise(b * TB + TB - 1, 1)
                    dve.wait_ge(seq_done, b + 1)
                    for kk in range(KC):
                        dve.tensor_tensor(k.kvblk[:, b, kk, :], psKV[:, kk, 0:P], k.blockdiag[:, :], ALU.mult)
                        ins = dve.tensor_scalar(k.ksum[:, b, kk, :], k.blockdiag[:, :], psKV[:, kk, P:P + 1], None,
                                                ALU.mult)
                    ins.then_inc(kv_out, 1)

            @block.scalar
            def _(act):
                act.sem_inc(raised, 1)
                act.sem_inc(x_out, 1)

                def first(t, j):
                    act.wait_ge(x_turned, t + 2)
                    act.activation(xnT[:, j, :, :], psT[:, j, 0:C].rearrange("p (k c) -> p k c", k=KC),
                                   ACT.Copy).then_inc(x_out, 1)

                def second(t, j):
                    act.wait_ge(clipped, t + 3)
                    act.activation(low[:, j, :], low[:, j, :], ACT.Exp).then_inc(raised, 1)
                    act.wait_ge(v_ready, t + 1)
                    act.wait_ge(kv_added, t)
                    act.activation(va[:, j, :, 0:P], psV[:, 0:C].rearrange("p (k c) -> p k c", k=KC),
                                   ACT.Copy).then_inc(v_out, 1)
                    act.wait_ge(q_turned, t + 1)
                    act.activation(k.qT[:, :, ds(t * P, P)], psQT[:, 0:C].rearrange("p (k c) -> p k c", k=KC),
                                   ACT.Copy).then_inc(q_out, 1)

                for b in range(NB):
                    first(b * TB, 0)
                    with act.Fori(0, TB // 2 - 1) as i:
                        for j in range(2):
                            first(b * TB + i * 2 + j + 1, (j + 1) % 2)
                            second(b * TB + i * 2 + j, j)
                    first(b * TB + TB - 1, 1)
                    second(b * TB + TB - 2, 0)
                    second(b * TB + TB - 1, 1)

            @block.tensor
            def _(pe):
                pe.wait_ge(start, 3)
                pe.sem_inc(x_turned, 1)
                pe.sem_inc(kv_added, 1)

                def turn(t, j):
                    pe.wait_ge(normed, t + 1)
                    pe.wait_ge(x_out, t)
                    for kk in range(KC):
                        mm = pe.transpose(psT[:, j, kk * P:(kk + 1) * P], xn[:, j, kk * P:(kk + 1) * P], k.ident[:, :])
                    mm.then_inc(x_turned, 1)

                def project(t, j):
                    pe.wait_ge(x_out, t + 2)
                    pe.wait_ge(phi_ready, t)
                    for kk in range(KC):
                        mm = pe.matmul(psQK[:, j, :], xnT[:, j, kk, :], k.wqkv[:, kk, 0:2 * C],
                                       start=(kk == 0), stop=(kk == KC - 1))
                    mm.then_inc(qk_ready, 1)
                    pe.wait_ge(v_out, t)
                    for kk in range(KC):
                        mm = pe.matmul(psV[:, 0:C], xnT[:, j, kk, :], k.wqkv[:, kk, 2 * C:3 * C],
                                       start=(kk == 0), stop=(kk == KC - 1))
                    mm.then_inc(v_ready, 1)

                def outer(t, j):
                    pe.wait_ge(phi_ready, t + 2)
                    pe.wait_ge(q_out, t)
                    for kk in range(KC):
                        mm = pe.transpose(psQT[:, kk * P:(kk + 1) * P], phi[:, j, kk * P:(kk + 1) * P], k.ident[:, :])
                    mm.then_inc(q_turned, 1)
                    pe.wait_ge(v_out, t + 1)
                    for kk in range(KC):
                        mm = pe.matmul(psKV[:, kk, 0:P + 1], phi[:, j, C + kk * P:C + (kk + 1) * P], va[:, j, kk, :],
                                       start=False, stop=False)
                    mm.then_inc(kv_added, 1)

                for b in range(NB):
                    if b:
                        pe.wait_ge(kv_out, b)
                    for kk in range(KC):
                        pe.matmul(psKV[:, kk, 0:P + 1], zero[0:1, 0:P], zero[:, :], start=True, stop=False)
                    turn(b * TB, 0)
                    turn(b * TB + 1, 1)
                    project(b * TB, 0)
                    with pe.Fori(0, TB // 2 - 1) as i:
                        for j in range(2):
                            t = b * TB + i * 2 + j
                            turn(t + 2, j)
                            project(t + 1, (j + 1) % 2)
                            outer(t, j)
                    project(b * TB + TB - 1, 1)
                    outer(b * TB + TB - 2, 0)
                    outer(b * TB + TB - 1, 1)
                    for kk in range(KC):
                        mm = pe.matmul(psKV[:, kk, 0:P + 1], zero[0:1, 0:P], zero[:, :], start=False, stop=True)
                    mm.then_inc(seq_done, 1)


def linear_attention_out(nc, k):
    CH = BANK
    NCH = TS // CH
    TC = CH // P
    with Stage(nc, "lao") as s:
        den = s.sb("den", [P, 2, CH])
        rden = s.sb("rden", [P, 2, CH])
        oT = s.sb("oT", [P, 2, KC, CH])
        psN = s.ps("psN", [P, 2, CH])
        psD = s.ps("psD", [P, 2, CH])
        psY = s.ps("psY", [P, 2, BANK])
        (biased, num_ready, den_ready, den_out, inverted, divided, y_ready, y_added) = (
            s.sem(v) for v in ("biased", "num", "den", "denout", "inv", "div", "y", "yadd"))
        with nc.Block() as block:

            @block.gpsimd
            def _(pool):
                with pool.Fori(0, NT) as t:
                    pool.tensor_tensor(tile(k.x, t), tile(k.x, t), k.bproj[:, :], ALU.add).then_inc(biased, 1)

            @block.tensor
            def _(pe):
                def heads(b, c, j):
                    for kk in range(KC):
                        rhs = k.qT[:, kk, ds(c * CH, CH)]
                        pe.wait_ge(divided, c * 2 + kk + 1)
                        pe.matmul(psD[:, kk, :], k.ksum[:, b, kk, :], rhs, start=True, stop=True).then_inc(den_ready, 1)
                        pe.matmul(psN[:, kk, :], k.kvblk[:, b, kk, :], rhs, start=True, stop=True).then_inc(num_ready, 1)

                def out(c, j):
                    pe.wait_ge(divided, c * 2 + 4)
                    for q in range(TC):
                        pe.wait_ge(y_added, c * TC + q + 1)
                        for kk in range(KC):
                            mm = pe.matmul(psY[:, q % 2, 0:C], oT[:, j, kk, q * P:(q + 1) * P], k.wproj[:, kk, :],
                                           start=(kk == 0), stop=(kk == KC - 1))
                        mm.then_inc(y_ready, 1)

                heads(0, 0, 0)
                for c in range(NB * NCH):
                    if c + 1 < NB * NCH:
                        heads((c + 1) // NCH, c + 1, (c + 1) % 2)
                    out(c, c % 2)

            @block.scalar
            def _(act):
                with act.Fori(0, NB * NCH) as c:
                    for kk in range(KC):
                        act.wait_ge(den_ready, c * 2 + kk + 1)
                        act.wait_ge(inverted, c * 2 + kk + 1)
                        act.activation(den[:, kk, :], psD[:, kk, :], ACT.Copy, bias=EPS).then_inc(den_out, 1)

            @block.vector
            def _(dve):
                dve.sem_inc(divided, 2)
                dve.sem_inc(inverted, 2)
                dve.sem_inc(y_added, 2)

                def divide(c, j):
                    for kk in range(KC):
                        dve.wait_ge(den_out, c * 2 + kk + 1)
                        dve.reciprocal(rden[:, kk, :], den[:, kk, :]).then_inc(inverted, 1)
                        dve.wait_ge(inverted, c * 2 + kk + 3)
                        dve.wait_ge(num_ready, c * 2 + kk + 1)
                        dve.tensor_tensor(oT[:, j, kk, :], psN[:, kk, :], rden[:, kk, :], ALU.mult).then_inc(divided, 1)

                def add(c):
                    for q in range(TC):
                        t = c * TC + q
                        dve.wait_ge(y_ready, t + 1)
                        dve.wait_ge(biased, t + 1)
                        dve.tensor_tensor(tile(k.x, t), tile(k.x, t), psY[:, q % 2, 0:C], ALU.add).then_inc(y_added, 1)

                n = NB * NCH
                divide(0, 0)
                with dve.Fori(0, n // 2 - 1) as i:
                    for j in range(2):
                        divide(i * 2 + j + 1, (j + 1) % 2)
                        add(i * 2 + j)
                divide(n - 1, 1)
                add(n - 2)
                add(n - 1)


def route(nc, k, name, layer, gateT, x):
    with Stage(nc, name) as s:
        R = 4
        xn = s.sb("xn", [P, R, C])
        xnT = s.sb("xnT", [P, 2, KC, P])
        sq = s.sb("sq", [P, C])
        cT2 = s.sb("cT2", [P, KC, E])
        xsq = s.sb("xsq", [P, NT])
        csq = s.sb("csq", [P, E])
        psT = s.ps("psT", [P, 2, BANK])
        psL = s.ps("psL", [P, BANK])
        psC = s.ps("psC", [P, BANK])
        psPre = s.ps("psPre", [P, BANK])
        psTot = s.ps("psTot", [P, BANK])
        psTab = s.ps("psTab", [P, BANK])
        normed, turned, x_out, logits, squared, csq_ready = (
            s.sem(v) for v in ("normed", "turned", "xout", "logits", "squared", "csq"))
        stored = s.sems("stored", R)
        vals, work, mask = s.sb("vals", [P, NT, E]), s.sb("work", [P, NT, E]), s.sb("mask", [P, NT, E])
        one1, one2, maskb = s.sb("one1", [P, NT, E]), s.sb("one2", [P, NT, E]), s.sb("maskb", [P, NT * E], BF16)
        tot, incl, pos = s.sb("tot", [P, NT, E]), s.sb("incl", [P, NT, E]), s.sb("pos", [P, NT, E])
        desc = s.sb("desc", [P, E])
        m1, m2, c1, row, row2 = (s.sb(v, [P, NT]) for v in ("m1", "m2", "c1", "row", "row2"))
        p12 = s.sb("p12", [P, NT, 2])
        w12 = s.sb("w12", [P, NT, 2])
        hi, lo, dstv = (s.sb(v, [P, NT, 2]) for v in ("hi", "lo", "dstv"))
        pi, pj = s.sb("pi", [P, NT * 2], I32), s.sb("pj", [P, NT * 2], I32)
        ni = s.sb("ni", [P, E], I32)
        nf, ends, first = s.sb("nf", [P, E]), s.sb("ends", [P, E]), s.sb("first", [P, E])
        zeroE, zeroT = s.sb("zeroE", [P, E]), s.sb("zeroT", [P, NT])
        te = s.sb("te", [P, NTILE, E])
        tes = s.sb("tes", [P, NTILE])
        RH = 4
        oneLo = s.sb("oneLo", [P, RH, P])
        oneHi = s.sb("oneHi", [P, RH, 2, NTILE])
        raw, pad, big = s.sb("raw", [P, NTILE]), s.sb("pad", [P, NTILE]), s.sb("big", [P, NTILE])
        chain, soft, softed, sums_asked, sums_ready, hot, tab_added, tab_done = (
            s.sem(v) for v in ("chain", "soft", "softed", "asked", "sums", "hot", "tabadd", "tabdone"))
        xn_d = k.xn_d.rearrange("(t p) c -> t p c", p=P)

        def bt(ap):
            return ap.unsqueeze(2).to_broadcast([P, NT, E])

        def be(ap):
            return ap.unsqueeze(1).to_broadcast([P, NT, E])

        with nc.Block() as block:

            @block.sync
            def _(sp):
                with sp.Fori(0, NT // R) as i:
                    for j in range(R):
                        sp.wait_ge(normed, i * R + j + 1)
                        sp.dma_start(xn_d[ds(i * R + j, 1), :, :].rearrange("a p c -> (a p) c"),
                                     xn[:, j, :]).then_inc(stored[j], 16)
                for j in range(R):
                    sp.wait_ge(stored[j], 16 * (NT // R))

            @block.scalar
            def _(act):
                with act.Fori(0, NT // 4) as i:
                    for jj in range(4):
                        t, j = i * 4 + jj, jj % 2
                        act.wait_ge(turned, t + 1 + 2)
                        act.wait_ge(logits, t + 1)
                        act.activation(xnT[:, j, :, :], psT[:, j, 0:C].rearrange("p (k c) -> p k c", k=KC),
                                       ACT.Copy).then_inc(x_out, 1)
                        if layer == 1:
                            act.activation(sq[:, :], xn[:, jj, :], ACT.Square,
                                           accum_out=xsq[:, ds(t, 1)]).then_inc(squared, 1)
                            act.wait_ge(squared, t + 1)
                if layer == 0:
                    act.wait_ge(soft, 1)
                    act.activation(work[:, :, :], work[:, :, :], ACT.Exp).then_inc(softed, 1)
                else:
                    act.wait_ge(soft, 1)
                    act.activation(p12[:, :, :], p12[:, :, :], ACT.Sqrt).then_inc(softed, 1)
                    act.wait_ge(soft, 2)
                    act.activation(m2[:, :], m2[:, :], ACT.Exp).then_inc(softed, 1)

            @block.tensor
            def _(pe):
                pe.sem_inc(turned, 2)
                pe.sem_inc(logits, 2)

                def turn(t, jj):
                    pe.wait_ge(normed, t + 1)
                    pe.wait_ge(x_out, t + 1)
                    for kk in range(KC):
                        mm = pe.transpose(psT[:, jj % 2, kk * P:(kk + 1) * P], xn[:, jj, kk * P:(kk + 1) * P],
                                          k.ident[:, :])
                    mm.then_inc(turned, 1)

                def score(t, jj):
                    pe.wait_ge(x_out, t + 3)
                    for kk in range(KC):
                        mm = pe.matmul(psL[:, ds(t * E, E)], xnT[:, jj % 2, kk, :], gateT[:, kk, :],
                                       start=(kk == 0), stop=(kk == KC - 1))
                    mm.then_inc(logits, 1)

                turn(0, 0)
                with pe.Fori(0, NT // 4 - 1) as i:
                    for jj in range(4):
                        turn(i * 4 + jj + 1, (jj + 1) % 4)
                        score(i * 4 + jj, jj)
                for jj in range(4):
                    if jj < 3:
                        turn(NT - 4 + jj + 1, jj + 1)
                    score(NT - 4 + jj, jj)
                if layer == 1:
                    pe.wait_ge(csq_ready, 1)
                    for kk in range(KC):
                        mm = pe.matmul(psC[:, 0:E], k.ones[:, :], cT2[:, kk, :], start=(kk == 0), stop=(kk == KC - 1))
                    mm.then_inc(csq_ready, 1)
                pe.wait_ge(sums_asked, 1)
                pe.matmul(psPre[:, 0:NT * E], k.upperb[:, :], maskb[:, :], start=True, stop=True)
                pe.matmul(psTot[:, 0:NT * E], k.onesb[:, :], maskb[:, :], start=True, stop=True).then_inc(sums_ready, 1)
                for n in range(2 * NT):
                    pe.wait_ge(hot, n + 1)
                    pe.matmul(psTab[:, 0:2 * NTILE], oneLo[:, n % RH, :],
                              oneHi[:, n % RH, :, :].rearrange("p a c -> p (a c)"),
                              start=(n == 0), stop=(n == 2 * NT - 1)).then_inc(tab_added, 1)

            @block.vector
            def _(dve):
                dve.sem_inc(x_out, 2)
                ser = Serial(dve, chain)
                with dve.Fori(0, NT // R) as i:
                    for j in range(R):
                        t = i * R + j
                        dve.wait_ge(stored[j], i * 16)
                        dve.wait_ge(turned, t)
                        if layer == 1:
                            dve.wait_ge(squared, t)
                        dve.tensor_scalar(xn[:, j, :], tile(x, t), k.mean[:, ds(t, 1)], k.rstd[:, ds(t, 1)],
                                          ALU.subtract, ALU.mult).then_inc(normed, 1)
                ser(dve.memset(zeroE[:, :], 0.0))
                ser(dve.memset(zeroT[:, :], 0.0))
                ser(dve.tensor_scalar(desc[:, :], k.lane[:, 0:E], -1.0, float(E), ALU.mult, ALU.add))
                if layer == 1:
                    dve.tensor_tensor(cT2[:, :, :], gateT[:, :, :], gateT[:, :, :], ALU.mult).then_inc(csq_ready, 1)
                    dve.wait_ge(csq_ready, 2)
                    ser(dve.tensor_copy(csq[:, :], psC[:, 0:E]))
                dve.wait_ge(logits, NT + 2)
                L = psL[:, 0:NT * E].rearrange("p (t e) -> p t e", e=E)
                if layer == 0:
                    ser(dve.tensor_reduce(m1[:, :], L, AX.X, ALU.max))
                    ser(dve.tensor_tensor(work[:, :, :], L, bt(m1[:, :]), ALU.subtract))
                    dve.sem_inc(soft, 1)
                    dve.wait_ge(softed, 1)
                    ser(dve.tensor_reduce(m1[:, :], work[:, :, :], AX.X, ALU.add))
                    ser(dve.reciprocal(m2[:, :], m1[:, :]))
                    ser(dve.tensor_tensor(vals[:, :, :], work[:, :, :], bt(m2[:, :]), ALU.mult))
                else:
                    dve.wait_ge(squared, NT)
                    ser(dve.tensor_scalar(work[:, :, :], L, -2.0, None, ALU.mult))
                    ser(dve.tensor_tensor(mask[:, :, :], be(csq[:, :]), bt(xsq[:, :]), ALU.add))
                    ser(dve.tensor_tensor(vals[:, :, :], work[:, :, :], mask[:, :, :], ALU.add))
                    ser(dve.tensor_scalar(vals[:, :, :], vals[:, :, :], 1e-12, None, ALU.max))

                def largest(v, val, onehot):
                    ser(dve.tensor_reduce(val, v, AX.X, ALU.max))
                    ser(dve.tensor_tensor(mask[:, :, :], v, bt(val), ALU.is_equal))
                    ser(dve.tensor_tensor(mask[:, :, :], mask[:, :, :], be(desc[:, :]), ALU.mult))
                    ser(dve.tensor_reduce(c1[:, :], mask[:, :, :], AX.X, ALU.max))
                    ser(dve.tensor_tensor(onehot, bt(c1[:, :]), be(desc[:, :]), ALU.is_equal))

                largest(vals[:, :, :], p12[:, :, 0], one1[:, :, :])
                ser(dve.tensor_scalar(mask[:, :, :], one1[:, :, :], -1.0, 1.0, ALU.mult, ALU.add))
                ser(dve.tensor_tensor(work[:, :, :], vals[:, :, :], mask[:, :, :], ALU.mult))
                ser(dve.tensor_tensor(work[:, :, :], work[:, :, :], one1[:, :, :], ALU.subtract))
                largest(work[:, :, :], p12[:, :, 1], one2[:, :, :])
                ser(dve.tensor_tensor(maskb[:, :].rearrange("p (t e) -> p t e", e=E), one1[:, :, :], one2[:, :, :],
                                      ALU.add))
                dve.sem_inc(sums_asked, 1)
                if layer == 0:
                    ser(dve.tensor_tensor(m1[:, :], p12[:, :, 0], p12[:, :, 1], ALU.add))
                    ser(dve.reciprocal(m2[:, :], m1[:, :]))
                    ser(dve.tensor_tensor(w12[:, :, :], p12[:, :, :], m2[:, :].unsqueeze(2).to_broadcast([P, NT, 2]),
                                          ALU.mult))
                else:
                    dve.sem_inc(soft, 1)
                    dve.wait_ge(softed, 1)
                    ser(dve.tensor_tensor(m2[:, :], p12[:, :, 1], p12[:, :, 0], ALU.subtract))
                    dve.sem_inc(soft, 1)
                    dve.wait_ge(softed, 2)
                    ser(dve.tensor_scalar(m1[:, :], m2[:, :], 1.0, None, ALU.add))
                    ser(dve.reciprocal(w12[:, :, 0], m1[:, :]))
                    ser(dve.tensor_tensor(w12[:, :, 1], w12[:, :, 0], m2[:, :], ALU.mult))
                dve.wait_ge(sums_ready, 1)
                ser(dve.tensor_copy(tot[:, :, :], psTot[:, 0:NT * E].rearrange("p (t e) -> p t e", e=E)))
                for e in range(E):
                    ins = dve.tensor_tensor_scan(incl[:, :, e], tot[:, :, e], zeroT[:, :], 0.0, ALU.add, ALU.add)
                ser(ins)
                ser(dve.tensor_scalar(nf[:, :], incl[:, NT - 1, :], float(P - 1), None, ALU.add))
                ser(dve.tensor_copy(ni[:, :], nf[:, :]))
                ser(dve.tensor_scalar(ni[:, :], ni[:, :], 7, None, ALU.logical_shift_right))
                ser(dve.tensor_copy(nf[:, :], ni[:, :]))
                ser(dve.tensor_tensor_scan(ends[:, :], nf[:, :], zeroE[:, :], 0.0, ALU.add, ALU.add))
                ser(dve.tensor_tensor(first[:, :], ends[:, :], nf[:, :], ALU.subtract))
                ser(dve.tensor_scalar(first[:, :], first[:, :], float(P), None, ALU.mult))
                ser(dve.tensor_tensor(pos[:, :, :], incl[:, :, :], tot[:, :, :], ALU.subtract))
                ser(dve.tensor_tensor(pos[:, :, :], pos[:, :, :], be(first[:, :]), ALU.add))
                ser(dve.tensor_tensor(pos[:, :, :], psPre[:, 0:NT * E].rearrange("p (t e) -> p t e", e=E),
                                      pos[:, :, :], ALU.add))
                for j, one in enumerate((one1, one2)):
                    ser(dve.tensor_tensor(work[:, :, :], one[:, :, :], pos[:, :, :], ALU.mult))
                    ser(dve.tensor_reduce(dstv[:, :, j], work[:, :, :], AX.X, ALU.add))
                flat = dstv[:, :, :].rearrange("p t j -> p (t j)")
                ser(dve.tensor_copy(pi[:, :], flat))
                ser(dve.tensor_scalar(pj[:, :], pi[:, :], 7, None, ALU.logical_shift_right))
                ser(dve.tensor_copy(hi[:, :, :].rearrange("p t j -> p (t j)"), pj[:, :]))
                ser(dve.tensor_scalar(pj[:, :], pi[:, :], P - 1, None, ALU.bitwise_and))
                ser(dve.tensor_copy(lo[:, :, :].rearrange("p t j -> p (t j)"), pj[:, :]))
                ser(dve.tensor_scalar(row[:, :], k.tilebase[:, :], k.lane1[:, 0:1], 1.0, ALU.add, ALU.add))
                ser(dve.tensor_copy(dstv[:, :, 0], row[:, :]))
                ser(dve.tensor_scalar(dstv[:, :, 1], row[:, :], float(T), None, ALU.add))
                for n in range(2 * NT):
                    t, j = n // 2, n % 2
                    if n >= RH:
                        dve.wait_ge(tab_added, n - RH + 1)
                    dve.tensor_scalar(oneLo[:, n % RH, :], k.lane[:, :], lo[:, t, j:j + 1], None, ALU.is_equal)
                    dve.tensor_scalar(oneHi[:, n % RH, 0, :], k.lane[:, 0:NTILE], hi[:, t, j:j + 1],
                                      dstv[:, t, j:j + 1], ALU.is_equal, ALU.mult)
                    dve.tensor_scalar(oneHi[:, n % RH, 1, :], k.lane[:, 0:NTILE], hi[:, t, j:j + 1],
                                      w12[:, t, j:j + 1], ALU.is_equal, ALU.mult).then_inc(hot, 1)
                ser(dve.tensor_tensor(te[:, :, :], k.lane[:, 0:NTILE].unsqueeze(2).to_broadcast([P, NTILE, E]),
                                      ends[:, :].unsqueeze(1).to_broadcast([P, NTILE, E]), ALU.is_ge))
                ser(dve.tensor_reduce(tes[:, :], te[:, :, :], AX.X, ALU.add))
                ser(dve.tensor_scalar(tes[:, :], tes[:, :], float(E - 1), None, ALU.min))
                ser(dve.tensor_copy(k.tile_expert[:, :], tes[0:1, :]))
                dve.wait_ge(tab_added, 2 * NT)
                ser(dve.tensor_copy(k.wgt[:, :], psTab[:, NTILE:2 * NTILE]))
                ser(dve.tensor_copy(raw[:, :], psTab[:, 0:NTILE]))
                ser(dve.tensor_scalar(pad[:, :], raw[:, :], 0.0, None, ALU.is_equal))
                ser(dve.tensor_scalar(big[:, :], k.odd_rows[:, :], k.lane1[:, 0:1], None, ALU.add))
                ser(dve.tensor_tensor(big[:, :], big[:, :], pad[:, :], ALU.mult))
                ser(dve.tensor_scalar(pad[:, :], pad[:, :], float(2 * T + 1), -1.0, ALU.mult, ALU.add))
                ser(dve.tensor_tensor(raw[:, :], raw[:, :], pad[:, :], ALU.add))
                ser(dve.tensor_tensor(raw[:, :], raw[:, :], big[:, :], ALU.add))
                ser(dve.tensor_copy(k.dst[:, :], raw[:, :]))
                ser(dve.tensor_scalar(k.tok[:, :], k.dst[:, :], T - 1, None, ALU.bitwise_and))


def experts0(nc, k):
    with Stage(nc, "ex0") as s:
        idx, odx = s.sb("idx", [P, GR, 1], U32), s.sb("odx", [P, 2, 1], U32)
        xg = s.sb("xg", [P, GR, C])
        xT = s.sb("xT", [P, 2, KC, P])
        sg = s.sb("sg", [P, 2, F0])
        h = s.sb("h", [P, 2, F0])
        hT = s.sb("hT", [P, 2, KC, P])
        y = s.sb("y", [P, 2, C])
        psX = s.ps("psX", [P, 2, BANK])
        psH = s.ps("psH", [P, 2, BANK])
        psG = s.ps("psG", [P, 2, BANK])
        psY = s.ps("psY", [P, 2, BANK])
        (x_turned, x_out, h_ready, gated, h_done, h_turned, h_out, y_ready, y_done) = (
            s.sem(v) for v in ("xturned", "xout", "hready", "gated", "hdone", "hturned", "hout", "yready",
                               "ydone"))
        got, put = s.sems("got", GR), s.sems("put", 2)
        with nc.Block() as block:

            @block.gpsimd
            def _(pool):
                def gather(t, g, lap):
                    pool.wait_ge(got[g], lap * 16)
                    pool.wait_ge(x_turned, t + 1)
                    pool.tensor_copy(idx[:, g, :], k.tok[:, ds(t, 1)])
                    pool.drain()
                    pool.indirect_dma_start(xg[:, g, :], None, k.xn_d,
                                            bass.IndirectOffsetOnAxis(idx[:, g, :], 0)).then_inc(got[g], 16)

                def scatter(t, j, lap):
                    pool.wait_ge(put[j], lap * 16)
                    pool.wait_ge(y_done, t + 3)
                    pool.tensor_copy(odx[:, j, :], k.dst[:, ds(t, 1)])
                    pool.drain()
                    pool.indirect_dma_start(k.y_d, bass.IndirectOffsetOnAxis(odx[:, j, :], 0), y[:, j, :],
                                            None).then_inc(put[j], 16)

                for g in range(GR):
                    gather(g, g, 0)
                with pool.Fori(0, NTILE // GR - 1) as i:
                    for g in range(GR):
                        t = i * GR + g
                        gather(t + GR, g, i + 1)
                        scatter(t, g % 2, i * 2 + g // 2)
                for g in range(GR):
                    t = NTILE - GR + g
                    scatter(t, g % 2, t // 2)
                for j in range(2):
                    pool.wait_ge(put[j], 16 * (NTILE // 2))

            @block.tensor
            def _(pe):
                pe.sem_inc(x_turned, GR)
                pe.sem_inc(h_turned, 2)
                te = k.tile_expert

                def turn(t, g, lap):
                    pe.wait_ge(got[g], lap * 16 + 16)
                    pe.wait_ge(x_out, t + 1)
                    for kk in range(KC):
                        mm = pe.transpose(psX[:, g % 2, kk * P:(kk + 1) * P], xg[:, g, kk * P:(kk + 1) * P],
                                          k.ident[:, :])
                    mm.then_inc(x_turned, 1)

                def up(t, j, e):
                    pe.wait_ge(x_out, t + 3)
                    pe.wait_ge(h_done, t + 1)
                    for kk in range(KC):
                        mm = pe.matmul(psH[:, j, :], xT[:, j, kk, :],
                                       k.w13[:, ds(e, 1), kk, :].rearrange("p a c -> p (a c)"),
                                       start=(kk == 0), stop=(kk == KC - 1))
                    mm.then_inc(h_ready, 1)

                def down(t, j, e):
                    pe.wait_ge(h_done, t + 3)
                    pe.wait_ge(h_out, t + 1)
                    for kk in range(KC):
                        mm = pe.transpose(psG[:, j, kk * P:(kk + 1) * P], h[:, j, kk * P:(kk + 1) * P], k.ident[:, :])
                    mm.then_inc(h_turned, 1)
                    pe.wait_ge(h_out, t + 3)
                    pe.wait_ge(y_done, t + 1)
                    for kk in range(KC):
                        mm = pe.matmul(psY[:, j, 0:C], hT[:, j, kk, :],
                                       k.w2[:, ds(e, 1), kk, :].rearrange("p a c -> p (a c)"),
                                       start=(kk == 0), stop=(kk == KC - 1))
                    mm.then_inc(y_ready, 1)

                def expert(t):
                    return pe.value_load(te[0:1, ds(t, 1)], min_val=0, max_val=E - 1)

                turn(0, 0, 0)
                turn(1, 1, 0)
                up(0, 0, expert(0))
                with pe.Fori(0, NTILE // GR - 1) as i:
                    for g in range(GR):
                        t = i * GR + g
                        turn(t + 2, (g + 2) % GR, i + (g + 2) // GR)
                        up(t + 1, (g + 1) % 2, expert(t + 1))
                        down(t, g % 2, expert(t))
                for t in range(NTILE - GR, NTILE):
                    if t + 2 < NTILE:
                        turn(t + 2, (t + 2) % GR, (t + 2) // GR)
                    if t + 1 < NTILE:
                        up(t + 1, (t + 1) % 2, expert(t + 1))
                    down(t, t % 2, expert(t))

            @block.scalar
            def _(act):
                act.sem_inc(x_out, 2)
                act.sem_inc(h_out, 2)

                def lead(t, j):
                    act.wait_ge(x_turned, t + 1 + GR)
                    act.activation(xT[:, j, :, :], psX[:, j, 0:C].rearrange("p (k c) -> p k c", k=KC),
                                   ACT.Copy).then_inc(x_out, 1)

                def gate(t, j):
                    act.wait_ge(h_ready, t + 1)
                    act.wait_ge(h_done, t + 1)
                    act.activation(sg[:, j, :], psH[:, j, 0:F0], ACT.Silu).then_inc(gated, 1)

                def turned(t, j):
                    act.wait_ge(h_turned, t + 3)
                    act.wait_ge(y_done, t + 1)
                    act.activation(hT[:, j, :, :], psG[:, j, 0:C].rearrange("p (k c) -> p k c", k=KC),
                                   ACT.Copy).then_inc(h_out, 1)

                lead(0, 0)
                lead(1, 1)
                gate(0, 0)
                with act.Fori(0, NTILE // 2 - 1) as i:
                    for j in range(2):
                        t = i * 2 + j
                        act.wait_ge(h_ready, t + 1)
                        lead(t + 2, j)
                        gate(t + 1, 1 - j)
                        turned(t, j)
                gate(NTILE - 1, 1)
                turned(NTILE - 2, 0)
                turned(NTILE - 1, 1)

            @block.vector
            def _(dve):
                dve.sem_inc(h_done, 2)
                dve.sem_inc(y_done, 2)

                def hidden(t, j):
                    dve.wait_ge(gated, t + 1)
                    dve.wait_ge(h_turned, t + 1)
                    dve.tensor_tensor(h[:, j, :], psH[:, j, F0:2 * F0], sg[:, j, :], ALU.mult).then_inc(h_done, 1)

                def weigh(t, j, lap):
                    dve.wait_ge(y_ready, t + 1)
                    dve.wait_ge(put[j], lap * 16)
                    dve.tensor_scalar(y[:, j, :], psY[:, j, 0:C], k.wgt[:, ds(t, 1)], None, ALU.mult).then_inc(y_done, 1)

                hidden(0, 0)
                with dve.Fori(0, NTILE // 2 - 1) as i:
                    for j in range(2):
                        hidden(i * 2 + j + 1, 1 - j)
                        weigh(i * 2 + j, j, i)
                hidden(NTILE - 1, 1)
                weigh(NTILE - 2, 0, NTILE // 2 - 1)
                weigh(NTILE - 1, 1, NTILE // 2 - 1)


def combine(nc, k, name, x_in, x_out_sb, x_out_dram):
    G = 2
    with Stage(nc, name) as s:
        y = s.sb("y", [P, 2, 2, G, C])
        got, added = s.sems("got", 2), s.sem("added")
        xr = s.sb("xr", [P, 2, G, C]) if x_in is not None else None
        out_sem = s.sems("out", 2)
        y0 = k.y_d[0:2 * T, :].rearrange("(n t p) c -> p n t c", p=P, n=2)
        half = s.sem("half")
        n_dma = 3 if x_in is not None else 2

        def dram(ap, i, j):
            return ap[:, ds((i * 2 + j) * G, G), :]

        with nc.Block() as block:

            @block.sync
            def _(sp):
                sp.sem_inc(added, 2)
                with sp.Fori(0, NT // G // 2) as i:
                    for j in range(2):
                        sp.wait_ge(added, i * 2 + j + 1)
                        for n in range(2):
                            sp.dma_start(y[:, j, n, :, :],
                                         y0[:, n, ds((i * 2 + j) * G, G), :]).then_inc(got[j], 16)
                        if x_in is not None:
                            sp.wait_ge(out_sem[j], i * 16)
                            sp.dma_start(xr[:, j, :, :], dram(x_in, i, j)).then_inc(got[j], 16)

            @block.vector
            def _(dve):
                with dve.Fori(0, NT // G // 2) as i:
                    for j in range(2):
                        base = xr[:, j, :, :] if x_in is not None else dram(x_out_sb, i, j)
                        dve.wait_ge(got[j], (i + 1) * 16 * n_dma)
                        dve.tensor_tensor(y[:, j, 0, :, :], y[:, j, 0, :, :], y[:, j, 1, :, :], ALU.add).then_inc(half, 1)
                        dve.wait_ge(half, i * 2 + j + 1)
                        dve.tensor_tensor(base, base, y[:, j, 0, :, :], ALU.add).then_inc(added, 1)

            @block.scalar
            def _(act):
                if x_out_dram is not None:
                    with act.Fori(0, NT // G // 2) as i:
                        for j in range(2):
                            src = xr[:, j, :, :] if x_in is not None else dram(x_out_sb, i, j)
                            act.wait_ge(added, i * 2 + j + 3)
                            act.dma_start(dram(x_out_dram, i, j), src).then_inc(out_sem[j], 16)
                    for j in range(2):
                        act.wait_ge(out_sem[j], 16 * (NT // G // 2))


def log_map(nc, k):
    with Stage(nc, "lm") as s:
        sp_ = s.sb("sp", [P, NT, C])
        junk = s.sb("junk", [P, C])
        s2, y0, a, am, b, d, f = (s.sb(v, [P, NT]) for v in ("s2", "y0", "a", "am", "b", "d", "f"))
        normed, clipped, squared, chain, asked, rooted, grouped = (
            s.sem(v) for v in ("normed", "clipped", "squared", "chain", "asked", "rooted", "grouped"))
        G = 4
        stored = s.sem("stored")
        with nc.Block() as block:

            @block.vector
            def _(dve):
                ser = Serial(dve, chain)
                with dve.Fori(0, NT) as t:
                    dve.tensor_scalar(tile(sp_, t), tile(k.x, t), k.mean[:, ds(t, 1)], k.rstd[:, ds(t, 1)],
                                      ALU.subtract, ALU.mult).then_inc(normed, 1)
                    dve.wait_ge(normed, t + 1)
                    dve.tensor_scalar(tile(sp_, t), tile(sp_, t), -8.0, 8.0, ALU.max, ALU.min).then_inc(clipped, 1)
                dve.wait_ge(squared, NT)
                ser(dve.tensor_scalar(y0[:, :], s2[:, :], 1.0, EPS, ALU.add, ALU.add))
                dve.sem_inc(asked, 1)
                dve.wait_ge(rooted, 1)
                ser(dve.tensor_scalar(a[:, :], y0[:, :], 1.0 + EPS, None, ALU.max))
                ser(dve.tensor_scalar(am[:, :], a[:, :], 1.0, None, ALU.subtract))
                ser(dve.scalar_tensor_tensor(b[:, :], a[:, :], 1.0, am[:, :], ALU.add, ALU.mult))
                ser(dve.tensor_tensor(y0[:, :], y0[:, :], a[:, :], ALU.subtract))
                ser(dve.tensor_tensor(d[:, :], y0[:, :], y0[:, :], ALU.mult))
                ser(dve.tensor_tensor(d[:, :], s2[:, :], d[:, :], ALU.subtract))
                ser(dve.tensor_scalar(d[:, :], d[:, :], EPS, None, ALU.max))
                dve.sem_inc(asked, 1)
                dve.wait_ge(rooted, 3)
                ser(dve.tensor_tensor(a[:, :], a[:, :], b[:, :], ALU.add))
                dve.sem_inc(asked, 1)
                dve.wait_ge(rooted, 4)
                ser(dve.tensor_scalar(a[:, :], a[:, :], 1e-3, None, ALU.max))
                ser(dve.tensor_scalar(d[:, :], d[:, :], EPS, None, ALU.add))
                ser(dve.reciprocal(b[:, :], d[:, :]))
                ser(dve.tensor_tensor(f[:, :], a[:, :], b[:, :], ALU.mult))
                for g in range(NT // G):
                    dve.tensor_tensor(sp_[:, g * G:(g + 1) * G, 1:C], sp_[:, g * G:(g + 1) * G, 1:C],
                                      f[:, g * G:(g + 1) * G].unsqueeze(2).to_broadcast([P, G, C - 1]), ALU.mult)
                    dve.tensor_tensor(sp_[:, g * G:(g + 1) * G, 0], y0[:, g * G:(g + 1) * G], f[:, g * G:(g + 1) * G],
                                      ALU.mult).then_inc(grouped, 1)

            @block.scalar
            def _(act):
                with act.Fori(0, NT) as t:
                    act.wait_ge(clipped, t + 1)
                    act.activation(junk[:, 1:C], tile(sp_, t)[:, 1:C], ACT.Square,
                                   accum_out=s2[:, ds(t, 1)]).then_inc(squared, 1)
                    act.wait_ge(squared, t + 1)
                act.wait_ge(asked, 1)
                act.activation(y0[:, :], y0[:, :], ACT.Sqrt).then_inc(rooted, 1)
                act.wait_ge(asked, 2)
                act.activation(b[:, :], b[:, :], ACT.Sqrt).then_inc(rooted, 1)
                act.activation(d[:, :], d[:, :], ACT.Sqrt).then_inc(rooted, 1)
                act.wait_ge(asked, 3)
                act.activation(a[:, :], a[:, :], ACT.Ln).then_inc(rooted, 1)

            @block.sync
            def _(sp):
                for g in range(NT // G):
                    sp.wait_ge(grouped, g + 1)
                    sp.dma_start(k.v_t[:, g * G:(g + 1) * G, :], sp_[:, g * G:(g + 1) * G, :]).then_inc(stored, 16)
                sp.wait_ge(stored, 16 * (NT // G))


def stacked_heads(nc, k, b):
    S2 = 6 * D
    with Stage(nc, f"sh{b}") as s:
        R = 2
        v = s.sb("v", [P, R, C])
        vT = s.sb("vT", [P, 2, KC, P])
        qk = s.sb("qk", [P, 2, 2 * H, D])
        sq = s.sb("sq", [P, 2 * H, D])
        root = s.sb("root", [P, 2, 2 * H])
        rest, rest2 = s.sb("rest", [P, 2 * H, D]), s.sb("rest2", [P, 2 * H, D])
        hml = s.sb("hml", [P, 2 * H, 3, D], BF16)
        stq, stk = s.sb("stq", [P, H, P], BF16), s.sb("stk", [P, H, P], BF16)
        psT = s.ps("psT", [P, BANK])
        psQK = s.ps("psQK", [P, 2, BANK])
        psV = s.ps("psV", [P, BANK])
        psS = s.ps("psS", [P, 4, 2 * BANK], BF16)
        HB = H // 2
        (turned, vT_out, qk_ready, v_ready, v_out, clipped, squared, summed, rooted, led, chain, parts, stacked,
         st_turned, evac_dve, evac_act, start) = (
            s.sem(n) for n in ("turned", "vTout", "qk", "vr", "vout", "clipped", "squared", "summed", "rooted", "led",
                               "chain", "parts", "stacked", "stturned", "evacd", "evaca", "start"))
        got = s.sems("got", R)
        with nc.Block() as block:

            @block.gpsimd
            def _(pool):
                pool.memset(stq[:, :, S2:P], 0.0).then_inc(start, 1)
                pool.memset(stk[:, :, S2 + 3:P], 0.0).then_inc(start, 1)
                pool.memset(stk[:, :, S2:S2 + 3], 1.0).then_inc(start, 1)

            @block.sync
            def _(sp):
                with sp.Fori(0, TB // R) as i:
                    for j in range(R):
                        sp.wait_ge(turned, i * R + j + 1)
                        sp.dma_start(v[:, j, :], k.v_t[:, ds(b * TB + i * R + j, 1), :].rearrange(
                            "p a c -> p (a c)")).then_inc(got[j], 16)

            @block.tensor
            def _(pe):
                pe.sem_inc(turned, 2)

                def turn(t, j, lap):
                    pe.wait_ge(got[j], lap * 16 + 16)
                    pe.wait_ge(vT_out, t)
                    for kk in range(KC):
                        mm = pe.transpose(psT[:, kk * P:(kk + 1) * P], v[:, j, kk * P:(kk + 1) * P], k.ident[:, :])
                    mm.then_inc(turned, 1)

                def project(t, j):
                    pe.wait_ge(vT_out, t + 1)
                    pe.wait_ge(clipped, t + 1)
                    for kk in range(KC):
                        mm = pe.matmul(psQK[:, j, :], vT[:, j, kk, :], k.w1qkv[:, kk, 0:2 * C],
                                       start=(kk == 0), stop=(kk == KC - 1))
                    mm.then_inc(qk_ready, 1)
                    pe.wait_ge(v_out, t)
                    for kk in range(KC):
                        mm = pe.matmul(psV[:, 0:C], vT[:, j, kk, :], k.w1qkv[:, kk, 2 * C:3 * C],
                                       start=(kk == 0), stop=(kk == KC - 1))
                    mm.then_inc(v_ready, 1)

                def stacks(t):
                    pe.wait_ge(stacked, t + 1)
                    for n, st in enumerate((stq, stk)):
                        for half in range(2):
                            pe.wait_ge(evac_dve if half == 0 else evac_act, t * 2 + n)
                            for hh in range(HB):
                                mm = pe.transpose(psS[:, n * 2 + half, hh * P:(hh + 1) * P],
                                                  st[:, half * HB + hh, :], k.identb[:, :])
                            mm.then_inc(st_turned, 1)

                turn(0, 0, 0)
                project(0, 0)
                with pe.Fori(0, TB // 2 - 1) as i:
                    for j in range(2):
                        t = i * 2 + j
                        turn(t + 1, 1 - j, i + j)
                        project(t + 1, 1 - j)
                        stacks(t)
                turn(TB - 1, 1, TB // 2 - 1)
                project(TB - 1, 1)
                stacks(TB - 2)
                stacks(TB - 1)

            def evacuate(eng, copy, t, half, sem):
                for n, dst in enumerate((k.QT, k.KT)):
                    eng.wait_ge(st_turned, t * 4 + n * 2 + half + 1)
                    copy(dst[:, half * HB:(half + 1) * HB, ds(t * P, P)],
                         psS[:, n * 2 + half, :].rearrange("p (h t) -> p h t", h=HB)).then_inc(sem, 1)

            @block.vector
            def _(dve):
                dve.sem_inc(clipped, 2)
                dve.sem_inc(evac_dve, 1)

                def clip(t, j):
                    dve.wait_ge(qk_ready, t + 1)
                    dve.tensor_scalar(qk[:, j, :, :].rearrange("p h d -> p (h d)"), psQK[:, j, :], -5.0, 5.0,
                                      ALU.max, ALU.min).then_inc(clipped, 1)

                def split(t, j):
                    dve.wait_ge(rooted, t + 1)
                    dve.tensor_scalar(qk[:, j, 0:H, 0], root[:, j, 0:H], -1.0, None, ALU.mult)
                    dve.tensor_copy(qk[:, j, H:2 * H, 0], root[:, j, H:2 * H]).then_inc(led, 1)
                    dve.wait_ge(led, t + 1)
                    dve.wait_ge(stacked, t)
                    dve.tensor_copy(hml[:, :, 0, :], qk[:, j, :, :]).then_inc(chain, 1)
                    dve.wait_ge(chain, t * 3 + 1)
                    dve.tensor_tensor(rest[:, :, :], qk[:, j, :, :], hml[:, :, 0, :], ALU.subtract).then_inc(chain, 1)
                    dve.wait_ge(chain, t * 3 + 2)
                    dve.tensor_copy(hml[:, :, 1, :], rest[:, :, :]).then_inc(chain, 1)
                    dve.wait_ge(chain, t * 3 + 3)
                    dve.tensor_tensor(hml[:, :, 2, :], rest[:, :, :], hml[:, :, 1, :], ALU.subtract).then_inc(parts, 1)

                def sums(t, j):
                    dve.wait_ge(squared, t + 1)
                    dve.tensor_reduce(root[:, j, :], sq[:, :, 1:D], AX.X, ALU.add).then_inc(summed, 1)
                    dve.wait_ge(summed, t * 2 + 1)
                    dve.tensor_scalar(root[:, j, :], root[:, j, :], 1.0, EPS, ALU.add, ALU.add).then_inc(summed, 1)

                clip(0, 0)
                sums(0, 0)
                with dve.Fori(0, TB // 2 - 1) as i:
                    for j in range(2):
                        t = i * 2 + j
                        clip(t + 1, 1 - j)
                        split(t, j)
                        sums(t + 1, 1 - j)
                        evacuate(dve, dve.tensor_copy, t, 0, evac_dve)
                clip(TB - 1, 1)
                split(TB - 2, 0)
                sums(TB - 1, 1)
                evacuate(dve, dve.tensor_copy, TB - 2, 0, evac_dve)
                split(TB - 1, 1)
                evacuate(dve, dve.tensor_copy, TB - 1, 0, evac_dve)

            @block.scalar
            def _(act):
                act.wait_ge(start, 3)
                act.sem_inc(evac_act, 1)

                def lead(t, j):
                    act.wait_ge(turned, t + 3)
                    act.activation(vT[:, j, :, :], psT[:, 0:C].rearrange("p (k c) -> p k c", k=KC),
                                   ACT.Copy).then_inc(vT_out, 1)

                def squares(t, j):
                    act.wait_ge(clipped, t + 3)
                    act.wait_ge(summed, t * 2)
                    act.activation(sq[:, :, :], qk[:, j, :, :], ACT.Square).then_inc(squared, 1)
                    act.wait_ge(v_ready, t + 1)
                    act.activation(k.V[:, ds(t, 1), :].rearrange("p a c -> p (a c)"), psV[:, 0:C],
                                   ACT.Copy).then_inc(v_out, 1)

                def roots(t, j):
                    act.wait_ge(summed, t * 2 + 2)
                    act.activation(root[:, j, :], root[:, j, :], ACT.Sqrt).then_inc(rooted, 1)

                def stack(t):
                    act.wait_ge(parts, t + 1)
                    act.wait_ge(st_turned, t * 4)
                    q, kk = hml[:, 0:H, :, :], hml[:, H:2 * H, :, :]

                    def secs(st, a, n):
                        return st[:, :, a * D:(a + n) * D].rearrange("p h (s d) -> p h s d", s=n)

                    act.activation(secs(stq, 0, 3), q[:, :, 0:1, :].to_broadcast([P, H, 3, D]), ACT.Copy)
                    act.activation(secs(stq, 3, 2), q[:, :, 1:2, :].to_broadcast([P, H, 2, D]), ACT.Copy)
                    act.activation(secs(stq, 5, 1), q[:, :, 2:3, :], ACT.Copy)
                    act.activation(secs(stk, 0, 3), kk, ACT.Copy)
                    act.activation(secs(stk, 3, 2), kk[:, :, 0:2, :], ACT.Copy)
                    act.activation(secs(stk, 5, 1), kk[:, :, 0:1, :], ACT.Copy).then_inc(stacked, 1)

                def copy(o, i):
                    return act.activation(o, i, ACT.Copy)

                lead(0, 0)
                squares(0, 0)
                roots(0, 0)
                with act.Fori(0, TB // 2 - 1) as i:
                    for j in range(2):
                        t = i * 2 + j
                        lead(t + 1, 1 - j)
                        squares(t + 1, 1 - j)
                        stack(t)
                        roots(t + 1, 1 - j)
                        evacuate(act, copy, t, 1, evac_act)
                lead(TB - 1, 1)
                squares(TB - 1, 1)
                stack(TB - 2)
                roots(TB - 1, 1)
                evacuate(act, copy, TB - 2, 1, evac_act)
                stack(TB - 1)
                evacuate(act, copy, TB - 1, 1, evac_act)


def attention(nc, k, b):
    KT16 = TB
    QC = TS // BANK
    GM = 4
    UN = 2 * BANK
    VW = 32
    with Stage(nc, f"at{b}") as s:
        pexp = s.sb("pexp", [P, 4, UN])
        vst = s.sb("vst", [P, 2, KT16, VW])
        ksumT = s.sb("ksumT", [P, 2, TS // GM], BF16)
        mx = s.sb("mx", [P, KT16])
        sa, sb_ = s.sb("sa", [P, KT16]), s.sb("sb", [P, KT16])
        shift = s.sb("shift", [P, KT16, 3], BF16)
        oT = s.sb("oT", [P, BANK])
        inv = s.sb("inv", [P, QC, QC])
        psS = s.ps("psS", [P, 2, UN])
        psO = s.ps("psO", [P, BANK])
        psM = s.ps("psM", [P, 2, BANK])
        psX = s.ps("psX", [P, BANK])
        (scored, raised, weighed, v_ready, o_out, o_turned, maxed, reduced, k_ready, q_ready, shifted, x_turned, x_free,
         chain, divided, start) = (
            s.sem(n) for n in ("scored", "raised", "weighed", "vready", "oout", "oturned", "maxed", "reduced", "kready",
                               "qready", "shifted", "xturned", "xfree", "chain", "divided", "start"))

        def shift_use(h, half):
            return 1 + half if isinstance(h, int) and h == 0 else h * 3 + half

        with nc.Block() as block:

            def head_of(ap, h):
                return ap[:, ds(h, 1), :].rearrange("p a t -> p (a t)")

            @block.gpsimd
            def _(pool):
                def take_v(h, j):
                    pool.tensor_copy(vst[:, j, :, 0:D], k.V[:, :, ds(h * D, D)]).then_inc(v_ready, 1)

                pool.memset(vst[:, :, :, :], 0.0).then_inc(start, 1)
                pool.wait_ge(start, 1)
                pool.memset(vst[:, :, :, D:D + 1], 1.0).then_inc(start, 1)
                pool.wait_ge(start, 2)
                take_v(0, 0)
                take_v(1, 1)
                with pool.Fori(0, H // 2 - 1) as i:
                    for j in range(2):
                        pool.wait_ge(weighed, (i * 2 + j + 1) * KT16 + 2)
                        take_v(i * 2 + j + 2, j)

            @block.tensor
            def _(pe):
                def scores(h, kt, u2):
                    u = h * 2 * KT16 + kt * 2 + u2
                    pe.wait_ge(raised, u + 1)
                    for c in range(2):
                        mm = pe.matmul(psS[:, u2, c * BANK:(c + 1) * BANK],
                                       k.KT[:, ds(h, 1), kt * P:(kt + 1) * P].rearrange("p a t -> p (a t)"),
                                       k.QT[:, ds(h, 1), u2 * UN + c * BANK:u2 * UN + (c + 1) * BANK].rearrange(
                                           "p a t -> p (a t)"), start=True, stop=True)
                    mm.then_inc(scored, 1)

                def weigh(h, j, kt):
                    pe.wait_ge(raised, h * 2 * KT16 + kt * 2 + 4)
                    if kt == 0:
                        pe.wait_ge(o_out, h)
                        pe.wait_ge(v_ready, h + 1)
                    for c in range(QC):
                        mm = pe.matmul(psO[c * VW:(c + 1) * VW, :], vst[:, j, kt, :],
                                       pexp[:, (kt % 2) * 2 + c // 2, (c % 2) * BANK:(c % 2 + 1) * BANK],
                                       start=(kt == 0), stop=(kt == KT16 - 1))
                    mm.then_inc(weighed, 1)

                def means(h, j, n):
                    if n == 0:
                        pe.wait_ge(k_ready, h + 1)
                    pe.wait_ge(reduced, h * KT16 + n + 1)
                    pe.matmul(psM[:, n % 2, :],
                              k.QT[:, ds(h, 1), n * P:(n + 1) * P].rearrange("p a t -> p (a t)"),
                              ksumT[:, j, :], start=True, stop=True).then_inc(maxed, 1)

                def turn_shift(h, half):
                    if half == 0:
                        pe.wait_ge(shifted, h + 1)
                    pe.wait_ge(x_free, shift_use(h, half) - 1)
                    view = psX[:, :].bitcast(BF16)
                    for n in range(KT16 // 2):
                        mm = pe.transpose(view[6 * D:6 * D + 3, n * P:(n + 1) * P],
                                          shift[:, half * (KT16 // 2) + n, :], k.identb[:, :])
                    mm.then_inc(x_turned, 1)

                def turn_out(h):
                    pe.wait_ge(o_out, h + 1)
                    pe.wait_ge(x_free, h * 3 + 4)
                    for c in range(QC):
                        mm = pe.transpose(psX[:, c * P:(c + 1) * P], oT[:, c * P:(c + 1) * P], k.ident[:, :])
                    mm.then_inc(x_turned, 1)

                def head(h, j, first=False, last=False):
                    pe.wait_ge(q_ready, h + 1)
                    for kt in range(KT16):
                        scores(h, kt, 0)
                        scores(h, kt, 1)
                        if kt:
                            weigh(h, j, kt - 1)
                        elif not first:
                            weigh(h - 1, 1 - j, KT16 - 1)
                        if kt < KT16 // 2 and not last:
                            means(h + 1, 1 - j, 2 * kt)
                            means(h + 1, 1 - j, 2 * kt + 1)
                        if kt == 2 and not first:
                            turn_out(h - 1)
                        if kt in (KT16 - 5, KT16 - 3) and not last:
                            turn_shift(h + 1, (kt - KT16 + 5) // 2)

                pe.wait_ge(start, 2)
                for n in range(KT16):
                    means(0, 0, n)
                for half in range(2):
                    turn_shift(0, half)
                head(0, 0, first=True)
                with pe.Fori(0, H // 2 - 1) as i:
                    head(i * 2 + 1, 1)
                    head(i * 2 + 2, 0)
                head(H - 1, 1, last=True)
                weigh(H - 1, 1, KT16 - 1)
                pe.wait_ge(o_out, H)
                pe.wait_ge(x_free, 3 * H - 1)
                for c in range(QC):
                    mm = pe.transpose(psX[:, c * P:(c + 1) * P], oT[:, c * P:(c + 1) * P], k.ident[:, :])
                mm.then_inc(x_turned, 1)

            @block.scalar
            def _(act):
                act.sem_inc(raised, 2)
                with act.Fori(0, H * KT16 // 2) as i:
                    for m in range(4):
                        act.wait_ge(scored, i * 4 + m + 1)
                        if m % 2 == 0:
                            act.wait_ge(weighed, i * 2 + m // 2 + 1)
                        act.activation(pexp[:, m, :], psS[:, m % 2, :], ACT.Exp, scale=D ** -0.5).then_inc(raised, 1)

            @block.vector
            def _(dve):
                dve.sem_inc(weighed, 2)
                dve.sem_inc(reduced, 2)

                def sum_keys(h, j):
                    with nc.allow_low_precision(reason="the shift need not be exact"):
                        dve.tensor_reduce(ksumT[:, j, :], head_of(k.KT, h).rearrange("p (g m) -> p g m", m=GM),
                                          AX.X, ALU.add).then_inc(k_ready, 1)

                def reduce(h, n):
                    dve.wait_ge(maxed, h * KT16 + n + 1)
                    dve.tensor_reduce(mx[:, n:n + 1], psM[:, n % 2, :], AX.X, ALU.max).then_inc(reduced, 1)

                def step(h, n, ins):
                    ins.then_inc(chain, 1)
                    dve.wait_ge(chain, h * 7 + n + 1)

                def make_shift(h):
                    dve.wait_ge(reduced, h * KT16 + KT16 + 2)
                    step(h, 0, dve.tensor_scalar(sa[:, :], mx[:, :], 0.25, 280.0, ALU.mult, ALU.add))
                    step(h, 1, dve.tensor_scalar(sa[:, :], sa[:, :], -280.0, None, ALU.min))
                    step(h, 2, dve.scalar_tensor_tensor(sb_[:, :], mx[:, :], 0.25, sa[:, :], ALU.mult, ALU.max))
                    step(h, 3, dve.tensor_scalar(sb_[:, :], sb_[:, :], -1.0, None, ALU.mult))
                    step(h, 4, dve.tensor_copy(shift[:, :, 0], sb_[:, :]))
                    step(h, 5, dve.tensor_tensor(sa[:, :], sb_[:, :], shift[:, :, 0], ALU.subtract))
                    step(h, 6, dve.tensor_copy(shift[:, :, 1], sa[:, :]))
                    dve.tensor_tensor(shift[:, :, 2], sa[:, :], shift[:, :, 1], ALU.subtract).then_inc(shifted, 1)

                def put_shift(h, half):
                    dve.wait_ge(x_turned, shift_use(h, half))
                    ins = dve.tensor_copy(
                        k.QT[6 * D:6 * D + 3, ds(h, 1), half * UN:(half + 1) * UN].rearrange("p a t -> p (a t)"),
                        psX[:, :].bitcast(BF16)[6 * D:6 * D + 3, :])
                    ins.then_inc(x_free, 1)
                    if half == 1:
                        dve.wait_ge(x_free, shift_use(h, 1))
                        dve.sem_inc(q_ready, 1)

                def take_out(h):
                    dve.wait_ge(weighed, h * KT16 + KT16 + 2)
                    dve.wait_ge(x_turned, h * 3 + 2)
                    dve.tensor_copy(oT[:, :], psO[:, :]).then_inc(o_out, 1)

                def divide(h, count):
                    dve.wait_ge(x_turned, count)
                    o = psX[:, :].rearrange("p (c j d) -> p c j d", c=QC, j=QC)
                    dve.reciprocal(inv[:, :, :], o[:, :, :, D]).then_inc(divided, 1)
                    dve.wait_ge(divided, h + 1)
                    dve.tensor_tensor(k.O[:, :, ds(h * D, D)].rearrange("p (j c) d -> p c j d", j=QC),
                                      o[:, :, :, 0:D], inv[:, :, :].unsqueeze(3).to_broadcast([P, QC, QC, D]),
                                      ALU.mult).then_inc(x_free, 1)

                def head(h, first=False, last=False):
                    if not last:
                        reduce(h + 1, 0)
                        reduce(h + 1, 1)
                    if not first:
                        take_out(h - 1)
                    for n in range(2, 6):
                        if not last:
                            reduce(h + 1, n)
                    if not first:
                        divide(h - 1, h * 3 + 2)
                    if last:
                        return
                    for n in range(6, KT16):
                        reduce(h + 1, n)
                    make_shift(h + 1)
                    put_shift(h + 1, 0)
                    put_shift(h + 1, 1)

                sum_keys(0, 0)
                for n in range(KT16):
                    reduce(0, n)
                make_shift(0)
                put_shift(0, 0)
                put_shift(0, 1)
                sum_keys(1, 1)
                head(0, first=True)
                sum_keys(2, 0)
                with dve.Fori(0, H // 2 - 2) as i:
                    head(i * 2 + 1)
                    sum_keys(i * 2 + 3, 1)
                    head(i * 2 + 2)
                    sum_keys(i * 2 + 4, 0)
                head(H - 3)
                sum_keys(H - 1, 1)
                head(H - 2)
                head(H - 1, last=True)
                take_out(H - 1)
                divide(H - 1, 3 * H)


def attention_out(nc, k, b):
    with Stage(nc, f"ao{b}") as s:
        x2 = s.sb("x2", [P, TB, C])
        u = s.sb("u", [P, TB, C])
        o = s.sb("o", [P, 2, C])
        oT = s.sb("oT", [P, 2, KC, P])
        junk = s.sb("junk", [P, TB, C])
        s2, vn, e1, e2, t2, pl, sm, g = (s.sb(v, [P, TB]) for v in ("s2", "vn", "e1", "e2", "t2", "pl", "sm", "g"))
        psT = s.ps("psT", [P, 2, BANK])
        psU = s.ps("psU", [P, 2, BANK])
        copied, turned, oT_out, u_ready, u_out, squared, chain, asked, done = (
            s.sem(v) for v in ("copied", "turned", "oTout", "uready", "uout", "squared", "chain", "asked", "done"))
        x2_in, x3_out, done_act = s.sem("x2in"), s.sem("x3out"), s.sem("doneact")
        with nc.Block() as block:

            @block.sync
            def _(sp):
                sp.dma_start(x2[:, :, :], k.x2_t[:, b * TB:(b + 1) * TB, :]).then_inc(x2_in, 16)
                sp.wait_ge(done, 2)
                sp.dma_start(k.x3_t[:, b * TB:(b + 1) * TB, :], u[:, :, :]).then_inc(x3_out, 16)
                sp.wait_ge(x3_out, 16)

            @block.tensor
            def _(pe):
                pe.sem_inc(turned, 2)
                with pe.Fori(0, TB // 2) as i:
                    for j in range(2):
                        t = i * 2 + j
                        pe.wait_ge(copied, t + 1)
                        pe.wait_ge(oT_out, t + 1)
                        for kk in range(KC):
                            mm = pe.transpose(psT[:, j, kk * P:(kk + 1) * P], o[:, j, kk * P:(kk + 1) * P],
                                              k.ident[:, :])
                        mm.then_inc(turned, 1)
                        pe.wait_ge(oT_out, t + 3)
                        pe.wait_ge(u_out, t + 1)
                        for kk in range(KC):
                            mm = pe.matmul(psU[:, j, 0:C], oT[:, j, kk, :], k.w1o[:, kk, :],
                                           start=(kk == 0), stop=(kk == KC - 1))
                        mm.then_inc(u_ready, 1)

            @block.vector
            def _(dve):
                dve.sem_inc(u_out, 2)
                ser = Serial(dve, chain)
                with dve.Fori(0, TB // 2) as i:
                    for j in range(2):
                        t = i * 2 + j
                        dve.wait_ge(turned, t + 1)
                        dve.tensor_copy(o[:, j, :], tile(k.O, t)).then_inc(copied, 1)
                        dve.wait_ge(u_ready, t + 1)
                        dve.tensor_copy(tile(u, t), psU[:, j, 0:C]).then_inc(u_out, 1)
                dve.wait_ge(squared, TB)
                ser(dve.tensor_scalar(vn[:, :], s2[:, :], 0.0, EPS, ALU.max, ALU.add))
                dve.sem_inc(asked, 1)
                dve.wait_ge(done_act, 1)
                ser(dve.tensor_scalar(vn[:, :], vn[:, :], 5.0, None, ALU.min))
                dve.sem_inc(asked, 1)
                ser(dve.tensor_tensor(t2[:, :], vn[:, :], vn[:, :], ALU.mult))
                ser(dve.tensor_scalar(pl[:, :], t2[:, :], 1.0 / 42.0, 1.0, ALU.mult, ALU.add))
                ser(dve.scalar_tensor_tensor(pl[:, :], t2[:, :], 1.0 / 20.0, pl[:, :], ALU.mult, ALU.mult))
                ser(dve.tensor_scalar(pl[:, :], pl[:, :], 1.0, None, ALU.add))
                ser(dve.scalar_tensor_tensor(pl[:, :], t2[:, :], 1.0 / 6.0, pl[:, :], ALU.mult, ALU.mult))
                ser(dve.tensor_scalar(pl[:, :], pl[:, :], 1.0, None, ALU.add))
                ser(dve.tensor_tensor(pl[:, :], pl[:, :], vn[:, :], ALU.mult))
                ser(dve.tensor_scalar(sm[:, :], vn[:, :], 0.5, None, ALU.is_lt))
                dve.wait_ge(done_act, 3)
                ser(dve.tensor_tensor(e1[:, :], e1[:, :], e2[:, :], ALU.subtract))
                ser(dve.tensor_scalar(e1[:, :], e1[:, :], 0.5, None, ALU.mult))
                ser(dve.tensor_tensor(pl[:, :], pl[:, :], e1[:, :], ALU.subtract))
                ser(dve.tensor_tensor(pl[:, :], pl[:, :], sm[:, :], ALU.mult))
                ser(dve.tensor_tensor(e1[:, :], e1[:, :], pl[:, :], ALU.add))
                ser(dve.tensor_scalar(t2[:, :], vn[:, :], EPS, None, ALU.add))
                ser(dve.reciprocal(e2[:, :], t2[:, :]))
                ser(dve.tensor_tensor(g[:, :], e1[:, :], e2[:, :], ALU.mult))
                ser(dve.tensor_tensor(u[:, :, :], u[:, :, :], g[:, :].unsqueeze(2).to_broadcast([P, TB, C]), ALU.mult))
                ser(dve.tensor_scalar(u[:, :, :], u[:, :, :], -8.0, 8.0, ALU.max, ALU.min))
                dve.sem_inc(asked, 1)
                dve.wait_ge(done_act, 4)
                ser(dve.tensor_reduce(s2[:, :], junk[:, :, 1:C], AX.X, ALU.add))
                ser(dve.tensor_scalar(s2[:, :], s2[:, :], 1.0, EPS, ALU.add, ALU.add))
                dve.sem_inc(asked, 1)
                dve.wait_ge(done_act, 5)
                ser(dve.tensor_copy(u[:, :, 0], s2[:, :]))
                dve.wait_ge(x2_in, 16)
                dve.tensor_tensor(u[:, :, :], u[:, :, :], x2[:, :, :], ALU.add).then_inc(done, 2)

            @block.scalar
            def _(act):
                act.sem_inc(oT_out, 2)
                with act.Fori(0, TB // 2) as i:
                    for j in range(2):
                        t = i * 2 + j
                        act.wait_ge(turned, t + 3)
                        act.activation(oT[:, j, :, :], psT[:, j, 0:C].rearrange("p (k c) -> p k c", k=KC),
                                       ACT.Copy).then_inc(oT_out, 1)
                        act.wait_ge(u_out, t + 3)
                        act.activation(junk[:, 0, 1:C], tile(u, t)[:, 1:C], ACT.Square,
                                       accum_out=s2[:, ds(t, 1)]).then_inc(squared, 1)
                        act.wait_ge(squared, t + 1)
                act.wait_ge(asked, 1)
                act.activation(vn[:, :], vn[:, :], ACT.Sqrt).then_inc(done_act, 1)
                act.wait_ge(asked, 2)
                act.activation(e1[:, :], vn[:, :], ACT.Exp).then_inc(done_act, 1)
                act.activation(e2[:, :], vn[:, :], ACT.Exp, scale=-1.0).then_inc(done_act, 1)
                act.wait_ge(asked, 3)
                act.activation(junk[:, :, :], u[:, :, :], ACT.Square).then_inc(done_act, 1)
                act.wait_ge(asked, 4)
                act.activation(s2[:, :], s2[:, :], ACT.Sqrt).then_inc(done_act, 1)


def load_expert_weights(nc, k, a):
    with Stage(nc, "lw") as s:
        cleared, b_in = s.sem("cleared"), s.sem("bin")
        picked, chain = s.sem("picked"), s.sem("chain")
        raw = s.sb("raw", [P, HG, 2, HW])
        part = s.sb("part", [P, 2, HG * 2 * HW], BF16)
        with nc.Block() as block:

            @block.sync
            def _(sp):
                sp.wait_ge(cleared, 1)
                for q in range(3):
                    for n, w in enumerate(("L1_ffn_bg", "L1_ffn_b1")):
                        sp.dma_start(raw[32 * q:32 * q + E, :, n, :],
                                     a[w].rearrange("e (g c) -> e g c", g=HG)).then_inc(b_in, 16)
                for e in range(E):
                    for n, w in enumerate(("L1_ffn_Wg", "L1_ffn_W1")):
                        for kk in range(KC):
                            sp.dma_start(k.wgu[:, e, kk, :, n, :],
                                         a[w][e, kk * P:(kk + 1) * P, :].rearrange("p (g c) -> p g c", g=HG)
                                         ).then_inc(k.w_in[e], 16)
                    sp.dma_start(k.w2b[0:HP, e, :, :],
                                 a["L1_ffn_W2"][e, :, :].rearrange("(n p) c -> p n c", p=HP)).then_inc(k.w_in[e], 16)
                    sp.dma_start(k.w2b[HP:HP + 1, e, HK - 1, :], a["L1_ffn_b2"][e:e + 1, :]).then_inc(k.w_in[e], 16)

            @block.gpsimd
            def _(pool):
                pool.memset(k.pick[:, :, :], 0.0).then_inc(picked, 1)
                pool.wait_ge(picked, 1)
                for q in range(3):
                    pool.affine_select(out=k.pick[32 * q:32 * (q + 1), :, :], in_=k.pick[32 * q:32 * (q + 1), :, :],
                                       compare_op=ALU.not_equal, fill=1.0, base=0, pattern=[[-1, E], [0, P]],
                                       channel_multiplier=1).then_inc(picked, 1)

            @block.vector
            def _(dve):
                ser = Serial(dve, chain)
                dve.memset(raw[:, :, :, :], 0.0).then_inc(cleared, 1)
                ser(dve.memset(k.bias[:, :], 0.0))
                dve.wait_ge(b_in, 16 * 6)
                flat = raw[:, :, :, :].rearrange("p g n c -> p (g n c)")
                ser(dve.tensor_copy(part[:, 0, :], flat))
                ser(dve.tensor_copy(k.bias[0:32, :], part[0:32, 0, :]))
                ser(dve.tensor_tensor(flat, flat, part[:, 0, :], ALU.subtract))
                ser(dve.tensor_copy(part[:, 1, :], flat))
                ser(dve.tensor_copy(k.bias[32:64, :], part[32:64, 1, :]))
                ser(dve.tensor_tensor(k.bias[64:96, :], flat[64:96, :], part[64:96, 1, :], ALU.subtract))


def load_stream(nc, k, src):
    G = 8
    with Stage(nc, "lds") as s:
        in_ = s.sem("in")
        with nc.Block() as block:

            @block.scalar
            def _(act):
                for g in range(NT // G):
                    act.dma_start(k.x[:, g * G:(g + 1) * G, :], src[:, g * G:(g + 1) * G, :]).then_inc(in_, 16)
                act.wait_ge(in_, 16 * (NT // G))


def experts1(nc, k):
    G2 = 2 * HW
    with Stage(nc, "ex1") as s:
        idx, odx = s.sb("idx", [P, GR, 1], U32), s.sb("odx", [P, 2, 1], U32)
        xg = s.sb("xg", [P, GR, C])
        xT = s.sb("xT", [P, 2, KC, P])
        sg = s.sb("sg", [P, HG, HW])
        h = s.sb("h", [P, 2, HG, HW])
        hT = s.sb("hT", [P, 2, HK, P])
        y = s.sb("y", [P, 2, C])
        psX = s.ps("psX", [P, 2, BANK])
        psH = s.ps("psH", [P, HG, BANK])
        psG = s.ps("psG", [P, 2, BANK])
        psY = s.ps("psY", [P, BANK])
        HB = HK // 2
        (x_turned, x_out, h_ready, gated, h_done, h_turned, h_out, y_ready, y_done, start) = (
            s.sem(v) for v in ("xturned", "xout", "hready", "gated", "hdone", "hturned", "hout", "yready",
                               "ydone", "start"))
        got, put = s.sems("got", GR), s.sems("put", 2)
        with nc.Block() as block:

            @block.gpsimd
            def _(pool):
                def gather(t, g, lap):
                    pool.wait_ge(got[g], lap * 16)
                    pool.wait_ge(x_turned, t + 1)
                    pool.tensor_copy(idx[:, g, :], k.tok[:, ds(t, 1)])
                    pool.drain()
                    pool.indirect_dma_start(xg[:, g, :], None, k.xn_d,
                                            bass.IndirectOffsetOnAxis(idx[:, g, :], 0)).then_inc(got[g], 16)

                def scatter(t, j, lap):
                    pool.wait_ge(put[j], lap * 16)
                    pool.wait_ge(y_done, t + 3)
                    pool.tensor_copy(odx[:, j, :], k.dst[:, ds(t, 1)])
                    pool.drain()
                    pool.indirect_dma_start(k.y_d, bass.IndirectOffsetOnAxis(odx[:, j, :], 0), y[:, j, :],
                                            None).then_inc(put[j], 16)

                for g in range(GR):
                    gather(g, g, 0)
                with pool.Fori(0, NTILE // GR - 1) as i:
                    for g in range(GR):
                        t = i * GR + g
                        gather(t + GR, g, i + 1)
                        scatter(t, g % 2, i * 2 + g // 2)
                for g in range(GR):
                    t = NTILE - GR + g
                    scatter(t, g % 2, t // 2)
                for j in range(2):
                    pool.wait_ge(put[j], 16 * (NTILE // 2))

            @block.tensor
            def _(pe):
                pe.sem_inc(x_turned, GR)
                pe.sem_inc(h_turned, 4)

                def expert(t):
                    return pe.value_load(k.tile_expert[0:1, ds(t, 1)], min_val=0, max_val=E - 1)

                def turn(t, g, lap):
                    pe.wait_ge(got[g], lap * 16 + 16)
                    pe.wait_ge(x_out, t + 1)
                    for kk in range(KC):
                        mm = pe.transpose(psX[:, g % 2, kk * P:(kk + 1) * P], xg[:, g, kk * P:(kk + 1) * P],
                                          k.ident[:, :])
                    mm.then_inc(x_turned, 1)

                def up(t, j, e):
                    pe.wait_ge(x_out, t + 3)
                    for n in range(HG):
                        pe.wait_ge(h_done, t * HG + n + 1)
                        pe.matmul(psH[:, n, 0:G2], k.pick[:, ds(e, 1), :].rearrange("p a c -> p (a c)"),
                                  k.bias[:, n * G2:(n + 1) * G2], start=True, stop=False)
                        for kk in range(KC):
                            mm = pe.matmul(psH[:, n, 0:G2], xT[:, j, kk, :],
                                           k.wgu[:, ds(e, 1), kk, n, :, :].rearrange("p a n c -> p (a n c)"),
                                           start=False, stop=(kk == KC - 1))
                        mm.then_inc(h_ready, 1)

                def down(t, j, e):
                    pe.wait_ge(h_done, t * HG + 2 * HG)
                    for n in range(2):
                        pe.wait_ge(h_out, t * 2 + n + 1)
                        for m in range(HB):
                            g = n * HB + m
                            mm = pe.transpose(psG[0:HP, n, m * P:(m + 1) * P],
                                              h[:, j, g // 2, (g % 2) * HP:(g % 2 + 1) * HP], k.ident[:, :])
                        mm.then_inc(h_turned, 1)
                    pe.wait_ge(y_done, t + 2)
                    for g in range(HK):
                        if g % HB == 0:
                            pe.wait_ge(h_out, t * 2 + g // HB + 3)
                        rows = HP + (g == HK - 1)
                        mm = pe.matmul(psY[:, 0:C], hT[0:rows, j, g, :],
                                       k.w2b[0:rows, ds(e, 1), g, :].rearrange("p a c -> p (a c)"),
                                       start=(g == 0), stop=(g == HK - 1))
                    mm.then_inc(y_ready, 1)

                for e in range(E):
                    pe.wait_ge(k.w_in[e], 16 * 6)
                pe.wait_ge(start, 2)
                turn(0, 0, 0)
                turn(1, 1, 0)
                up(0, 0, expert(0))
                with pe.Fori(0, NTILE // GR - 1) as i:
                    for g in range(GR):
                        t = i * GR + g
                        turn(t + 2, (g + 2) % GR, i + (g + 2) // GR)
                        up(t + 1, (g + 1) % 2, expert(t + 1))
                        down(t, g % 2, expert(t))
                for t in range(NTILE - GR, NTILE):
                    if t + 2 < NTILE:
                        turn(t + 2, (t + 2) % GR, (t + 2) // GR)
                    if t + 1 < NTILE:
                        up(t + 1, (t + 1) % 2, expert(t + 1))
                    down(t, t % 2, expert(t))

            @block.scalar
            def _(act):
                act.sem_inc(x_out, 2)

                def lead(t, j):
                    act.wait_ge(x_turned, t + 1 + GR)
                    act.activation(xT[:, j, :, :], psX[:, j, 0:C].rearrange("p (k c) -> p k c", k=KC),
                                   ACT.Copy).then_inc(x_out, 1)

                def gate(t):
                    for n in range(HG):
                        act.wait_ge(h_ready, t * HG + n + 1)
                        act.wait_ge(h_done, t * HG + n + 1)
                        act.activation(sg[:, n, :], psH[:, n, 0:HW], ACT.Silu).then_inc(gated, 1)

                def turned(t, j):
                    act.wait_ge(h_turned, t * 2 + 6)
                    act.wait_ge(h_out, t * 2 + 3)
                    act.activation(hT[0:HP, j, HB:HK, :], psG[0:HP, 1, 0:HB * P].rearrange("p (k c) -> p k c", k=HB),
                                   ACT.Copy).then_inc(h_out, 1)

                lead(0, 0)
                lead(1, 1)
                gate(0)
                with act.Fori(0, NTILE // 2 - 1) as i:
                    for j in range(2):
                        t = i * 2 + j
                        act.wait_ge(h_ready, t * HG + HG)
                        lead(t + 2, j)
                        gate(t + 1)
                        turned(t, j)
                gate(NTILE - 1)
                turned(NTILE - 2, 0)
                turned(NTILE - 1, 1)

            @block.vector
            def _(dve):
                dve.memset(hT[:, 0, HK - 1, :], 1.0).then_inc(start, 1)
                dve.memset(hT[:, 1, HK - 1, :], 1.0).then_inc(start, 1)
                dve.wait_ge(start, 2)
                dve.sem_inc(h_out, 2)
                dve.sem_inc(h_done, HG)
                dve.sem_inc(y_done, 2)

                def hidden(t, j):
                    dve.wait_ge(h_turned, t * 2 + 2)
                    for n in range(HG):
                        dve.wait_ge(gated, t * HG + n + 1)
                        dve.tensor_tensor(h[:, j, n, :], psH[:, n, HW:2 * HW], sg[:, n, :],
                                          ALU.mult).then_inc(h_done, 1)

                def turned(t, j):
                    dve.wait_ge(h_turned, t * 2 + 5)
                    dve.tensor_copy(hT[0:HP, j, 0:HB, :],
                                    psG[0:HP, 0, 0:HB * P].rearrange("p (k c) -> p k c", k=HB)).then_inc(h_out, 1)

                def weigh(t, j, lap):
                    dve.wait_ge(y_ready, t + 1)
                    dve.wait_ge(put[j], lap * 16)
                    dve.tensor_scalar(y[:, j, :], psY[:, 0:C], k.wgt[:, ds(t, 1)], None, ALU.mult).then_inc(y_done, 1)

                hidden(0, 0)
                with dve.Fori(0, NTILE // 2 - 1) as i:
                    for j in range(2):
                        t = i * 2 + j
                        hidden(t + 1, 1 - j)
                        turned(t, j)
                        weigh(t, j, i)
                hidden(NTILE - 1, 1)
                for j in range(2):
                    turned(NTILE - 2 + j, j)
                    weigh(NTILE - 2 + j, j, NTILE // 2 - 1)


def program(nc, a, out):
    k = Consts()
    top = Stage(nc, "top")
    with top:
        constants(nc, top, k)
        k.mean = top.sb("mean", [P, NT])
        k.rstd = top.sb("rstd", [P, NT])
        k.tok = top.sb("tok", [P, NTILE], I32)
        k.dst = top.sb("dst", [P, NTILE], I32)
        k.wgt = top.sb("wgt", [P, NTILE])
        k.tile_expert = top.sb("tile_expert", [1, NTILE], I32)
        k.tilebase = top.sb("tilebase", [P, NT])
        tile_bases(nc, k)
        k.xn_d = nc.dram_tensor("normed", [T, C], F32).ap()
        k.y_d = nc.dram_tensor("expert_rows", [2 * T + 2 * P, C], F32).ap()
        k.x2_d = nc.dram_tensor("stream", [T, C], F32).ap()
        k.x2_t = k.x2_d.rearrange("(t p) c -> p t c", p=P)
        k.x3_t = nc.dram_tensor("stream3", [T, C], F32).ap().rearrange("(t p) c -> p t c", p=P)
        k.v_t = nc.dram_tensor("tangents", [T, C], F32).ap().rearrange("(t p) c -> p t c", p=P)
        res = Stage(nc, "res")
        with res:
            k.x = res.sb("x", [P, NT, C])
            l0 = Stage(nc, "l0")
            with l0:
                k.wqkv = l0.sb("wqkv", [P, KC, 3 * C])
                k.wproj = l0.sb("wproj", [P, KC, C])
                k.gate = l0.sb("gate", [P, KC, E])
                k.w13 = l0.sb("w13", [P, E, KC, 2 * F0])
                k.w2 = l0.sb("w2", [P, E, KC, C])
                k.bproj = l0.sb("bproj", [P, C])
                load_x(nc, k, a["L0_attn_x"])
                squares = [(a["L0_attn_Wqkv"][i * C:(i + 1) * C, :], k.wqkv[:, :, i * C:(i + 1) * C]) for i in range(3)]
                squares.append((a["L0_attn_Wproj"], k.wproj[:, :, :]))

                def expert(w):
                    return lambda e: w[ds(e, 1), :, :].rearrange("a r c -> (a r) c")

                def into(w, c0):
                    return lambda e: w[:, ds(e, 1), :, c0:c0 + C].rearrange("p a k c -> p (a k) c")

                transpose_squares(nc, k, "w0", squares, [(a["L0_ffn_gate_w"], k.gate[:, :, :])],
                                  (E, [expert(a[w]) for w in ("L0_ffn_w1", "L0_ffn_w3", "L0_ffn_w2")],
                                   [into(k.w13, 0), into(k.w13, C), into(k.w2, 0)]))
                with Stage(nc, "la") as la:
                    k.qT = la.sb("qT", [P, KC, T])
                    k.kvblk = la.sb("kvblk", [P, NB, KC, P])
                    k.ksum = la.sb("ksum", [P, NB, KC, P])
                    ln_stats(nc, k, "ln0", k.x)
                    linear_attention_in(nc, k, la)
                    with Stage(nc, "bp") as s:
                        got = s.sem("got")
                        with nc.Block() as block:
                            @block.sync
                            def _(sp):
                                sp.dma_start(k.bproj[:, :], a["L0_attn_bproj"].partition_broadcast(P)).then_inc(got, 16)
                                sp.wait_ge(got, 16)
                    linear_attention_out(nc, k)
                ln_stats(nc, k, "ln1", k.x)
                route(nc, k, "rt0", 0, k.gate, k.x)
                experts0(nc, k)
            combine(nc, k, "cb0", None, k.x, k.x2_t)
            ln_stats(nc, k, "ln2", k.x)
            log_map(nc, k)
        l1 = Stage(nc, "l1")
        with l1:
            k.w1qkv = l1.sb("wqkv", [P, KC, 3 * C])
            k.w1o = l1.sb("wo", [P, KC, C])
            squares = [(a[f"L1_attn_W{n}"], k.w1qkv[:, :, i * C:(i + 1) * C]) for i, n in enumerate("qkv")]
            squares.append((a["L1_attn_Wo"], k.w1o[:, :, :]))
            transpose_squares(nc, k, "w1", squares, [])
            for b in range(NB):
                with Stage(nc, f"l1b{b}") as lb:
                    k.O = lb.sb("O", [P, TB, C])
                    with Stage(nc, f"l1c{b}") as lc:
                        k.V = lc.sb("V", [P, TB, C])
                        k.QT = lc.sb("QT", [P, H, TS], BF16)
                        k.KT = lc.sb("KT", [P, H, TS], BF16)
                        stacked_heads(nc, k, b)
                        attention(nc, k, b)
                    attention_out(nc, k, b)
        l2 = Stage(nc, "l2")
        with l2:
            k.wgu = l2.sb("wgu", [P, E, KC, HG, 2, HW])
            k.w2b = l2.sb("w2b", [P, E, HK, C])
            k.bias = l2.sb("bias", [P, HG * 2 * HW], BF16)
            k.pick = l2.sb("pick", [P, E, P], BF16)
            k.w_in = l2.sems("win", E)
            load_expert_weights(nc, k, a)
            with Stage(nc, "r4") as r4:
                k.x = r4.sb("x", [P, NT, C])
                k.cent = r4.sb("cent", [P, KC, E])
                load_stream(nc, k, k.x3_t)
                transpose_squares(nc, k, "wc", [], [(a["L1_ffn_centroid"], k.cent[:, :, :])])
                ln_stats(nc, k, "ln3", k.x)
                route(nc, k, "rt1", 1, k.cent, k.x)
            experts1(nc, k)
        combine(nc, k, "cb1", k.x3_t, None, out.rearrange("b (t p) c -> p (b t) c", p=P))


def tile_bases(nc, k):
    with Stage(nc, "tb") as s:
        with nc.Block() as block:

            @block.vector
            def _(dve):
                dve.tensor_scalar(k.tilebase[:, :], k.lane[:, 0:NT], float(P), None, ALU.mult)


INPUTS = ("L0_attn_x", "L0_attn_Wqkv", "L0_attn_Wproj", "L0_attn_bproj", "L0_ffn_gate_w", "L0_ffn_w1", "L0_ffn_w3",
          "L0_ffn_w2", "L1_attn_Wq", "L1_attn_Wk", "L1_attn_Wv", "L1_attn_Wo", "L1_ffn_centroid", "L1_ffn_Wg",
          "L1_ffn_bg", "L1_ffn_W1", "L1_ffn_b1", "L1_ffn_W2", "L1_ffn_b2")


def kernel(**inputs):
    import concourse.bacc as bacc
    import numpy as np
    from concourse.bass_utils import run_bass_kernel_spmd

    nc = bacc.Bacc("TRN2", target_bir_lowering=False, num_devices=1)
    arrays, args = {}, {}
    for name in INPUTS:
        array = np.ascontiguousarray(inputs[name])
        arrays["in_" + name] = array
        args[name] = nc.dram_tensor("in_" + name, array.shape, mybir.dt.from_np(array.dtype), kind="ExternalInput").ap()
    out = nc.dram_tensor("out", (NB, TS, C), F32, kind="ExternalOutput").ap()
    program(nc, args, out)
    result = run_bass_kernel_spmd(nc, [arrays], core_ids=[0])
    return result.results[0]["out"]
```

```python
from contextlib import ExitStack

import concourse.bass as bass
from concourse import mybir

ALU = mybir.AluOpType
ACT = mybir.ActivationFunctionType
AX = mybir.AxisListType
F32 = mybir.dt.float32
BF16 = mybir.dt.bfloat16
I32 = mybir.dt.int32
U32 = mybir.dt.uint32

P = 128
T, C = 4096, 256
KC = C // P
NT = T // P
NB = 2
TB = NT // NB
TS = T // NB
H, D = 16, 16
E = 8
F0 = 256
F1 = 684
HG, HW = 3, 228
HK, HP = 6, 114
NTILE = 2 * T // P + E
BANK = 512
LN_EPS = 1e-5
EPS = 1e-6
GR = 4
ds = bass.ds


class Serial:

    def __init__(self, eng, sem):
        self.eng, self.sem, self.n = eng, sem, 0

    def __call__(self, ins):
        ins.then_inc(self.sem, 1)
        self.n += 1
        self.eng.wait_ge(self.sem, self.n)


class Stage:

    def __init__(self, nc, name):
        self.nc, self.name, self.stack, self.held = nc, name, ExitStack(), []

    def __enter__(self):
        self.stack.__enter__()
        return self

    def __exit__(self, *a):
        if self.held and a[0] is None:
            self.nc.clear_and_free_semaphores(self.held)
            self.nc.all_engine_barrier()
        return self.stack.__exit__(*a)

    def close(self):
        self.__exit__(None, None, None)

    def sb(self, name, shape, dt=F32, side="left"):
        return self.stack.enter_context(self.nc.sbuf_tensor(f"{self.name}_{name}", shape, dt, side=side))

    def ps(self, name, shape, dt=F32):
        return self.stack.enter_context(self.nc.psum_tensor(f"{self.name}_{name}", shape, dt))

    def sem(self, name):
        self.held.append(self.nc.alloc_semaphore(f"{self.name}_{name}"))
        return self.held[-1]

    def sems(self, name, n):
        return [self.sem(f"{name}{i}") for i in range(n)]


class Step:

    def __init__(self, i, m, unroll, n):
        self.i, self.m, self.unroll, self.n = i, m, unroll, n

    def tile(self, lag=0):
        return self.i * self.unroll + self.m - lag

    def on(self, lag=0):
        return not isinstance(self.i, int) or 0 <= self.tile(lag) < self.n

    def slot(self, lag, ring):
        return (self.m - lag) % ring

    def lap(self, lag, ring):
        return self.i * (self.unroll // ring) + (self.m - lag) // ring

    def again(self, eng, sem, value):
        if not isinstance(value, int) or value > 0:
            eng.wait_ge(sem, value)


def steps(eng, n, unroll, depth):
    assert n % unroll == 0 and depth <= unroll
    for m in range(unroll):
        yield Step(0, m, unroll, n)
    with eng.Fori(1, n // unroll) as i:
        for m in range(unroll):
            yield Step(i, m, unroll, n)
    for m in range(depth):
        yield Step(n // unroll, m, unroll, n)


class Consts:
    pass


def bc(ap, shape):
    return ap.to_broadcast(shape)


def constants(nc, st, k):
    k.ident = st.sb("ident", [P, P])
    k.identb = st.sb("identb", [P, P], BF16)
    k.ones = st.sb("ones", [P, P])
    k.onesb = st.sb("onesb", [P, P], BF16)
    k.upperb = st.sb("upperb", [P, P], BF16)
    k.blockdiag = st.sb("blockdiag", [P, P])
    k.lane = st.sb("lane", [P, P])
    k.lane1 = st.sb("lane1", [P, 1])
    k.odd_rows = st.sb("odd_rows", [P, NTILE])
    with Stage(nc, "cst") as s:
        tmp = s.sb("tmp", [P, P], I32)
        tcol = s.sb("tcol", [P, 1], I32)
        todd = s.sb("todd", [P, NTILE], I32)
        filled, picked, turned = s.sem("filled"), s.sem("picked"), s.sem("turned")
        with nc.Block() as block:

            @block.gpsimd
            def _(pool):
                pool.memset(k.ident[:, :], 0.0).then_inc(filled, 1)
                pool.memset(k.ones[:, :], 1.0).then_inc(filled, 1)
                pool.memset(k.blockdiag[:, :], 1.0).then_inc(filled, 1)
                pool.iota(tmp[:, :], pattern=[[1, P]], base=0, channel_multiplier=0).then_inc(filled, 1)
                pool.iota(tcol[:, :], pattern=[[1, 1]], base=0, channel_multiplier=1).then_inc(filled, 1)
                pool.iota(todd[:, :].rearrange("p (a b) -> p a b", b=2), pattern=[[0, NTILE // 2], [P, 2]], base=0,
                          channel_multiplier=0).then_inc(filled, 1)
                pool.wait_ge(filled, 6)
                pool.affine_select(out=k.ident[:, :], in_=k.ident[:, :], compare_op=ALU.not_equal, fill=1.0,
                                   base=0, pattern=[[-1, P]], channel_multiplier=1).then_inc(picked, 1)
                pool.affine_select(out=k.upperb[:, :], in_=k.ones[:, :], compare_op=ALU.is_gt, fill=0.0,
                                   base=0, pattern=[[1, P]], channel_multiplier=-1).then_inc(picked, 1)
                bd = k.blockdiag[:, :].rearrange("p (h d) -> p h d", d=D)
                pool.affine_select(out=bd, in_=bd, compare_op=ALU.is_ge, fill=0.0,
                                   base=0, pattern=[[-D, P // D], [0, D]], channel_multiplier=1).then_inc(picked, 1)
                pool.wait_ge(picked, 3)
                pool.affine_select(out=bd, in_=bd, compare_op=ALU.is_ge, fill=0.0,
                                   base=D - 1, pattern=[[D, P // D], [0, D]], channel_multiplier=-1).then_inc(picked, 1)

            @block.vector
            def _(dve):
                dve.wait_ge(filled, 6)
                dve.tensor_copy(k.lane[:, :], tmp[:, :]).then_inc(turned, 1)
                dve.tensor_copy(k.odd_rows[:, :], todd[:, :]).then_inc(turned, 1)
                dve.tensor_copy(k.lane1[:, :], tcol[:, :]).then_inc(turned, 1)
                dve.tensor_copy(k.onesb[:, :], k.ones[:, :]).then_inc(turned, 1)
                dve.wait_ge(picked, 3)
                dve.tensor_copy(k.identb[:, :], k.ident[:, :]).then_inc(turned, 1)


def transpose_squares(nc, k, name, squares, small, looped=None):
    RING = 6
    with Stage(nc, name) as s:
        raw = s.sb("raw", [P, RING, KC, C])
        rawsm = s.sb("rawsm", [E, max(len(small), 1), C])
        ps = s.ps("ps", [P, RING, KC * C])
        pss = s.ps("pss", [P, BANK])
        loaded = s.sems("loaded", RING)
        sm_loaded = s.sem("sm_loaded")
        turned, out_dve, out_act, sm_turned, sm_out = (s.sem(x) for x in ("turned", "odve", "oact", "smt", "smo"))
        n0 = len(squares)
        per = len(looped[1]) if looped else 0
        steps = looped[0] * per // RING if looped else 0
        assert not looped or (looped[0] * per) % RING == 0 and RING % per == 0

        def rows(src):
            return src.rearrange("(b p) c -> p b c", p=P)

        def target(i, m, n):
            if m is None:
                return squares[n][1]
            e = i * (RING // per) + m // per
            return looped[2][m % per](e)

        def walk(eng, step):
            for n in range(n0):
                step(None, None, n, n % RING, n // RING)
            if looped:
                with eng.Fori(0, steps) as i:
                    for m in range(RING):
                        n = n0 + m
                        step(i, m, n, n % RING, i + n // RING)

        def again(eng, sem, per_lap, lap, n, extra=0):
            eng.wait_ge(sem, per_lap)

        with nc.Block() as block:

            @block.sync
            def _(sp):
                for j, (src, _) in enumerate(small):
                    sp.dma_start(rawsm[:, j, :], src).then_inc(sm_loaded, 16)

                def load(i, m, n, slot, lap):
                    if m is None:
                        src = squares[n][0]
                    else:
                        src = looped[1][m % per](i * (RING // per) + m // per)
                    if m is not None or n >= RING:
                        sp.wait_ge(turned, (i * RING if m is not None else 0) + n + 1)
                    sp.dma_start(raw[:, slot, :, :], rows(src)).then_inc(loaded[slot], 16)

                walk(sp, load)

            @block.tensor
            def _(pe):
                pe.sem_inc(turned, RING)

                def turn(i, m, n, slot, lap):
                    pe.wait_ge(loaded[slot], lap * 16 + 16)
                    if m is not None or n >= RING:
                        par = out_dve if n % 2 == 0 else out_act
                        pe.wait_ge(par, (i * (RING // 2) if m is not None else 0) + n // 2 + 1)
                    for kk in range(KC):
                        for b in range(KC):
                            mm = pe.transpose(ps[:, slot, kk * C + b * P:kk * C + (b + 1) * P],
                                              raw[:, slot, b, kk * P:(kk + 1) * P], k.ident[:, :])
                    mm.then_inc(turned, 1)

                walk(pe, turn)
                if small:
                    pe.wait_ge(sm_loaded, 16 * len(small))
                    for j in range(len(small)):
                        for kk in range(KC):
                            mm = pe.transpose(pss[:, (j * KC + kk) * E:(j * KC + kk + 1) * E],
                                              rawsm[:, j, kk * P:(kk + 1) * P], k.ident[0:E, 0:E])
                    mm.then_inc(sm_turned, 1)

            def copier(which, sem):
                def copy_out(eng, copy):
                    eng.sem_inc(sem, RING // 2)

                    def out(i, m, n, slot, lap):
                        if n % 2 != which:
                            return
                        eng.wait_ge(turned, (i * RING if m is not None else 0) + n + 1 + RING)
                        copy(target(i, m, n), ps[:, slot, :].rearrange("p (k c) -> p k c", k=KC)).then_inc(sem, 1)

                    walk(eng, out)
                return copy_out

            @block.vector
            def _(dve):
                copier(0, out_dve)(dve, dve.tensor_copy)
                if small:
                    dve.wait_ge(sm_turned, 1)
                    for j, (_, dst) in enumerate(small):
                        dve.tensor_copy(dst, pss[:, j * KC * E:(j + 1) * KC * E].rearrange("p (k e) -> p k e", k=KC))

            @block.scalar
            def _(act):
                copier(1, out_act)(act, lambda o, i: act.activation(o, i, ACT.Copy))


def tile(ap, t):
    return ap[:, ds(t, 1), :].rearrange("p a c -> p (a c)")


class Norm:

    def __init__(self, s, k):
        self.k, self.std = k, s.sb("std", [P, NT])
        self.merged, self.rooted, self.inverted = s.sem("merged"), s.sem("rooted_var"), s.sem("inverted_std")

    def vector(self, dve):
        k = self.k
        for t in range(NT):
            dve.bn_aggr(k.mv[:, t, :], k.st6[:, t, :]).then_inc(self.merged, 1)
        dve.wait_ge(self.merged, NT)
        dve.tensor_scalar(self.std[:, :], k.mv[:, :, 1], LN_EPS, None, ALU.add).then_inc(self.merged, 1)
        dve.wait_ge(self.rooted, 1)
        dve.reciprocal(k.rstd[:, :], self.std[:, :]).then_inc(self.inverted, 1)
        dve.wait_ge(self.inverted, 1)

    def scalar(self, act):
        act.wait_ge(self.merged, NT + 1)
        act.activation(self.std[:, :], self.std[:, :], ACT.Sqrt).then_inc(self.rooted, 1)

    def apply(self, dve, out, x, t):
        return dve.tensor_scalar(out, tile(x, t), self.k.mv[:, ds(t, 1), 0], self.k.rstd[:, ds(t, 1)],
                                 ALU.subtract, ALU.mult)


def load_x(nc, k, x, bproj):
    G = 4
    with Stage(nc, "ldx") as s:
        in_ = s.sems("in", NT // G)
        b_in = s.sem("bin")
        with nc.Block() as block:

            @block.sync
            def _(sp):
                xd = x.rearrange("b (t p) c -> p (b t) c", p=P)
                for g in range(NT // G):
                    sp.dma_start(k.x[:, g * G:(g + 1) * G, :], xd[:, g * G:(g + 1) * G, :]).then_inc(in_[g], 16)
                sp.dma_start(k.bproj[:, :], bproj.partition_broadcast(P)).then_inc(b_in, 16)
                sp.wait_ge(b_in, 16)

            @block.vector
            def _(dve):
                for g in range(NT // G):
                    dve.wait_ge(in_[g], 16)
                    for t in range(g * G, (g + 1) * G):
                        dve.bn_stats(k.st6[:, t, :], k.x[:, t, :])


def linear_attention_in(nc, k):
    CH = BANK
    TC = CH // P
    NCH = T // CH
    SCH = NCH // NB
    with Stage(nc, "lai") as s:
        XR = 4
        xn = s.sb("xn", [P, XR, TC, C + 1])
        xnT = s.sb("xnT", [P, 2, KC, CH])
        low = s.sb("low", [P, 4, CH])
        phik = s.sb("phik", [P, 2, TC, C])
        kx = s.sb("kx", [P, NB, KC, C + 1])
        kxT = s.sb("kxT", [P, KC, NB * KC, P])
        psT = s.ps("psT", [P, KC, CH])
        psQ = s.ps("psQ", [P, KC, CH])
        psK = s.ps("psK", [P, 2, 2 * C])
        psG = s.ps("psG", [P, KC, BANK])
        norm = Norm(s, k)
        (start, normed, x_turned, x_out, projected, clipped, raised, phi_ready, kx_added, kx_saved, kx_turned,
         kx_out, kv_ready) = (
            s.sem(v) for v in ("start", "normed", "xturned", "xout", "projected", "clipped", "raised", "phi", "kxadded",
                               "kxsaved", "kxturned", "kxout", "kvready"))

        def unit(u):
            return psQ[:, u, :] if u < 2 else psK[:, u - 2, :]

        with nc.Block() as block:

            @block.gpsimd
            def _(pool):
                pool.memset(xn[:, :, :, C:C + 1], 1.0).then_inc(start, 1)

            @block.vector
            def _(dve):
                norm.vector(dve)

                def normalise(t):
                    c = t // TC
                    if c >= XR:
                        dve.wait_ge(kx_added, c - XR + 1)
                    norm.apply(dve, xn[:, c % XR, t % TC, 0:C], k.x, t).then_inc(normed, 1)

                def clip(n):
                    c, u = n // 4, n % 4
                    dve.wait_ge(projected, n + 1)
                    dve.tensor_scalar(low[:, u, :], unit(u), 0.0, None, ALU.min).then_inc(clipped, 1)

                def phi(n):
                    c, u = n // 4, n % 4
                    dve.wait_ge(raised, n + 1)
                    if u < 2:
                        out = k.qT[:, u, c * CH:(c + 1) * CH]
                    else:
                        if c >= 2:
                            dve.wait_ge(kx_added, c - 1)
                        out = phik[:, c % 2, (u - 2) * 2:(u - 1) * 2, :].rearrange("p t c -> p (t c)")
                    dve.scalar_tensor_tensor(out, unit(u), 0.0, low[:, u, :], ALU.max, ALU.add).then_inc(phi_ready, 1)

                def save(b):
                    dve.wait_ge(kx_added, (b + 1) * SCH)
                    dve.tensor_copy(kx[:, b, :, :], psG[:, :, 0:C + 1]).then_inc(kx_saved, 1)
                    dve.wait_ge(kx_saved, b + 1)
                    for kk in range(KC):
                        dve.tensor_scalar(k.kvd[:, b, kk, P:P + H // KC],
                                          k.blockdiag[:, :].rearrange("p (h d) -> p h d", d=D)[:, :, 0],
                                          kx[:, b, kk, C:C + 1], None, ALU.mult)

                for t in range(2 * TC):
                    normalise(t)
                for c in range(NCH):
                    for u in range(4):
                        n = c * 4 + u
                        if n:
                            phi(n - 1)
                        clip(n)
                        if c + 2 < NCH:
                            normalise((c + 2) * TC + u)
                    if c == SCH + 1:
                        save(0)
                phi(NCH * 4 - 1)
                save(1)
                dve.wait_ge(kv_ready, 1)
                dve.tensor_tensor(k.kvd[:, :, :, 0:P].rearrange("p b k c -> p (b k) c"),
                                  psQ[:, 0, :].rearrange("p (n c) -> p n c", c=P),
                                  k.blockdiag[:, :].unsqueeze(1).to_broadcast([P, NB * KC, P]), ALU.mult)

            @block.scalar
            def _(act):
                norm.scalar(act)
                for c in range(NCH + 1):
                    if c < NCH:
                        for kk in range(KC):
                            act.wait_ge(x_turned, c * 2 + kk + 1)
                            if c >= 2:
                                act.wait_ge(projected, (c - 1) * 4)
                            act.activation(xnT[:, c % 2, kk, :], psT[:, kk, :], ACT.Copy).then_inc(x_out, 1)
                    if c:
                        for u in range(4):
                            act.wait_ge(clipped, (c - 1) * 4 + u + 1)
                            act.activation(low[:, u, :], low[:, u, :], ACT.Exp).then_inc(raised, 1)
                for cc in range(KC):
                    act.wait_ge(kx_turned, 1)
                    act.activation(kxT[:, cc, :, :].rearrange("p n c -> p (n c)"), psT[:, cc, :],
                                   ACT.Copy).then_inc(kx_out, 1)

            @block.tensor
            def _(pe):
                pe.wait_ge(start, 1)

                def turn(c):
                    pe.wait_ge(normed, (c + 1) * TC)
                    for kk in range(KC):
                        if c:
                            pe.wait_ge(x_out, (c - 1) * 2 + kk + 1)
                        for q in range(TC):
                            mm = pe.transpose(psT[:, kk, q * P:(q + 1) * P], xn[:, c % XR, q, kk * P:(kk + 1) * P],
                                              k.ident[:, :])
                        mm.then_inc(x_turned, 1)

                def project(c):
                    pe.wait_ge(x_out, c * 2 + 2)
                    for u in range(4):
                        if c:
                            pe.wait_ge(phi_ready, (c - 1) * 4 + u + 1)
                        if u < 2:
                            for kk in range(KC):
                                mm = pe.matmul(psQ[:, u, :], k.wqkv[:, kk, u * P:(u + 1) * P], xnT[:, c % 2, kk, :],
                                               start=(kk == 0), stop=(kk == KC - 1))
                        else:
                            for q in range(2):
                                r = (u - 2) * 2 + q
                                for kk in range(KC):
                                    mm = pe.matmul(psK[:, u - 2, q * C:(q + 1) * C],
                                                   xnT[:, c % 2, kk, r * P:(r + 1) * P], k.wqkv[:, kk, C:2 * C],
                                                   start=(kk == 0), stop=(kk == KC - 1))
                        mm.then_inc(projected, 1)

                def add_kx(c):
                    pe.wait_ge(phi_ready, (c + 1) * 4)
                    if c == SCH:
                        pe.wait_ge(kx_saved, 1)
                    for q in range(TC):
                        for kk in range(KC):
                            mm = pe.matmul(psG[:, kk, 0:C + 1], phik[:, c % 2, q, kk * P:(kk + 1) * P],
                                           xn[:, c % XR, q, :], start=(c % SCH == 0 and q == 0),
                                           stop=(c % SCH == SCH - 1 and q == TC - 1))
                    mm.then_inc(kx_added, 1)

                for c in range(NCH + 2):
                    if c < NCH:
                        turn(c)
                    if 0 <= c - 1 < NCH:
                        project(c - 1)
                    if c - 2 >= 0:
                        add_kx(c - 2)
                pe.wait_ge(kx_saved, 2)
                for cc in range(KC):
                    for n in range(NB * KC):
                        mm = pe.transpose(psT[:, cc, n * P:(n + 1) * P],
                                          kx[:, n // KC, n % KC, cc * P:(cc + 1) * P], k.ident[:, :])
                mm.then_inc(kx_turned, 1)
                pe.wait_ge(kx_out, KC)
                for n in range(NB * KC):
                    kk = n % KC
                    for cc in range(KC):
                        mm = pe.matmul(psQ[:, 0, n * P:(n + 1) * P], kxT[:, cc, n, :],
                                       k.wqkv[:, cc, 2 * C + kk * P:2 * C + (kk + 1) * P],
                                       start=(cc == 0), stop=(cc == KC - 1))
                mm.then_inc(kv_ready, 1)


def linear_attention_out(nc, k):
    NPR = NT // 2
    HH = H // KC
    with Stage(nc, "lao") as s:
        den = s.sb("den", [P, 2, 2, KC, HH])
        inv = s.sb("inv", [P, 2, 2, KC, HH])
        o = s.sb("o", [P, 2, 2, C])
        oT = s.sb("oT", [P, 2, KC, 2, P])
        psN = s.ps("psN", [P, 2, 2, BANK])
        psT = s.ps("psT", [P, 2, BANK])
        psY = s.ps("psY", [P, 2, 2 * C])
        (biased, multiplied, guarded, inverted, divided, o_turned, o_out, y_ready, y_added) = (
            s.sem(v) for v in ("biased", "mult", "guarded", "inverted", "div", "oturned", "oout", "y", "yadd"))

        def sums(j):
            v = psN[:, j, :, 0:KC * (P + HH)].rearrange("p t (k c) -> p t k c", k=KC)
            return v[:, :, :, 0:P].rearrange("p t k (h d) -> p t k h d", d=D), v[:, :, :, P:P + HH]

        with nc.Block() as block:

            @block.gpsimd
            def _(pool):
                for n in range(NPR):
                    x = k.x[:, 2 * n:2 * n + 2, :]
                    pool.tensor_tensor(x, x, k.bproj[:, :].unsqueeze(1).to_broadcast([P, 2, C]),
                                       ALU.add).then_inc(biased, 1)

            @block.tensor
            def _(pe):
                for st in range(NPR + 2):
                    if st < NPR:
                        n = st
                        if n >= 2:
                            pe.wait_ge(divided, (n - 1) * 2)
                        for q in range(2):
                            t = 2 * n + q
                            for kk in range(KC):
                                mm = pe.matmul(psN[:, n % 2, q, kk * (P + HH):(kk + 1) * (P + HH)],
                                               k.qT[:, kk, t * P:(t + 1) * P], k.kvd[:, t // TB, kk, :],
                                               start=True, stop=True)
                        mm.then_inc(multiplied, 1)
                    if 0 <= st - 1 < NPR:
                        n = st - 1
                        pe.wait_ge(divided, n * 2 + 2)
                        if n >= 2:
                            pe.wait_ge(o_out, n - 1)
                        for kk in range(KC):
                            for q in range(2):
                                mm = pe.transpose(psT[:, n % 2, (kk * 2 + q) * P:(kk * 2 + q + 1) * P],
                                                  o[:, n % 2, q, kk * P:(kk + 1) * P], k.ident[:, :])
                        mm.then_inc(o_turned, 1)
                    if st >= 2:
                        n = st - 2
                        pe.wait_ge(o_out, n + 1)
                        if n >= 2:
                            pe.wait_ge(y_added, n - 1)
                        for q in range(2):
                            for kk in range(KC):
                                mm = pe.matmul(psY[:, n % 2, q * C:(q + 1) * C], oT[:, n % 2, kk, q, :],
                                               k.wproj[:, kk, :], start=(kk == 0), stop=(kk == KC - 1))
                        mm.then_inc(y_ready, 1)

            @block.scalar
            def _(act):
                for n in range(NPR):
                    act.wait_ge(o_turned, n + 1)
                    if n >= 2:
                        act.wait_ge(y_ready, n - 1)
                    act.activation(oT[:, n % 2, :, :, :].rearrange("p k q c -> p (k q c)"), psT[:, n % 2, :],
                                   ACT.Copy).then_inc(o_out, 1)

            @block.vector
            def _(dve):
                for st in range(NPR + 3):
                    if st < NPR:
                        n = st
                        num, d = sums(n % 2)
                        dve.wait_ge(multiplied, n + 1)
                        dve.tensor_scalar(den[:, n % 2, :, :, :], d, EPS, None, ALU.add).then_inc(guarded, 1)
                        dve.wait_ge(guarded, n + 1)
                        dve.reciprocal(inv[:, n % 2, :, :, :], den[:, n % 2, :, :, :]).then_inc(inverted, 1)
                        dve.wait_ge(inverted, n + 1)
                        if n >= 2:
                            dve.wait_ge(o_turned, n - 1)
                        for q in range(2):
                            dve.tensor_tensor(o[:, n % 2, q, :].rearrange("p (k h d) -> p k h d", k=KC, d=D),
                                              num[:, q, :, :, :],
                                              inv[:, n % 2, q, :, :].unsqueeze(3).to_broadcast([P, KC, HH, D]),
                                              ALU.mult).then_inc(divided, 1)
                    if 0 <= st - 2 < NPR:
                        n = st - 2
                        dve.wait_ge(biased, n + 1)
                        dve.wait_ge(y_ready, n + 1)
                        dve.tensor_tensor(k.x[:, 2 * n:2 * n + 2, :],
                                          psY[:, n % 2, :].rearrange("p (t c) -> p t c", c=C),
                                          k.x[:, 2 * n:2 * n + 2, :], ALU.add).then_inc(y_added, 1)
                    if st >= 3:
                        n = st - 3
                        dve.wait_ge(y_added, n + 1)
                        for t in range(2 * n, 2 * n + 2):
                            dve.bn_stats(k.st6[:, t, :], k.x[:, t, :])


def route(nc, k, name, layer, gateT, x):
    with Stage(nc, name) as s:
        R = 4
        xn = s.sb("xn", [P, R, C])
        xnT = s.sb("xnT", [P, 2, KC, P])
        sq = s.sb("sq", [P, C])
        cT2 = s.sb("cT2", [P, KC, E])
        xsq = s.sb("xsq", [P, NT])
        csq = s.sb("csq", [P, E])
        psT = s.ps("psT", [P, 2, BANK])
        psL = s.ps("psL", [P, BANK])
        psC = s.ps("psC", [P, BANK])
        psPre = s.ps("psPre", [P, BANK])
        psTot = s.ps("psTot", [P, BANK])
        psTab = s.ps("psTab", [P, BANK])
        normed, turned, x_out, logits, squared, csq_ready = (
            s.sem(v) for v in ("normed", "turned", "xout", "logits", "squared", "csq"))
        stored = s.sems("stored", R)
        norm = Norm(s, k)
        vals, work, mask = s.sb("vals", [P, NT, E]), s.sb("work", [P, NT, E]), s.sb("mask", [P, NT, E])
        one1, one2, maskb = s.sb("one1", [P, NT, E]), s.sb("one2", [P, NT, E]), s.sb("maskb", [P, NT * E], BF16)
        tot, incl, pos = s.sb("tot", [P, NT, E]), s.sb("incl", [P, NT, E]), s.sb("pos", [P, NT, E])
        desc = s.sb("desc", [P, E])
        m1, m2, c1, row, row2 = (s.sb(v, [P, NT]) for v in ("m1", "m2", "c1", "row", "row2"))
        p12 = s.sb("p12", [P, NT, 2])
        w12 = s.sb("w12", [P, NT, 2])
        hi, lo, dstv = (s.sb(v, [P, NT, 2]) for v in ("hi", "lo", "dstv"))
        pi, pj = s.sb("pi", [P, NT * 2], I32), s.sb("pj", [P, NT * 2], I32)
        ni = s.sb("ni", [P, E], I32)
        nf, ends, first = s.sb("nf", [P, E]), s.sb("ends", [P, E]), s.sb("first", [P, E])
        zeroE, zeroT = s.sb("zeroE", [P, E]), s.sb("zeroT", [P, NT])
        te = s.sb("te", [P, NTILE, E])
        tes = s.sb("tes", [P, NTILE])
        RH = 4
        oneLo = s.sb("oneLo", [P, RH, P])
        oneHi = s.sb("oneHi", [P, RH, 2, NTILE])
        raw, pad, big = s.sb("raw", [P, NTILE]), s.sb("pad", [P, NTILE]), s.sb("big", [P, NTILE])
        chain, soft, softed, sums_asked, sums_ready, hot, tab_added, tab_done = (
            s.sem(v) for v in ("chain", "soft", "softed", "asked", "sums", "hot", "tabadd", "tabdone"))
        xn_d = k.xn_d.rearrange("(t p) c -> t p c", p=P)

        def bt(ap):
            return ap.unsqueeze(2).to_broadcast([P, NT, E])

        def be(ap):
            return ap.unsqueeze(1).to_broadcast([P, NT, E])

        with nc.Block() as block:

            @block.sync
            def _(sp):
                with sp.Fori(0, NT // R) as i:
                    for j in range(R):
                        sp.wait_ge(normed, i * R + j + 1)
                        sp.dma_start(xn_d[ds(i * R + j, 1), :, :].rearrange("a p c -> (a p) c"),
                                     xn[:, j, :]).then_inc(stored[j], 16)
                for j in range(R):
                    sp.wait_ge(stored[j], 16 * (NT // R))

            @block.scalar
            def _(act):
                norm.scalar(act)
                with act.Fori(0, NT // 4) as i:
                    for jj in range(4):
                        t, j = i * 4 + jj, jj % 2
                        act.wait_ge(turned, t + 1 + 2)
                        act.wait_ge(logits, t + 1)
                        act.activation(xnT[:, j, :, :], psT[:, j, 0:C].rearrange("p (k c) -> p k c", k=KC),
                                       ACT.Copy).then_inc(x_out, 1)
                        if layer == 1:
                            act.activation(sq[:, :], xn[:, jj, :], ACT.Square,
                                           accum_out=xsq[:, ds(t, 1)]).then_inc(squared, 1)
                            act.wait_ge(squared, t + 1)
                if layer == 0:
                    act.wait_ge(soft, 1)
                    act.activation(work[:, :, :], work[:, :, :], ACT.Exp).then_inc(softed, 1)
                else:
                    act.wait_ge(soft, 1)
                    act.activation(p12[:, :, :], p12[:, :, :], ACT.Sqrt).then_inc(softed, 1)
                    act.wait_ge(soft, 2)
                    act.activation(m2[:, :], m2[:, :], ACT.Exp).then_inc(softed, 1)

            @block.tensor
            def _(pe):
                pe.sem_inc(turned, 2)
                pe.sem_inc(logits, 2)

                def turn(t, jj):
                    pe.wait_ge(normed, t + 1)
                    pe.wait_ge(x_out, t + 1)
                    for kk in range(KC):
                        mm = pe.transpose(psT[:, jj % 2, kk * P:(kk + 1) * P], xn[:, jj, kk * P:(kk + 1) * P],
                                          k.ident[:, :])
                    mm.then_inc(turned, 1)

                def score(t, jj):
                    pe.wait_ge(x_out, t + 3)
                    for kk in range(KC):
                        mm = pe.matmul(psL[:, ds(t * E, E)], xnT[:, jj % 2, kk, :], gateT[:, kk, :],
                                       start=(kk == 0), stop=(kk == KC - 1))
                    mm.then_inc(logits, 1)

                turn(0, 0)
                with pe.Fori(0, NT // 4 - 1) as i:
                    for jj in range(4):
                        turn(i * 4 + jj + 1, (jj + 1) % 4)
                        score(i * 4 + jj, jj)
                for jj in range(4):
                    if jj < 3:
                        turn(NT - 4 + jj + 1, jj + 1)
                    score(NT - 4 + jj, jj)
                if layer == 1:
                    pe.wait_ge(csq_ready, 1)
                    for kk in range(KC):
                        mm = pe.matmul(psC[:, 0:E], k.ones[:, :], cT2[:, kk, :], start=(kk == 0), stop=(kk == KC - 1))
                    mm.then_inc(csq_ready, 1)
                pe.wait_ge(sums_asked, 1)
                pe.matmul(psPre[:, 0:NT * E], k.upperb[:, :], maskb[:, :], start=True, stop=True)
                pe.matmul(psTot[:, 0:NT * E], k.onesb[:, :], maskb[:, :], start=True, stop=True).then_inc(sums_ready, 1)
                for n in range(2 * NT):
                    pe.wait_ge(hot, n + 1)
                    pe.matmul(psTab[:, 0:2 * NTILE], oneLo[:, n % RH, :],
                              oneHi[:, n % RH, :, :].rearrange("p a c -> p (a c)"),
                              start=(n == 0), stop=(n == 2 * NT - 1)).then_inc(tab_added, 1)

            @block.vector
            def _(dve):
                dve.sem_inc(x_out, 2)
                norm.vector(dve)
                if layer == 1:
                    dve.wait_ge(k.x_in, 16)
                ser = Serial(dve, chain)
                with dve.Fori(0, NT // R) as i:
                    for j in range(R):
                        t = i * R + j
                        dve.wait_ge(stored[j], i * 16)
                        dve.wait_ge(turned, t)
                        if layer == 1:
                            dve.wait_ge(squared, t)
                        norm.apply(dve, xn[:, j, :], x, t).then_inc(normed, 1)
                ser(dve.memset(zeroE[:, :], 0.0))
                ser(dve.memset(zeroT[:, :], 0.0))
                ser(dve.tensor_scalar(desc[:, :], k.lane[:, 0:E], -1.0, float(E), ALU.mult, ALU.add))
                if layer == 1:
                    dve.tensor_tensor(cT2[:, :, :], gateT[:, :, :], gateT[:, :, :], ALU.mult).then_inc(csq_ready, 1)
                    dve.wait_ge(csq_ready, 2)
                    ser(dve.tensor_copy(csq[:, :], psC[:, 0:E]))
                dve.wait_ge(logits, NT + 2)
                L = psL[:, 0:NT * E].rearrange("p (t e) -> p t e", e=E)
                if layer == 0:
                    ser(dve.tensor_reduce(m1[:, :], L, AX.X, ALU.max))
                    ser(dve.tensor_tensor(work[:, :, :], L, bt(m1[:, :]), ALU.subtract))
                    dve.sem_inc(soft, 1)
                    dve.wait_ge(softed, 1)
                    ser(dve.tensor_reduce(m1[:, :], work[:, :, :], AX.X, ALU.add))
                    ser(dve.reciprocal(m2[:, :], m1[:, :]))
                    ser(dve.tensor_tensor(vals[:, :, :], work[:, :, :], bt(m2[:, :]), ALU.mult))
                else:
                    dve.wait_ge(squared, NT)
                    ser(dve.tensor_scalar(work[:, :, :], L, -2.0, None, ALU.mult))
                    ser(dve.tensor_tensor(mask[:, :, :], be(csq[:, :]), bt(xsq[:, :]), ALU.add))
                    ser(dve.tensor_tensor(vals[:, :, :], work[:, :, :], mask[:, :, :], ALU.add))
                    ser(dve.tensor_scalar(vals[:, :, :], vals[:, :, :], 1e-12, None, ALU.max))

                def largest(v, val, onehot):
                    ser(dve.tensor_reduce(val, v, AX.X, ALU.max))
                    ser(dve.tensor_tensor(mask[:, :, :], v, bt(val), ALU.is_equal))
                    ser(dve.tensor_tensor(mask[:, :, :], mask[:, :, :], be(desc[:, :]), ALU.mult))
                    ser(dve.tensor_reduce(c1[:, :], mask[:, :, :], AX.X, ALU.max))
                    ser(dve.tensor_tensor(onehot, bt(c1[:, :]), be(desc[:, :]), ALU.is_equal))

                largest(vals[:, :, :], p12[:, :, 0], one1[:, :, :])
                ser(dve.tensor_scalar(mask[:, :, :], one1[:, :, :], -1.0, 1.0, ALU.mult, ALU.add))
                ser(dve.tensor_tensor(work[:, :, :], vals[:, :, :], mask[:, :, :], ALU.mult))
                ser(dve.tensor_tensor(work[:, :, :], work[:, :, :], one1[:, :, :], ALU.subtract))
                largest(work[:, :, :], p12[:, :, 1], one2[:, :, :])
                ser(dve.tensor_tensor(maskb[:, :].rearrange("p (t e) -> p t e", e=E), one1[:, :, :], one2[:, :, :],
                                      ALU.add))
                dve.sem_inc(sums_asked, 1)
                if layer == 0:
                    ser(dve.tensor_tensor(m1[:, :], p12[:, :, 0], p12[:, :, 1], ALU.add))
                    ser(dve.reciprocal(m2[:, :], m1[:, :]))
                    ser(dve.tensor_tensor(w12[:, :, :], p12[:, :, :], m2[:, :].unsqueeze(2).to_broadcast([P, NT, 2]),
                                          ALU.mult))
                else:
                    dve.sem_inc(soft, 1)
                    dve.wait_ge(softed, 1)
                    ser(dve.tensor_tensor(m2[:, :], p12[:, :, 1], p12[:, :, 0], ALU.subtract))
                    dve.sem_inc(soft, 1)
                    dve.wait_ge(softed, 2)
                    ser(dve.tensor_scalar(m1[:, :], m2[:, :], 1.0, None, ALU.add))
                    ser(dve.reciprocal(w12[:, :, 0], m1[:, :]))
                    ser(dve.tensor_tensor(w12[:, :, 1], w12[:, :, 0], m2[:, :], ALU.mult))
                dve.wait_ge(sums_ready, 1)
                ser(dve.tensor_copy(tot[:, :, :], psTot[:, 0:NT * E].rearrange("p (t e) -> p t e", e=E)))
                for e in range(E):
                    ins = dve.tensor_tensor_scan(incl[:, :, e], tot[:, :, e], zeroT[:, :], 0.0, ALU.add, ALU.add)
                ser(ins)
                ser(dve.tensor_scalar(nf[:, :], incl[:, NT - 1, :], float(P - 1), None, ALU.add))
                ser(dve.tensor_copy(ni[:, :], nf[:, :]))
                ser(dve.tensor_scalar(ni[:, :], ni[:, :], 7, None, ALU.logical_shift_right))
                ser(dve.tensor_copy(nf[:, :], ni[:, :]))
                ser(dve.tensor_tensor_scan(ends[:, :], nf[:, :], zeroE[:, :], 0.0, ALU.add, ALU.add))
                ser(dve.tensor_tensor(first[:, :], ends[:, :], nf[:, :], ALU.subtract))
                ser(dve.tensor_scalar(first[:, :], first[:, :], float(P), None, ALU.mult))
                ser(dve.tensor_tensor(pos[:, :, :], incl[:, :, :], tot[:, :, :], ALU.subtract))
                ser(dve.tensor_tensor(pos[:, :, :], pos[:, :, :], be(first[:, :]), ALU.add))
                ser(dve.tensor_tensor(pos[:, :, :], psPre[:, 0:NT * E].rearrange("p (t e) -> p t e", e=E),
                                      pos[:, :, :], ALU.add))
                for j, one in enumerate((one1, one2)):
                    ser(dve.tensor_tensor(work[:, :, :], one[:, :, :], pos[:, :, :], ALU.mult))
                    ser(dve.tensor_reduce(dstv[:, :, j], work[:, :, :], AX.X, ALU.add))
                flat = dstv[:, :, :].rearrange("p t j -> p (t j)")
                ser(dve.tensor_copy(pi[:, :], flat))
                ser(dve.tensor_scalar(pj[:, :], pi[:, :], 7, None, ALU.logical_shift_right))
                ser(dve.tensor_copy(hi[:, :, :].rearrange("p t j -> p (t j)"), pj[:, :]))
                ser(dve.tensor_scalar(pj[:, :], pi[:, :], P - 1, None, ALU.bitwise_and))
                ser(dve.tensor_copy(lo[:, :, :].rearrange("p t j -> p (t j)"), pj[:, :]))
                ser(dve.tensor_scalar(row[:, :], k.tilebase[:, :], k.lane1[:, 0:1], 1.0, ALU.add, ALU.add))
                ser(dve.tensor_copy(dstv[:, :, 0], row[:, :]))
                ser(dve.tensor_scalar(dstv[:, :, 1], row[:, :], float(T), None, ALU.add))
                for n in range(2 * NT):
                    t, j = n // 2, n % 2
                    if n >= RH:
                        dve.wait_ge(tab_added, n - RH + 1)
                    dve.tensor_scalar(oneLo[:, n % RH, :], k.lane[:, :], lo[:, t, j:j + 1], None, ALU.is_equal)
                    dve.tensor_scalar(oneHi[:, n % RH, 0, :], k.lane[:, 0:NTILE], hi[:, t, j:j + 1],
                                      dstv[:, t, j:j + 1], ALU.is_equal, ALU.mult)
                    dve.tensor_scalar(oneHi[:, n % RH, 1, :], k.lane[:, 0:NTILE], hi[:, t, j:j + 1],
                                      w12[:, t, j:j + 1], ALU.is_equal, ALU.mult).then_inc(hot, 1)
                ser(dve.tensor_tensor(te[:, :, :], k.lane[:, 0:NTILE].unsqueeze(2).to_broadcast([P, NTILE, E]),
                                      ends[:, :].unsqueeze(1).to_broadcast([P, NTILE, E]), ALU.is_ge))
                ser(dve.tensor_reduce(tes[:, :], te[:, :, :], AX.X, ALU.add))
                ser(dve.tensor_scalar(tes[:, :], tes[:, :], float(E - 1), None, ALU.min))
                ser(dve.tensor_copy(k.tile_expert[:, :], tes[0:1, :]))
                dve.wait_ge(tab_added, 2 * NT)
                ser(dve.tensor_copy(k.wgt[:, :], psTab[:, NTILE:2 * NTILE]))
                ser(dve.tensor_copy(raw[:, :], psTab[:, 0:NTILE]))
                ser(dve.tensor_scalar(pad[:, :], raw[:, :], 0.0, None, ALU.is_equal))
                ser(dve.tensor_scalar(big[:, :], k.odd_rows[:, :], k.lane1[:, 0:1], None, ALU.add))
                ser(dve.tensor_tensor(big[:, :], big[:, :], pad[:, :], ALU.mult))
                ser(dve.tensor_scalar(pad[:, :], pad[:, :], float(2 * T + 1), -1.0, ALU.mult, ALU.add))
                ser(dve.tensor_tensor(raw[:, :], raw[:, :], pad[:, :], ALU.add))
                ser(dve.tensor_tensor(raw[:, :], raw[:, :], big[:, :], ALU.add))
                ser(dve.tensor_copy(k.dst[:, :], raw[:, :]))
                ser(dve.tensor_scalar(k.tok[:, :], k.dst[:, :], T - 1, None, ALU.bitwise_and))


def slot_transfers(pool, k, idx, odx, xg, y, got, put, x_turned, y_done, indexed, passed):
    LAG = GR + 2
    for st in steps(pool, NTILE, 8, LAG):
        if st.on(0):
            t, g = st.tile(0), st.slot(0, GR)
            st.again(pool, got[g], st.lap(0, GR) * 16)
            st.again(pool, x_turned, t - GR + 1)
            pool.tensor_copy(idx[:, g, :], k.tok[:, ds(t, 1)]).then_inc(indexed, 1)
        if st.on(LAG):
            t, j = st.tile(LAG), st.slot(LAG, 2)
            st.again(pool, put[j], st.lap(LAG, 2) * 16)
            pool.tensor_copy(odx[:, j, :], k.dst[:, ds(t, 1)]).then_inc(indexed, 1)
        if isinstance(st.i, int):
            count = min(st.tile() + 1, NTILE) + max(st.tile() - LAG + 1, 0)
        else:
            count = st.i * 16 + 2 * st.m + 2 - LAG
        if st.on(0):
            pool.wait_ge(indexed, count)
            pool.sem_inc(passed, 1)
            pool.indirect_dma_start(xg[:, g, :], None, k.xn_d,
                                    bass.IndirectOffsetOnAxis(idx[:, g, :], 0)).then_inc(got[g], 16)
        if st.on(LAG):
            pool.wait_ge(indexed, count)
            pool.wait_ge(y_done, t + 1)
            pool.sem_inc(passed, 1)
            pool.indirect_dma_start(k.y_d, bass.IndirectOffsetOnAxis(odx[:, j, :], 0), y[:, j, :],
                                    None).then_inc(put[j], 16)
    for j in range(2):
        pool.wait_ge(put[j], 16 * (NTILE // 2))


def experts0(nc, k):
    with Stage(nc, "ex0") as s:
        idx, odx = s.sb("idx", [P, GR, 1], U32), s.sb("odx", [P, 2, 1], U32)
        xg = s.sb("xg", [P, GR, C])
        xT = s.sb("xT", [P, 2, KC, P])
        sg = s.sb("sg", [P, 2, F0])
        h = s.sb("h", [P, 2, F0])
        hT = s.sb("hT", [P, 2, KC, P])
        y = s.sb("y", [P, 2, C])
        psX = s.ps("psX", [P, 2, BANK])
        psH = s.ps("psH", [P, 2, BANK])
        psG = s.ps("psG", [P, 2, BANK])
        psY = s.ps("psY", [P, 2, BANK])
        (x_turned, x_out, h_ready, gated, h_done, h_turned, h_out, y_ready, y_done) = (
            s.sem(v) for v in ("xturned", "xout", "hready", "gated", "hdone", "hturned", "hout", "yready",
                               "ydone"))
        got, put = s.sems("got", GR), s.sems("put", 2)
        indexed, passed = s.sem("indexed"), s.sem("passed")
        with nc.Block() as block:

            @block.gpsimd
            def _(pool):
                slot_transfers(pool, k, idx, odx, xg, y, got, put, x_turned, y_done, indexed, passed)

            @block.tensor
            def _(pe):
                for st in steps(pe, NTILE, 8, 3):
                    if st.on(0):
                        t, g, j = st.tile(0), st.slot(0, GR), st.slot(0, 2)
                        pe.wait_ge(got[g], st.lap(0, GR) * 16 + 16)
                        st.again(pe, x_out, t - 1)
                        for kk in range(KC):
                            mm = pe.transpose(psX[:, j, kk * P:(kk + 1) * P], xg[:, g, kk * P:(kk + 1) * P],
                                              k.ident[:, :])
                        mm.then_inc(x_turned, 1)
                    if st.on(1):
                        t, j = st.tile(1), st.slot(1, 2)
                        e = pe.value_load(k.tile_expert[0:1, ds(t, 1)], min_val=0, max_val=E - 1)
                        pe.wait_ge(x_out, t + 1)
                        st.again(pe, h_done, t - 1)
                        for kk in range(KC):
                            mm = pe.matmul(psH[:, j, :], xT[:, j, kk, :],
                                           k.w13[:, ds(e, 1), kk, :].rearrange("p a c -> p (a c)"),
                                           start=(kk == 0), stop=(kk == KC - 1))
                        mm.then_inc(h_ready, 1)
                    if st.on(2):
                        t, j = st.tile(2), st.slot(2, 2)
                        pe.wait_ge(h_done, t + 1)
                        st.again(pe, h_out, t - 1)
                        for kk in range(KC):
                            mm = pe.transpose(psG[:, j, kk * P:(kk + 1) * P], h[:, j, kk * P:(kk + 1) * P],
                                              k.ident[:, :])
                        mm.then_inc(h_turned, 1)
                    if st.on(3):
                        t, j = st.tile(3), st.slot(3, 2)
                        e = pe.value_load(k.tile_expert[0:1, ds(t, 1)], min_val=0, max_val=E - 1)
                        pe.wait_ge(h_out, t + 1)
                        st.again(pe, y_done, t - 1)
                        for kk in range(KC):
                            mm = pe.matmul(psY[:, j, 0:C], hT[:, j, kk, :],
                                           k.w2[:, ds(e, 1), kk, :].rearrange("p a c -> p (a c)"),
                                           start=(kk == 0), stop=(kk == KC - 1))
                        mm.then_inc(y_ready, 1)

            @block.scalar
            def _(act):
                for st in steps(act, NTILE, 8, 2):
                    if st.on(0):
                        t, j = st.tile(0), st.slot(0, 2)
                        act.wait_ge(x_turned, t + 1)
                        st.again(act, h_ready, t - 1)
                        act.activation(xT[:, j, :, :], psX[:, j, 0:C].rearrange("p (k c) -> p k c", k=KC),
                                       ACT.Copy).then_inc(x_out, 1)
                    if st.on(2):
                        t, j = st.tile(2), st.slot(2, 2)
                        act.wait_ge(h_turned, t + 1)
                        st.again(act, y_ready, t - 1)
                        act.activation(hT[:, j, :, :], psG[:, j, 0:C].rearrange("p (k c) -> p k c", k=KC),
                                       ACT.Copy).then_inc(h_out, 1)
                    if st.on(1):
                        t, j = st.tile(1), st.slot(1, 2)
                        act.wait_ge(h_ready, t + 1)
                        st.again(act, h_done, t - 1)
                        act.activation(sg[:, j, :], psH[:, j, 0:F0], ACT.Silu).then_inc(gated, 1)

            @block.vector
            def _(dve):
                for st in steps(dve, NTILE, 4, 1):
                    if st.on(0):
                        t, j = st.tile(0), st.slot(0, 2)
                        dve.wait_ge(gated, t + 1)
                        st.again(dve, h_turned, t - 1)
                        dve.tensor_tensor(h[:, j, :], psH[:, j, F0:2 * F0], sg[:, j, :], ALU.mult).then_inc(h_done, 1)
                    if st.on(1):
                        t, j = st.tile(1), st.slot(1, 2)
                        dve.wait_ge(y_ready, t + 1)
                        st.again(dve, put[j], st.lap(1, 2) * 16)
                        dve.tensor_scalar(y[:, j, :], psY[:, j, 0:C], k.wgt[:, ds(t, 1)], None,
                                          ALU.mult).then_inc(y_done, 1)


def combine(nc, k, name, x_out_dram, stats):
    G = 4
    R = 4
    with Stage(nc, name) as s:
        y = s.sb("y", [P, R, 2, G, C])
        got, paired, added, out_sem = s.sems("got", R), s.sem("paired"), s.sem("added"), s.sem("out")
        y0 = k.y_d[0:2 * T, :].rearrange("(n t p) c -> p n t c", p=P, n=2)
        with nc.Block() as block:

            @block.sync
            def _(sp):
                for g in range(NT // G):
                    if g >= R:
                        sp.wait_ge(added, g - R + 1)
                    for n in range(2):
                        sp.dma_start(y[:, g % R, n, :, :], y0[:, n, g * G:(g + 1) * G, :]).then_inc(got[g % R], 16)

            @block.vector
            def _(dve):
                for g in range(NT // G):
                    x = k.x[:, g * G:(g + 1) * G, :]
                    dve.wait_ge(got[g % R], (g // R + 1) * 32)
                    dve.tensor_tensor(y[:, g % R, 0, :, :], y[:, g % R, 0, :, :], y[:, g % R, 1, :, :],
                                      ALU.add).then_inc(paired, 1)
                    dve.wait_ge(paired, g + 1)
                    dve.tensor_tensor(x, x, y[:, g % R, 0, :, :], ALU.add).then_inc(added, 1)
                    if stats:
                        dve.wait_ge(added, g + 1)
                        for t in range(g * G, (g + 1) * G):
                            dve.bn_stats(k.st6[:, t, :], k.x[:, t, :])

            @block.scalar
            def _(act):
                for g in range(NT // G):
                    act.wait_ge(added, g + 1)
                    act.dma_start(x_out_dram[:, g * G:(g + 1) * G, :], k.x[:, g * G:(g + 1) * G, :]).then_inc(out_sem, 16)
                act.wait_ge(out_sem, 16 * (NT // G))


def log_map(nc, k):
    with Stage(nc, "lm") as s:
        sp_ = s.sb("sp", [P, NT, C])
        junk = s.sb("junk", [P, C])
        s2, y0, a, am, b, d, f = (s.sb(v, [P, NT]) for v in ("s2", "y0", "a", "am", "b", "d", "f"))
        normed, clipped, squared, chain, asked, rooted, grouped = (
            s.sem(v) for v in ("normed", "clipped", "squared", "chain", "asked", "rooted", "grouped"))
        G = 4
        norm = Norm(s, k)
        stored = s.sem("stored")
        with nc.Block() as block:

            @block.vector
            def _(dve):
                norm.vector(dve)
                ser = Serial(dve, chain)
                with dve.Fori(0, NT) as t:
                    norm.apply(dve, tile(sp_, t), k.x, t).then_inc(normed, 1)
                    dve.wait_ge(normed, t + 1)
                    dve.tensor_scalar(tile(sp_, t), tile(sp_, t), -8.0, 8.0, ALU.max, ALU.min).then_inc(clipped, 1)
                dve.wait_ge(squared, NT)
                ser(dve.tensor_scalar(y0[:, :], s2[:, :], 1.0, EPS, ALU.add, ALU.add))
                dve.sem_inc(asked, 1)
                dve.wait_ge(rooted, 1)
                ser(dve.tensor_scalar(a[:, :], y0[:, :], 1.0 + EPS, None, ALU.max))
                ser(dve.tensor_scalar(am[:, :], a[:, :], 1.0, None, ALU.subtract))
                ser(dve.scalar_tensor_tensor(b[:, :], a[:, :], 1.0, am[:, :], ALU.add, ALU.mult))
                ser(dve.tensor_tensor(y0[:, :], y0[:, :], a[:, :], ALU.subtract))
                ser(dve.tensor_tensor(d[:, :], y0[:, :], y0[:, :], ALU.mult))
                ser(dve.tensor_tensor(d[:, :], s2[:, :], d[:, :], ALU.subtract))
                ser(dve.tensor_scalar(d[:, :], d[:, :], EPS, None, ALU.max))
                dve.sem_inc(asked, 1)
                dve.wait_ge(rooted, 3)
                ser(dve.tensor_tensor(a[:, :], a[:, :], b[:, :], ALU.add))
                dve.sem_inc(asked, 1)
                dve.wait_ge(rooted, 4)
                ser(dve.tensor_scalar(a[:, :], a[:, :], 1e-3, None, ALU.max))
                ser(dve.tensor_scalar(d[:, :], d[:, :], EPS, None, ALU.add))
                ser(dve.reciprocal(b[:, :], d[:, :]))
                ser(dve.tensor_tensor(f[:, :], a[:, :], b[:, :], ALU.mult))
                for g in range(NT // G):
                    dve.tensor_tensor(sp_[:, g * G:(g + 1) * G, 1:C], sp_[:, g * G:(g + 1) * G, 1:C],
                                      f[:, g * G:(g + 1) * G].unsqueeze(2).to_broadcast([P, G, C - 1]), ALU.mult)
                    dve.tensor_tensor(sp_[:, g * G:(g + 1) * G, 0], y0[:, g * G:(g + 1) * G], f[:, g * G:(g + 1) * G],
                                      ALU.mult).then_inc(grouped, 1)

            @block.scalar
            def _(act):
                norm.scalar(act)
                with act.Fori(0, NT) as t:
                    act.wait_ge(clipped, t + 1)
                    act.activation(junk[:, 1:C], tile(sp_, t)[:, 1:C], ACT.Square,
                                   accum_out=s2[:, ds(t, 1)]).then_inc(squared, 1)
                    act.wait_ge(squared, t + 1)
                act.wait_ge(asked, 1)
                act.activation(y0[:, :], y0[:, :], ACT.Sqrt).then_inc(rooted, 1)
                act.wait_ge(asked, 2)
                act.activation(b[:, :], b[:, :], ACT.Sqrt).then_inc(rooted, 1)
                act.activation(d[:, :], d[:, :], ACT.Sqrt).then_inc(rooted, 1)
                act.wait_ge(asked, 3)
                act.activation(a[:, :], a[:, :], ACT.Ln).then_inc(rooted, 1)

            @block.sync
            def _(sp):
                for g in range(NT // G):
                    sp.wait_ge(grouped, g + 1)
                    sp.dma_start(k.v_t[:, g * G:(g + 1) * G, :], sp_[:, g * G:(g + 1) * G, :]).then_inc(stored, 16)
                sp.wait_ge(stored, 16 * (NT // G))


def stacked_heads(nc, k, b):
    S2 = 6 * D
    HB = H // 2
    R = 4
    with Stage(nc, f"sh{b}") as s:
        v = s.sb("v", [P, R, C])
        vT = s.sb("vT", [P, 2, KC, P])
        qk = s.sb("qk", [P, 2, 2 * H, D])
        sq = s.sb("sq", [P, 2 * H, D])
        root = s.sb("root", [P, 2, 2 * H])
        rest = s.sb("rest", [P, 2, 2 * H, D])
        hm = s.sb("hm", [P, 2, 2 * H, 2, D], BF16)
        stq, stk = s.sb("stq", [P, 2, H, P], BF16), s.sb("stk", [P, 2, H, P], BF16)
        psT = s.ps("psT", [P, BANK])
        psQK = s.ps("psQK", [P, 2, BANK])
        psV = s.ps("psV", [P, BANK])
        psS = s.ps("psS", [P, 4, 2 * BANK], BF16)
        (start, turned, vT_out, qk_ready, v_ready, v_out, clipped, squared, summed, rooted, led, high, left, middle,
         low, stacked, pool_stacked, st_turned, evac_dve, evac_act) = (
            s.sem(n) for n in ("start", "turned", "vTout", "qk", "vr", "vout", "clipped", "squared", "summed", "rooted",
                               "led", "high", "left", "middle", "low", "stacked", "pstacked", "stturned", "evacd",
                               "evaca"))
        got = s.sems("got", R)
        passed = s.sem("passed")

        def section(buf, j, a):
            return buf[:, j, :, a * D:(a + 1) * D]

        def evacuate(eng, copy, st, n, half, sem):
            t, dst = st.tile(4), (k.QT, k.KT)[n]
            eng.wait_ge(st_turned, t * 4 + n * 2 + half + 2)
            copy(dst[:, half * HB:(half + 1) * HB, ds(t * P, P)],
                 psS[:, n * 2 + half, :].rearrange("p (h t) -> p h t", h=HB)).then_inc(sem, 1)

        with nc.Block() as block:

            @block.sync
            def _(sp):
                for st in steps(sp, TB, R, 0):
                    t, j = st.tile(), st.slot(0, R)
                    st.again(sp, turned, t - R + 1)
                    sp.dma_start(v[:, j, :], tile(k.v_t, b * TB + t)).then_inc(got[j], 16)

            @block.gpsimd
            def _(pool):
                pool.memset(stq[:, :, :, S2:P], 0.0).then_inc(start, 1)
                pool.memset(stk[:, :, :, S2 + 3:P], 0.0).then_inc(start, 1)
                pool.memset(stk[:, :, :, S2:S2 + 3], 1.0).then_inc(start, 1)
                for st in steps(pool, TB, 4, 3):
                    if st.on(3):
                        t, j = st.tile(3), st.slot(3, 2)
                        pool.wait_ge(high, t + 1)
                        st.again(pool, st_turned, t * 4 - 3)
                        pool.sem_inc(passed, 1)
                        pool.tensor_copy(section(stk, j, 5), hm[:, j, H:2 * H, 0, :]).then_inc(pool_stacked, 1)

            @block.tensor
            def _(pe):
                pe.wait_ge(start, 3)
                pe.sem_inc(st_turned, 1)
                for st in steps(pe, TB, 4, 4):
                    if st.on(0):
                        t, j = st.tile(), st.slot(0, R)
                        pe.wait_ge(got[j], st.lap(0, R) * 16 + 16)
                        st.again(pe, vT_out, t)
                        for kk in range(KC):
                            mm = pe.transpose(psT[:, kk * P:(kk + 1) * P], v[:, j, kk * P:(kk + 1) * P], k.ident[:, :])
                        mm.then_inc(turned, 1)
                    if st.on(1):
                        t, j = st.tile(1), st.slot(1, 2)
                        pe.wait_ge(vT_out, t + 1)
                        st.again(pe, clipped, t - 1)
                        for kk in range(KC):
                            mm = pe.matmul(psQK[:, j, :], vT[:, j, kk, :], k.w1qkv[:, kk, 0:2 * C],
                                           start=(kk == 0), stop=(kk == KC - 1))
                        mm.then_inc(qk_ready, 1)
                        st.again(pe, v_out, t)
                        for kk in range(KC):
                            mm = pe.matmul(psV[:, 0:C], vT[:, j, kk, :], k.w1qkv[:, kk, 2 * C:3 * C],
                                           start=(kk == 0), stop=(kk == KC - 1))
                        mm.then_inc(v_ready, 1)
                    if st.on(4):
                        t, j = st.tile(4), st.slot(4, 2)
                        pe.wait_ge(stacked, t + 1)
                        pe.wait_ge(low, t + 1)
                        pe.wait_ge(pool_stacked, t + 1)
                        for n, stk_ in enumerate((stq, stk)):
                            for half in range(2):
                                pe.wait_ge(evac_dve if half == 0 else evac_act, t * 2 + 1 + n)
                                for hh in range(HB):
                                    mm = pe.transpose(psS[:, n * 2 + half, hh * P:(hh + 1) * P],
                                                      stk_[:, j, half * HB + hh, :], k.identb[:, :])
                                mm.then_inc(st_turned, 1)

            @block.vector
            def _(dve):
                dve.sem_inc(evac_dve, 2)
                for st in steps(dve, TB, 4, 4):
                    if st.on(1):
                        t, j = st.tile(1), st.slot(1, 2)
                        dve.wait_ge(qk_ready, t + 1)
                        dve.tensor_scalar(qk[:, j, :, :].rearrange("p h d -> p (h d)"), psQK[:, j, :], -5.0, 5.0,
                                          ALU.max, ALU.min).then_inc(clipped, 1)
                    if st.on(2):
                        t, j = st.tile(2), st.slot(2, 2)
                        dve.wait_ge(rooted, t + 1)
                        dve.tensor_scalar(qk[:, j, 0:H, 0], root[:, j, 0:H], -1.0, None, ALU.mult)
                        dve.tensor_copy(qk[:, j, H:2 * H, 0], root[:, j, H:2 * H]).then_inc(led, 1)
                    if st.on(4):
                        evacuate(dve, dve.tensor_copy, st, 0, 0, evac_dve)
                    if st.on(3):
                        t, j = st.tile(3), st.slot(3, 2)
                        dve.wait_ge(middle, t + 1)
                        st.again(dve, st_turned, t * 4 - 3)
                        dve.tensor_tensor(section(stq, j, 5), rest[:, j, 0:H, :], hm[:, j, 0:H, 1, :], ALU.subtract)
                        dve.tensor_tensor(section(stk, j, 2), rest[:, j, H:2 * H, :], hm[:, j, H:2 * H, 1, :],
                                          ALU.subtract).then_inc(low, 1)
                    if st.on(2):
                        t, j = st.tile(2), st.slot(2, 2)
                        dve.wait_ge(led, t + 1)
                        st.again(dve, stacked, t - 1)
                        st.again(dve, pool_stacked, t - 1)
                        dve.tensor_copy(hm[:, j, :, 0, :], qk[:, j, :, :]).then_inc(high, 1)
                    if st.on(4):
                        evacuate(dve, dve.tensor_copy, st, 1, 0, evac_dve)
                    if st.on(2):
                        dve.wait_ge(high, t + 1)
                        dve.tensor_tensor(rest[:, j, :, :], qk[:, j, :, :], hm[:, j, :, 0, :],
                                          ALU.subtract).then_inc(left, 1)
                    if st.on(1):
                        u, i = st.tile(1), st.slot(1, 2)
                        dve.wait_ge(squared, u + 1)
                        dve.tensor_reduce(root[:, i, :], sq[:, :, 1:D], AX.X, ALU.add).then_inc(summed, 1)
                    if st.on(2):
                        dve.wait_ge(left, t + 1)
                        dve.tensor_copy(hm[:, j, :, 1, :], rest[:, j, :, :]).then_inc(middle, 1)
                    if st.on(1):
                        dve.wait_ge(summed, u * 2 + 1)
                        dve.tensor_scalar(root[:, i, :], root[:, i, :], 1.0, EPS, ALU.add, ALU.add).then_inc(summed, 1)

            @block.scalar
            def _(act):
                def copy(o, i):
                    return act.activation(o, i, ACT.Copy)

                act.wait_ge(start, 3)
                act.sem_inc(evac_act, 2)
                for st in steps(act, TB, 4, 4):
                    if st.on(0):
                        t, j = st.tile(), st.slot(0, 2)
                        act.wait_ge(turned, t + 1)
                        st.again(act, v_ready, t - 1)
                        copy(vT[:, j, :, :], psT[:, 0:C].rearrange("p (k c) -> p k c", k=KC)).then_inc(vT_out, 1)
                    if st.on(2):
                        t, j = st.tile(2), st.slot(2, 2)
                        act.wait_ge(summed, t * 2 + 2)
                        act.activation(root[:, j, :], root[:, j, :], ACT.Sqrt).then_inc(rooted, 1)
                    if st.on(1):
                        t, j = st.tile(1), st.slot(1, 2)
                        act.wait_ge(clipped, t + 1)
                        st.again(act, summed, t * 2)
                        act.activation(sq[:, :, :], qk[:, j, :, :], ACT.Square).then_inc(squared, 1)
                    if st.on(4):
                        evacuate(act, copy, st, 0, 1, evac_act)
                    if st.on(1):
                        act.wait_ge(v_ready, t + 1)
                        copy(tile(k.V, t), psV[:, 0:C]).then_inc(v_out, 1)
                    if st.on(3):
                        t, j = st.tile(3), st.slot(3, 2)
                        act.wait_ge(middle, t + 1)
                        st.again(act, st_turned, t * 4 - 3)
                        q, kk = hm[:, j, 0:H, :, :], hm[:, j, H:2 * H, :, :]
                        copy(stq[:, j, :, 0:3 * D].rearrange("p h (s d) -> p h s d", d=D),
                             q[:, :, 0:1, :].to_broadcast([P, H, 3, D]))
                        copy(stq[:, j, :, 3 * D:5 * D].rearrange("p h (s d) -> p h s d", d=D),
                             q[:, :, 1:2, :].to_broadcast([P, H, 2, D]))
                        copy(stk[:, j, :, 0:6 * D].rearrange("p h (r s) -> p h r s", r=2)[:, :, :, 0:2 * D],
                             kk.rearrange("p h s d -> p h (s d)").unsqueeze(2).to_broadcast([P, H, 2, 2 * D])
                             ).then_inc(stacked, 1)
                    if st.on(4):
                        evacuate(act, copy, st, 1, 1, evac_act)


def attention(nc, k, b):
    KT16 = TB
    QC = TS // BANK
    GM = 4
    UN = 2 * BANK
    VW = 32
    with Stage(nc, f"at{b}") as s:
        pexp = s.sb("pexp", [P, 4, UN])
        vst = s.sb("vst", [P, 2, KT16, VW])
        ksumT = s.sb("ksumT", [P, 2, TS // GM], BF16)
        mx = s.sb("mx", [P, KT16])
        sa, sb_ = s.sb("sa", [P, KT16]), s.sb("sb", [P, KT16])
        shift = s.sb("shift", [P, KT16, 3], BF16)
        oT = s.sb("oT", [P, BANK])
        inv = s.sb("inv", [P, QC, QC])
        psS = s.ps("psS", [P, 2, UN])
        psO = s.ps("psO", [P, BANK])
        psM = s.ps("psM", [P, 2, BANK])
        psX = s.ps("psX", [P, BANK])
        (scored, raised, weighed, v_ready, o_out, o_turned, maxed, reduced, k_ready, q_ready, shifted, x_turned, x_free,
         chain, divided, start) = (
            s.sem(n) for n in ("scored", "raised", "weighed", "vready", "oout", "oturned", "maxed", "reduced", "kready",
                               "qready", "shifted", "xturned", "xfree", "chain", "divided", "start"))

        def shift_use(h, half):
            return 1 + half if isinstance(h, int) and h == 0 else h * 3 + half

        with nc.Block() as block:

            def head_of(ap, h):
                return ap[:, ds(h, 1), :].rearrange("p a t -> p (a t)")

            @block.gpsimd
            def _(pool):
                def take_v(h, j):
                    pool.tensor_copy(vst[:, j, :, 0:D], k.V[:, :, ds(h * D, D)]).then_inc(v_ready, 1)

                pool.memset(vst[:, :, :, :], 0.0).then_inc(start, 1)
                pool.wait_ge(start, 1)
                pool.memset(vst[:, :, :, D:D + 1], 1.0).then_inc(start, 1)
                pool.wait_ge(start, 2)
                take_v(0, 0)
                take_v(1, 1)
                with pool.Fori(0, H // 2 - 1) as i:
                    for j in range(2):
                        pool.wait_ge(weighed, (i * 2 + j + 1) * KT16 + 2)
                        take_v(i * 2 + j + 2, j)

            @block.tensor
            def _(pe):
                def scores(h, kt, u2):
                    u = h * 2 * KT16 + kt * 2 + u2
                    pe.wait_ge(raised, u + 1)
                    for c in range(2):
                        mm = pe.matmul(psS[:, u2, c * BANK:(c + 1) * BANK],
                                       k.KT[:, ds(h, 1), kt * P:(kt + 1) * P].rearrange("p a t -> p (a t)"),
                                       k.QT[:, ds(h, 1), u2 * UN + c * BANK:u2 * UN + (c + 1) * BANK].rearrange(
                                           "p a t -> p (a t)"), start=True, stop=True)
                    mm.then_inc(scored, 1)

                def weigh(h, j, kt):
                    pe.wait_ge(raised, h * 2 * KT16 + kt * 2 + 4)
                    if kt == 0:
                        pe.wait_ge(o_out, h)
                        pe.wait_ge(v_ready, h + 1)
                    for c in range(QC):
                        mm = pe.matmul(psO[c * VW:(c + 1) * VW, :], vst[:, j, kt, :],
                                       pexp[:, (kt % 2) * 2 + c // 2, (c % 2) * BANK:(c % 2 + 1) * BANK],
                                       start=(kt == 0), stop=(kt == KT16 - 1))
                    mm.then_inc(weighed, 1)

                def means(h, j, n):
                    if n == 0:
                        pe.wait_ge(k_ready, h + 1)
                    pe.wait_ge(reduced, h * KT16 + n + 1)
                    pe.matmul(psM[:, n % 2, :],
                              k.QT[:, ds(h, 1), n * P:(n + 1) * P].rearrange("p a t -> p (a t)"),
                              ksumT[:, j, :], start=True, stop=True).then_inc(maxed, 1)

                def turn_shift(h, half):
                    if half == 0:
                        pe.wait_ge(shifted, h + 1)
                    pe.wait_ge(x_free, shift_use(h, half) - 1)
                    view = psX[:, :].bitcast(BF16)
                    for n in range(KT16 // 2):
                        mm = pe.transpose(view[6 * D:6 * D + 3, n * P:(n + 1) * P],
                                          shift[:, half * (KT16 // 2) + n, :], k.identb[:, :])
                    mm.then_inc(x_turned, 1)

                def turn_out(h):
                    pe.wait_ge(o_out, h + 1)
                    pe.wait_ge(x_free, h * 3 + 4)
                    for c in range(QC):
                        mm = pe.transpose(psX[:, c * P:(c + 1) * P], oT[:, c * P:(c + 1) * P], k.ident[:, :])
                    mm.then_inc(x_turned, 1)

                def head(h, j, first=False, last=False):
                    pe.wait_ge(q_ready, h + 1)
                    for kt in range(KT16):
                        scores(h, kt, 0)
                        scores(h, kt, 1)
                        if kt:
                            weigh(h, j, kt - 1)
                        elif not first:
                            weigh(h - 1, 1 - j, KT16 - 1)
                        if kt < KT16 // 2 and not last:
                            means(h + 1, 1 - j, 2 * kt)
                            means(h + 1, 1 - j, 2 * kt + 1)
                        if kt == 2 and not first:
                            turn_out(h - 1)
                        if kt in (KT16 - 5, KT16 - 3) and not last:
                            turn_shift(h + 1, (kt - KT16 + 5) // 2)

                pe.wait_ge(start, 2)
                for n in range(KT16):
                    means(0, 0, n)
                for half in range(2):
                    turn_shift(0, half)
                head(0, 0, first=True)
                with pe.Fori(0, H // 2 - 1) as i:
                    head(i * 2 + 1, 1)
                    head(i * 2 + 2, 0)
                head(H - 1, 1, last=True)
                weigh(H - 1, 1, KT16 - 1)
                pe.wait_ge(o_out, H)
                pe.wait_ge(x_free, 3 * H - 1)
                for c in range(QC):
                    mm = pe.transpose(psX[:, c * P:(c + 1) * P], oT[:, c * P:(c + 1) * P], k.ident[:, :])
                mm.then_inc(x_turned, 1)

            @block.scalar
            def _(act):
                act.sem_inc(raised, 2)
                with act.Fori(0, H) as h:
                    for u in range(2 * KT16):
                        act.wait_ge(scored, h * 2 * KT16 + u + 1)
                        if u % 2 == 0:
                            act.wait_ge(weighed, h * KT16 + u // 2 + 1)
                        act.activation(pexp[:, u % 4, :], psS[:, u % 2, :], ACT.Exp,
                                       scale=D ** -0.5).then_inc(raised, 1)

            @block.vector
            def _(dve):
                dve.sem_inc(weighed, 2)
                dve.sem_inc(reduced, 2)

                def sum_keys(h, j):
                    with nc.allow_low_precision(reason="the shift need not be exact"):
                        dve.tensor_reduce(ksumT[:, j, :], head_of(k.KT, h).rearrange("p (g m) -> p g m", m=GM),
                                          AX.X, ALU.add).then_inc(k_ready, 1)

                def reduce(h, n):
                    dve.wait_ge(maxed, h * KT16 + n + 1)
                    dve.tensor_reduce(mx[:, n:n + 1], psM[:, n % 2, :], AX.X, ALU.max).then_inc(reduced, 1)

                def step(h, n, ins):
                    ins.then_inc(chain, 1)
                    dve.wait_ge(chain, h * 7 + n + 1)

                def make_shift(h):
                    dve.wait_ge(reduced, h * KT16 + KT16 + 2)
                    step(h, 0, dve.tensor_scalar(sa[:, :], mx[:, :], 0.25, 280.0, ALU.mult, ALU.add))
                    step(h, 1, dve.tensor_scalar(sa[:, :], sa[:, :], -280.0, None, ALU.min))
                    step(h, 2, dve.scalar_tensor_tensor(sb_[:, :], mx[:, :], 0.25, sa[:, :], ALU.mult, ALU.max))
                    step(h, 3, dve.tensor_scalar(sb_[:, :], sb_[:, :], -1.0, None, ALU.mult))
                    step(h, 4, dve.tensor_copy(shift[:, :, 0], sb_[:, :]))
                    step(h, 5, dve.tensor_tensor(sa[:, :], sb_[:, :], shift[:, :, 0], ALU.subtract))
                    step(h, 6, dve.tensor_copy(shift[:, :, 1], sa[:, :]))
                    dve.tensor_tensor(shift[:, :, 2], sa[:, :], shift[:, :, 1], ALU.subtract).then_inc(shifted, 1)

                def put_shift(h, half):
                    dve.wait_ge(x_turned, shift_use(h, half))
                    ins = dve.tensor_copy(
                        k.QT[6 * D:6 * D + 3, ds(h, 1), half * UN:(half + 1) * UN].rearrange("p a t -> p (a t)"),
                        psX[:, :].bitcast(BF16)[6 * D:6 * D + 3, :])
                    ins.then_inc(x_free, 1)
                    if half == 1:
                        dve.wait_ge(x_free, shift_use(h, 1))
                        dve.sem_inc(q_ready, 1)

                def take_out(h):
                    dve.wait_ge(weighed, h * KT16 + KT16 + 2)
                    dve.wait_ge(x_turned, h * 3 + 2)
                    dve.tensor_copy(oT[:, :], psO[:, :]).then_inc(o_out, 1)

                def divide(h, count):
                    dve.wait_ge(x_turned, count)
                    o = psX[:, :].rearrange("p (c j d) -> p c j d", c=QC, j=QC)
                    dve.reciprocal(inv[:, :, :], o[:, :, :, D]).then_inc(divided, 1)
                    dve.wait_ge(divided, h + 1)
                    dve.tensor_tensor(k.O[:, :, ds(h * D, D)].rearrange("p (j c) d -> p c j d", j=QC),
                                      o[:, :, :, 0:D], inv[:, :, :].unsqueeze(3).to_broadcast([P, QC, QC, D]),
                                      ALU.mult).then_inc(x_free, 1)

                def head(h, first=False, last=False):
                    if not last:
                        reduce(h + 1, 0)
                        reduce(h + 1, 1)
                    if not first:
                        take_out(h - 1)
                    for n in range(2, 6):
                        if not last:
                            reduce(h + 1, n)
                    if not first:
                        divide(h - 1, h * 3 + 2)
                    if last:
                        return
                    for n in range(6, KT16):
                        reduce(h + 1, n)
                    make_shift(h + 1)
                    put_shift(h + 1, 0)
                    put_shift(h + 1, 1)

                sum_keys(0, 0)
                for n in range(KT16):
                    reduce(0, n)
                make_shift(0)
                put_shift(0, 0)
                put_shift(0, 1)
                sum_keys(1, 1)
                head(0, first=True)
                sum_keys(2, 0)
                with dve.Fori(0, H // 2 - 2) as i:
                    head(i * 2 + 1)
                    sum_keys(i * 2 + 3, 1)
                    head(i * 2 + 2)
                    sum_keys(i * 2 + 4, 0)
                head(H - 3)
                sum_keys(H - 1, 1)
                head(H - 2)
                head(H - 1, last=True)
                take_out(H - 1)
                divide(H - 1, 3 * H)


def attention_out(nc, k, b, u, x3_out):
    G = 4
    NG, NPR = TB // G, TB // 2
    with Stage(nc, f"ao{b}") as s:
        x2 = s.sb("x2", [P, 2, G, C])
        oT = s.sb("oT", [P, 2, KC, 2, P])
        junk = s.sb("junk", [P, C])
        s2, vn, e1, e2, t2, pl, sm, g = (s.sb(v, [P, TB]) for v in ("s2", "vn", "e1", "e2", "t2", "pl", "sm", "g"))
        psT = s.ps("psT", [P, 2, BANK])
        psU = s.ps("psU", [P, 3, 2 * C])
        (turned, oT_out, u_ready, u_out, squared, chain, asked, done_act, scaled, clipped, led, added, x3_stored) = (
            s.sem(v) for v in ("turned", "oTout", "uready", "uout", "squared", "chain", "asked", "doneact", "scaled",
                               "clipped", "led", "added", "x3stored"))
        x2_in = s.sems("x2in", 2)
        with nc.Block() as block:

            @block.sync
            def _(sp):
                for n in range(NG):
                    if n >= 2:
                        sp.wait_ge(added, n - 1)
                    sp.dma_start(x2[:, n % 2, :, :], k.x2_t[:, b * TB + n * G:b * TB + (n + 1) * G, :]).then_inc(
                        x2_in[n % 2], 16)
                if x3_out is not None:
                    for n in range(NG):
                        sp.wait_ge(added, n + 1)
                        sp.dma_start(x3_out[:, n * G:(n + 1) * G, :], u[:, n * G:(n + 1) * G, :]).then_inc(x3_stored, 16)
                    sp.wait_ge(x3_stored, 16 * NG)

            @block.tensor
            def _(pe):
                for n in range(NPR + 1):
                    if n < NPR:
                        if n >= 2:
                            pe.wait_ge(oT_out, n - 1)
                        for kk in range(KC):
                            for q in range(2):
                                mm = pe.transpose(psT[:, n % 2, (kk * 2 + q) * P:(kk * 2 + q + 1) * P],
                                                  k.O[:, 2 * n + q, kk * P:(kk + 1) * P], k.ident[:, :])
                        mm.then_inc(turned, 1)
                    if n:
                        m = n - 1
                        pe.wait_ge(oT_out, m + 1)
                        if m >= 3:
                            pe.wait_ge(u_out, m - 2)
                        for q in range(2):
                            for kk in range(KC):
                                mm = pe.matmul(psU[:, m % 3, q * C:(q + 1) * C], oT[:, m % 2, kk, q, :],
                                               k.w1o[:, kk, :], start=(kk == 0), stop=(kk == KC - 1))
                        mm.then_inc(u_ready, 1)

            @block.vector
            def _(dve):
                ser = Serial(dve, chain)
                for n in range(NPR):
                    dve.wait_ge(u_ready, n + 1)
                    dve.tensor_copy(u[:, 2 * n:2 * n + 2, :],
                                    psU[:, n % 3, :].rearrange("p (t c) -> p t c", c=C)).then_inc(u_out, 1)
                dve.wait_ge(squared, TB)
                ser(dve.tensor_scalar(vn[:, :], s2[:, :], 0.0, EPS, ALU.max, ALU.add))
                dve.sem_inc(asked, 1)
                dve.wait_ge(done_act, 1)
                ser(dve.tensor_scalar(vn[:, :], vn[:, :], 5.0, None, ALU.min))
                dve.sem_inc(asked, 1)
                ser(dve.tensor_tensor(t2[:, :], vn[:, :], vn[:, :], ALU.mult))
                ser(dve.tensor_scalar(pl[:, :], t2[:, :], 1.0 / 42.0, 1.0, ALU.mult, ALU.add))
                ser(dve.scalar_tensor_tensor(pl[:, :], t2[:, :], 1.0 / 20.0, pl[:, :], ALU.mult, ALU.mult))
                ser(dve.tensor_scalar(pl[:, :], pl[:, :], 1.0, None, ALU.add))
                ser(dve.scalar_tensor_tensor(pl[:, :], t2[:, :], 1.0 / 6.0, pl[:, :], ALU.mult, ALU.mult))
                ser(dve.tensor_scalar(pl[:, :], pl[:, :], 1.0, None, ALU.add))
                ser(dve.tensor_tensor(pl[:, :], pl[:, :], vn[:, :], ALU.mult))
                ser(dve.tensor_scalar(sm[:, :], vn[:, :], 0.5, None, ALU.is_lt))
                dve.wait_ge(done_act, 3)
                ser(dve.tensor_tensor(e1[:, :], e1[:, :], e2[:, :], ALU.subtract))
                ser(dve.tensor_scalar(e1[:, :], e1[:, :], 0.5, None, ALU.mult))
                ser(dve.tensor_tensor(pl[:, :], pl[:, :], e1[:, :], ALU.subtract))
                ser(dve.tensor_tensor(pl[:, :], pl[:, :], sm[:, :], ALU.mult))
                ser(dve.tensor_tensor(e1[:, :], e1[:, :], pl[:, :], ALU.add))
                ser(dve.tensor_scalar(t2[:, :], vn[:, :], EPS, None, ALU.add))
                ser(dve.reciprocal(e2[:, :], t2[:, :]))
                ser(dve.tensor_tensor(g[:, :], e1[:, :], e2[:, :], ALU.mult))
                dve.sem_inc(asked, 1)
                for n in range(NG):
                    part = u[:, n * G:(n + 1) * G, :]
                    dve.wait_ge(scaled, (n + 1) * G)
                    dve.tensor_scalar(part, part, -8.0, 8.0, ALU.max, ALU.min).then_inc(clipped, 1)
                dve.wait_ge(squared, 2 * TB)
                ser(dve.tensor_scalar(s2[:, :], s2[:, :], 1.0, EPS, ALU.add, ALU.add))
                dve.sem_inc(asked, 1)
                dve.wait_ge(done_act, 4)
                dve.tensor_copy(u[:, :, 0], s2[:, :]).then_inc(led, 1)
                dve.wait_ge(led, 1)
                for n in range(NG):
                    part = u[:, n * G:(n + 1) * G, :]
                    dve.wait_ge(x2_in[n % 2], (n // 2 + 1) * 16)
                    dve.tensor_tensor(part, part, x2[:, n % 2, :, :], ALU.add).then_inc(added, 1)
                    dve.wait_ge(added, n + 1)
                    for t in range(n * G, (n + 1) * G):
                        dve.bn_stats(k.st6[:, b * TB + t, :], u[:, t, :])

            @block.scalar
            def _(act):
                for n in range(NPR + 1):
                    if n < NPR:
                        act.wait_ge(turned, n + 1)
                        if n >= 2:
                            act.wait_ge(u_ready, n - 1)
                        act.activation(oT[:, n % 2, :, :, :].rearrange("p k q c -> p (k q c)"), psT[:, n % 2, :],
                                       ACT.Copy).then_inc(oT_out, 1)
                    if n:
                        m = n - 1
                        act.wait_ge(u_out, m + 1)
                        for q in range(2):
                            if m or q:
                                act.wait_ge(squared, 2 * m + q)
                            act.activation(junk[:, 1:C], u[:, 2 * m + q, 1:C], ACT.Square,
                                           accum_out=s2[:, 2 * m + q:2 * m + q + 1]).then_inc(squared, 1)
                act.wait_ge(asked, 1)
                act.activation(vn[:, :], vn[:, :], ACT.Sqrt).then_inc(done_act, 1)
                act.wait_ge(asked, 2)
                act.activation(e1[:, :], vn[:, :], ACT.Exp).then_inc(done_act, 1)
                act.activation(e2[:, :], vn[:, :], ACT.Exp, scale=-1.0).then_inc(done_act, 1)
                act.wait_ge(asked, 3)
                act.wait_ge(u_out, NPR)

                def scale(n):
                    for t in range(n * G, (n + 1) * G):
                        act.activation(u[:, t, :], u[:, t, :], ACT.Copy, scale=g[:, t:t + 1]).then_inc(scaled, 1)

                scale(0)
                for n in range(NG):
                    if n + 1 < NG:
                        scale(n + 1)
                    act.wait_ge(clipped, n + 1)
                    for t in range(n * G, (n + 1) * G):
                        act.wait_ge(squared, TB + t)
                        act.activation(junk[:, 1:C], u[:, t, 1:C], ACT.Square,
                                       accum_out=s2[:, t:t + 1]).then_inc(squared, 1)
                act.wait_ge(asked, 4)
                act.activation(s2[:, :], s2[:, :], ACT.Sqrt).then_inc(done_act, 1)


def load_expert_weights(nc, k, a):
    with Stage(nc, "lw") as s:
        cleared, b_in = s.sem("cleared"), s.sem("bin")
        picked, chain = s.sem("picked"), s.sem("chain")
        raw = s.sb("raw", [P, HG, 2, HW])
        part = s.sb("part", [P, 2, HG * 2 * HW], BF16)
        with nc.Block() as block:

            @block.sync
            def _(sp):
                sp.wait_ge(cleared, 1)
                for q in range(3):
                    for n, w in enumerate(("L1_ffn_bg", "L1_ffn_b1")):
                        sp.dma_start(raw[32 * q:32 * q + E, :, n, :],
                                     a[w].rearrange("e (g c) -> e g c", g=HG)).then_inc(b_in, 16)
                sp.dma_start(k.x[:, 0:TB, :], k.x3_t).then_inc(k.x_in, 16)
                for e in range(E):
                    for n, w in enumerate(("L1_ffn_Wg", "L1_ffn_W1")):
                        for kk in range(KC):
                            sp.dma_start(k.wgu[:, e, kk, :, n, :],
                                         a[w][e, kk * P:(kk + 1) * P, :].rearrange("p (g c) -> p g c", g=HG)
                                         ).then_inc(k.w_in[e], 16)
                    sp.dma_start(k.w2b[0:HP, e, :, :],
                                 a["L1_ffn_W2"][e, :, :].rearrange("(n p) c -> p n c", p=HP)).then_inc(k.w_in[e], 16)
                    sp.dma_start(k.w2b[HP:HP + 1, e, HK - 1, :], a["L1_ffn_b2"][e:e + 1, :]).then_inc(k.w_in[e], 16)

            @block.gpsimd
            def _(pool):
                pool.memset(k.pick[:, :, :], 0.0).then_inc(picked, 1)
                pool.wait_ge(picked, 1)
                for q in range(3):
                    pool.affine_select(out=k.pick[32 * q:32 * (q + 1), :, :], in_=k.pick[32 * q:32 * (q + 1), :, :],
                                       compare_op=ALU.not_equal, fill=1.0, base=0, pattern=[[-1, E], [0, P]],
                                       channel_multiplier=1).then_inc(picked, 1)

            @block.vector
            def _(dve):
                ser = Serial(dve, chain)
                dve.memset(raw[:, :, :, :], 0.0).then_inc(cleared, 1)
                ser(dve.memset(k.bias[:, :], 0.0))
                dve.wait_ge(b_in, 16 * 6)
                flat = raw[:, :, :, :].rearrange("p g n c -> p (g n c)")
                ser(dve.tensor_copy(part[:, 0, :], flat))
                ser(dve.tensor_copy(k.bias[0:32, :], part[0:32, 0, :]))
                ser(dve.tensor_tensor(flat, flat, part[:, 0, :], ALU.subtract))
                ser(dve.tensor_copy(part[:, 1, :], flat))
                ser(dve.tensor_copy(k.bias[32:64, :], part[32:64, 1, :]))
                ser(dve.tensor_tensor(k.bias[64:96, :], flat[64:96, :], part[64:96, 1, :], ALU.subtract))


def experts1(nc, k):
    G2 = 2 * HW
    with Stage(nc, "ex1") as s:
        idx, odx = s.sb("idx", [P, GR, 1], U32), s.sb("odx", [P, 2, 1], U32)
        xg = s.sb("xg", [P, GR, C])
        xT = s.sb("xT", [P, 2, KC, P])
        sg = s.sb("sg", [P, HG, HW])
        h = s.sb("h", [P, 2, HG, HW])
        hT = s.sb("hT", [P, 2, HK, P])
        y = s.sb("y", [P, 2, C])
        psX = s.ps("psX", [P, 2, BANK])
        psH = s.ps("psH", [P, HG, BANK])
        psG = s.ps("psG", [P, 2, BANK])
        psY = s.ps("psY", [P, BANK])
        HB = HK // 2
        (x_turned, x_out, h_ready, gated, h_done, h_turned, hl_out, hr_out, y_ready,
         y_done, start) = (
            s.sem(v) for v in ("xturned", "xout", "hready", "gated", "hdone", "hturned", "hlout", "hrout", "yready",
                               "ydone", "start"))
        got, put = s.sems("got", GR), s.sems("put", 2)
        indexed, passed = s.sem("indexed"), s.sem("passed")
        with nc.Block() as block:

            @block.gpsimd
            def _(pool):
                slot_transfers(pool, k, idx, odx, xg, y, got, put, x_turned, y_done, indexed, passed)

            @block.tensor
            def _(pe):
                for e in range(E):
                    pe.wait_ge(k.w_in[e], 16 * 6)
                pe.wait_ge(start, 2)
                for st in steps(pe, NTILE, 4, 3):
                    if st.on(0):
                        t, g, j = st.tile(0), st.slot(0, GR), st.slot(0, 2)
                        pe.wait_ge(got[g], st.lap(0, GR) * 16 + 16)
                        st.again(pe, x_out, t - 1)
                        for kk in range(KC):
                            mm = pe.transpose(psX[:, j, kk * P:(kk + 1) * P], xg[:, g, kk * P:(kk + 1) * P],
                                              k.ident[:, :])
                        mm.then_inc(x_turned, 1)
                    if st.on(1):
                        t, j = st.tile(1), st.slot(1, 2)
                        e = pe.value_load(k.tile_expert[0:1, ds(t, 1)], min_val=0, max_val=E - 1)
                        pe.wait_ge(x_out, t + 1)
                        for n in range(HG):
                            st.again(pe, h_done, t * HG - HG + n + 1)
                            pe.matmul(psH[:, n, 0:G2], k.pick[:, ds(e, 1), :].rearrange("p a c -> p (a c)"),
                                      k.bias[:, n * G2:(n + 1) * G2], start=True, stop=False)
                            for kk in range(KC):
                                mm = pe.matmul(psH[:, n, 0:G2], xT[:, j, kk, :],
                                               k.wgu[:, ds(e, 1), kk, n, :, :].rearrange("p a n c -> p (a n c)"),
                                               start=False, stop=(kk == KC - 1))
                            mm.then_inc(h_ready, 1)
                    if st.on(2):
                        t, j = st.tile(2), st.slot(2, 2)
                        pe.wait_ge(h_done, t * HG + HG)
                        for n, out in enumerate((hl_out, hr_out)):
                            st.again(pe, out, t)
                            for m in range(HB):
                                g = n * HB + m
                                mm = pe.transpose(psG[0:HP, n, m * P:(m + 1) * P],
                                                  h[:, j, g // 2, (g % 2) * HP:(g % 2 + 1) * HP], k.ident[:, :])
                            mm.then_inc(h_turned, 1)
                    if st.on(3):
                        t, j = st.tile(3), st.slot(3, 2)
                        e = pe.value_load(k.tile_expert[0:1, ds(t, 1)], min_val=0, max_val=E - 1)
                        st.again(pe, y_done, t)
                        for g in range(HK):
                            if g % HB == 0:
                                pe.wait_ge((hl_out, hr_out)[g // HB], t + 1)
                            rows = HP + (g == HK - 1)
                            mm = pe.matmul(psY[:, 0:C], hT[0:rows, j, g, :],
                                           k.w2b[0:rows, ds(e, 1), g, :].rearrange("p a c -> p (a c)"),
                                           start=(g == 0), stop=(g == HK - 1))
                        mm.then_inc(y_ready, 1)

            @block.scalar
            def _(act):
                for st in steps(act, NTILE, 8, 2):
                    if st.on(0):
                        t, j = st.tile(0), st.slot(0, 2)
                        act.wait_ge(x_turned, t + 1)
                        st.again(act, h_ready, (t - 1) * HG)
                        act.activation(xT[:, j, :, :], psX[:, j, 0:C].rearrange("p (k c) -> p k c", k=KC),
                                       ACT.Copy).then_inc(x_out, 1)
                    if st.on(1):
                        t = st.tile(1)
                        for n in range(HG):
                            act.wait_ge(h_ready, t * HG + n + 1)
                            st.again(act, h_done, t * HG - HG + n + 1)
                            act.activation(sg[:, n, :], psH[:, n, 0:HW], ACT.Silu).then_inc(gated, 1)
                    if st.on(2):
                        t, j = st.tile(2), st.slot(2, 2)
                        act.wait_ge(h_turned, t * 2 + 2)
                        st.again(act, y_ready, t - 1)
                        act.activation(hT[0:HP, j, HB:HK, :],
                                       psG[0:HP, 1, 0:HB * P].rearrange("p (k c) -> p k c", k=HB),
                                       ACT.Copy).then_inc(hr_out, 1)

            @block.vector
            def _(dve):
                dve.memset(hT[:, 0, HK - 1, :], 1.0).then_inc(start, 1)
                dve.memset(hT[:, 1, HK - 1, :], 1.0).then_inc(start, 1)
                dve.wait_ge(start, 2)
                for st in steps(dve, NTILE, 4, 2):
                    if st.on(0):
                        t, j = st.tile(0), st.slot(0, 2)
                        st.again(dve, h_turned, t * 2 - 2)
                        for n in range(HG):
                            dve.wait_ge(gated, t * HG + n + 1)
                            dve.tensor_tensor(h[:, j, n, :], psH[:, n, HW:2 * HW], sg[:, n, :],
                                              ALU.mult).then_inc(h_done, 1)
                    if st.on(1):
                        t, j = st.tile(1), st.slot(1, 2)
                        dve.wait_ge(h_turned, t * 2 + 1)
                        st.again(dve, y_ready, t - 1)
                        dve.tensor_copy(hT[0:HP, j, 0:HB, :],
                                        psG[0:HP, 0, 0:HB * P].rearrange("p (k c) -> p k c", k=HB)).then_inc(hl_out, 1)
                    if st.on(2):
                        t, j = st.tile(2), st.slot(2, 2)
                        dve.wait_ge(y_ready, t + 1)
                        st.again(dve, put[j], st.lap(2, 2) * 16)
                        dve.tensor_scalar(y[:, j, :], psY[:, 0:C], k.wgt[:, ds(t, 1)], None,
                                          ALU.mult).then_inc(y_done, 1)


def program(nc, a, out):
    k = Consts()
    top = Stage(nc, "top")
    with top:
        constants(nc, top, k)
        k.st6 = top.sb("st6", [P, NT, 6])
        k.mv = top.sb("mv", [P, NT, 2])
        k.rstd = top.sb("rstd", [P, NT])
        k.tok = top.sb("tok", [P, NTILE], I32)
        k.dst = top.sb("dst", [P, NTILE], I32)
        k.wgt = top.sb("wgt", [P, NTILE])
        k.tile_expert = top.sb("tile_expert", [1, NTILE], I32)
        k.tilebase = top.sb("tilebase", [P, NT])
        tile_bases(nc, k)
        k.xn_d = nc.dram_tensor("normed", [T, C], F32).ap()
        k.y_d = nc.dram_tensor("expert_rows", [2 * T + 2 * P, C], F32).ap()
        k.x2_d = nc.dram_tensor("stream", [T, C], F32).ap()
        k.x2_t = k.x2_d.rearrange("(t p) c -> p t c", p=P)
        k.x3_t = nc.dram_tensor("stream3", [TS, C], F32).ap().rearrange("(t p) c -> p t c", p=P)
        k.v_t = nc.dram_tensor("tangents", [T, C], F32).ap().rearrange("(t p) c -> p t c", p=P)
        res = Stage(nc, "res")
        with res:
            k.x = res.sb("x", [P, NT, C])
            l0 = Stage(nc, "l0")
            with l0:
                k.wqkv = l0.sb("wqkv", [P, KC, 3 * C])
                k.wproj = l0.sb("wproj", [P, KC, C])
                k.gate = l0.sb("gate", [P, KC, E])
                k.w13 = l0.sb("w13", [P, E, KC, 2 * F0])
                k.w2 = l0.sb("w2", [P, E, KC, C])
                k.bproj = l0.sb("bproj", [P, C])
                load_x(nc, k, a["L0_attn_x"], a["L0_attn_bproj"])
                squares = [(a["L0_attn_Wqkv"][i * C:(i + 1) * C, :], k.wqkv[:, :, i * C:(i + 1) * C]) for i in range(3)]
                squares.append((a["L0_attn_Wproj"], k.wproj[:, :, :]))

                def expert(w):
                    return lambda e: w[ds(e, 1), :, :].rearrange("a r c -> (a r) c")

                def into(w, c0):
                    return lambda e: w[:, ds(e, 1), :, c0:c0 + C].rearrange("p a k c -> p (a k) c")

                transpose_squares(nc, k, "w0", squares, [(a["L0_ffn_gate_w"], k.gate[:, :, :])],
                                  (E, [expert(a[w]) for w in ("L0_ffn_w1", "L0_ffn_w3", "L0_ffn_w2")],
                                   [into(k.w13, 0), into(k.w13, C), into(k.w2, 0)]))
                with Stage(nc, "la") as la:
                    k.qT = la.sb("qT", [P, KC, T])
                    k.kvd = la.sb("kvd", [P, NB, KC, P + H // KC])
                    linear_attention_in(nc, k)
                    linear_attention_out(nc, k)
                route(nc, k, "rt0", 0, k.gate, k.x)
                experts0(nc, k)
            combine(nc, k, "cb0", k.x2_t, True)
            log_map(nc, k)
        wide, stacks = Stage(nc, "wide"), Stage(nc, "l1w")
        stacks.__enter__()
        with Stage(nc, "l1") as l1:
            k.w1o = l1.sb("wo", [P, KC, C])
            k.w1qkv = stacks.sb("wqkv", [P, KC, 3 * C], side="right")
            squares = [(a[f"L1_attn_W{n}"], k.w1qkv[:, :, i * C:(i + 1) * C]) for i, n in enumerate("qkv")]
            squares.append((a["L1_attn_Wo"], k.w1o[:, :, :]))
            transpose_squares(nc, k, "w1", squares, [])
            for b in range(NB):
                with Stage(nc, f"l1b{b}") as lb:
                    with Stage(nc, f"l1c{b}") as lc:
                        k.V = lc.sb("V", [P, TB, C], side="right")
                        k.QT = lc.sb("QT", [P, H, TS], BF16, side="right")
                        k.KT = lc.sb("KT", [P, H, TS], BF16, side="right")
                        stacked_heads(nc, k, b)
                        k.O = lb.sb("O", [P, TB, C])
                        attention(nc, k, b)
                    if b < NB - 1:
                        u = lb.sb("u", [P, TB, C])
                        attention_out(nc, k, b, u, k.x3_t)
                    else:
                        stacks.close()
                        wide.__enter__()
                        k.wgu = wide.sb("wgu", [P, E, KC, HG, 2, HW], side="right")
                        k.w2b = wide.sb("w2b", [P, E, HK, C], side="right")
                        k.bias = wide.sb("bias", [P, HG * 2 * HW], BF16, side="right")
                        k.pick = wide.sb("pick", [P, E, P], BF16, side="right")
                        k.x = wide.sb("x", [P, NT, C], side="right")
                        k.w_in, k.x_in = wide.sems("win", E), wide.sem("xin")
                        load_expert_weights(nc, k, a)
                        attention_out(nc, k, b, k.x[:, TB:NT, :], None)
        with Stage(nc, "r4") as r4:
            k.cent = r4.sb("cent", [P, KC, E])
            transpose_squares(nc, k, "wc", [], [(a["L1_ffn_centroid"], k.cent[:, :, :])])
            route(nc, k, "rt1", 1, k.cent, k.x)
        experts1(nc, k)
        combine(nc, k, "cb1", out.rearrange("b (t p) c -> p (b t) c", p=P), False)
        wide.close()


def tile_bases(nc, k):
    with Stage(nc, "tb") as s:
        with nc.Block() as block:

            @block.vector
            def _(dve):
                dve.tensor_scalar(k.tilebase[:, :], k.lane[:, 0:NT], float(P), None, ALU.mult)


INPUTS = ("L0_attn_x", "L0_attn_Wqkv", "L0_attn_Wproj", "L0_attn_bproj", "L0_ffn_gate_w", "L0_ffn_w1", "L0_ffn_w3",
          "L0_ffn_w2", "L1_attn_Wq", "L1_attn_Wk", "L1_attn_Wv", "L1_attn_Wo", "L1_ffn_centroid", "L1_ffn_Wg",
          "L1_ffn_bg", "L1_ffn_W1", "L1_ffn_b1", "L1_ffn_W2", "L1_ffn_b2")


def kernel(**inputs):
    import concourse.bacc as bacc
    import numpy as np
    from concourse.bass_utils import run_bass_kernel_spmd

    nc = bacc.Bacc("TRN2", target_bir_lowering=False, num_devices=1)
    arrays, args = {}, {}
    for name in INPUTS:
        array = np.ascontiguousarray(inputs[name])
        arrays["in_" + name] = array
        args[name] = nc.dram_tensor("in_" + name, array.shape, mybir.dt.from_np(array.dtype), kind="ExternalInput").ap()
    out = nc.dram_tensor("out", (NB, TS, C), F32, kind="ExternalOutput").ap()
    program(nc, args, out)
    result = run_bass_kernel_spmd(nc, [arrays], core_ids=[0])
    return result.results[0]["out"]
```

```python
from contextlib import ExitStack

import concourse.bass as bass
from concourse import mybir

ALU = mybir.AluOpType
ACT = mybir.ActivationFunctionType
AX = mybir.AxisListType
F32 = mybir.dt.float32
BF16 = mybir.dt.bfloat16
I32 = mybir.dt.int32
U32 = mybir.dt.uint32

P = 128
T, C = 4096, 256
KC = C // P
NT = T // P
NB = 2
TB = NT // NB
TS = T // NB
H, D = 16, 16
E = 8
F0 = 256
F1 = 684
HG, HW = 3, 228
HK, HP = 6, 114
NTILE = 2 * T // P + E - 1
BANK = 512
LN_EPS = 1e-5
EPS = 1e-6
GR = 4
ds = bass.ds


class Serial:

    def __init__(self, eng, sem):
        self.eng, self.sem, self.n = eng, sem, 0

    def __call__(self, ins):
        ins.then_inc(self.sem, 1)
        self.n += 1
        self.eng.wait_ge(self.sem, self.n)


class Stage:

    def __init__(self, nc, name):
        self.nc, self.name, self.stack, self.held = nc, name, ExitStack(), []

    def __enter__(self):
        self.stack.__enter__()
        return self

    def __exit__(self, *a):
        if self.held and a[0] is None:
            self.nc.clear_and_free_semaphores(self.held)
            self.nc.all_engine_barrier()
        return self.stack.__exit__(*a)

    def close(self):
        self.__exit__(None, None, None)

    def sb(self, name, shape, dt=F32, side="left"):
        return self.stack.enter_context(self.nc.sbuf_tensor(f"{self.name}_{name}", shape, dt, side=side))

    def ps(self, name, shape, dt=F32):
        return self.stack.enter_context(self.nc.psum_tensor(f"{self.name}_{name}", shape, dt))

    def sem(self, name):
        self.held.append(self.nc.alloc_semaphore(f"{self.name}_{name}"))
        return self.held[-1]

    def sems(self, name, n):
        return [self.sem(f"{name}{i}") for i in range(n)]


class Step:

    def __init__(self, i, m, unroll, n):
        self.i, self.m, self.unroll, self.n = i, m, unroll, n

    def tile(self, lag=0):
        return self.i * self.unroll + self.m - lag

    def on(self, lag=0):
        return not isinstance(self.i, int) or 0 <= self.tile(lag) < self.n

    def slot(self, lag, ring):
        return (self.m - lag) % ring

    def lap(self, lag, ring):
        return self.i * (self.unroll // ring) + (self.m - lag) // ring

    def again(self, eng, sem, value):
        if not isinstance(value, int) or value > 0:
            eng.wait_ge(sem, value)


def steps(eng, n, unroll, depth):
    assert depth <= unroll < n
    for m in range(unroll):
        yield Step(0, m, unroll, n)
    with eng.Fori(1, n // unroll) as i:
        for m in range(unroll):
            yield Step(i, m, unroll, n)
    for m in range(n % unroll + depth):
        yield Step(n // unroll, m, unroll, n)


class Consts:
    pass


def constants(nc, st, k):
    k.ident = st.sb("ident", [P, P])
    k.identb = st.sb("identb", [P, P], BF16)
    k.ones = st.sb("ones", [P, P])
    k.onesb = st.sb("onesb", [P, P], BF16)
    k.upperb = st.sb("upperb", [P, P], BF16)
    k.blockdiag = st.sb("blockdiag", [P, P])
    k.lane = st.sb("lane", [P, P])
    k.lane1 = st.sb("lane1", [P, 1])
    k.odd_rows = st.sb("odd_rows", [P, 2 * ((NTILE + 1) // 2)])
    with Stage(nc, "cst") as s:
        tmp = s.sb("tmp", [P, P], I32)
        tcol = s.sb("tcol", [P, 1], I32)
        todd = s.sb("todd", [P, 2 * ((NTILE + 1) // 2)], I32)
        filled, picked, turned = s.sem("filled"), s.sem("picked"), s.sem("turned")
        with nc.Block() as block:

            @block.gpsimd
            def _(pool):
                pool.memset(k.ident[:, :], 0.0).then_inc(filled, 1)
                pool.memset(k.ones[:, :], 1.0).then_inc(filled, 1)
                pool.memset(k.blockdiag[:, :], 1.0).then_inc(filled, 1)
                pool.iota(tmp[:, :], pattern=[[1, P]], base=0, channel_multiplier=0).then_inc(filled, 1)
                pool.iota(tcol[:, :], pattern=[[1, 1]], base=0, channel_multiplier=1).then_inc(filled, 1)
                pool.iota(todd[:, :].rearrange("p (a b) -> p a b", b=2), pattern=[[0, (NTILE + 1) // 2], [P, 2]], base=0,
                          channel_multiplier=0).then_inc(filled, 1)
                pool.wait_ge(filled, 6)
                pool.affine_select(out=k.ident[:, :], in_=k.ident[:, :], compare_op=ALU.not_equal, fill=1.0,
                                   base=0, pattern=[[-1, P]], channel_multiplier=1).then_inc(picked, 1)
                pool.affine_select(out=k.upperb[:, :], in_=k.ones[:, :], compare_op=ALU.is_gt, fill=0.0,
                                   base=0, pattern=[[1, P]], channel_multiplier=-1).then_inc(picked, 1)
                bd = k.blockdiag[:, :].rearrange("p (h d) -> p h d", d=D)
                pool.affine_select(out=bd, in_=bd, compare_op=ALU.is_ge, fill=0.0,
                                   base=0, pattern=[[-D, P // D], [0, D]], channel_multiplier=1).then_inc(picked, 1)
                pool.wait_ge(picked, 3)
                pool.affine_select(out=bd, in_=bd, compare_op=ALU.is_ge, fill=0.0,
                                   base=D - 1, pattern=[[D, P // D], [0, D]], channel_multiplier=-1).then_inc(picked, 1)

            @block.vector
            def _(dve):
                dve.wait_ge(filled, 6)
                dve.tensor_copy(k.lane[:, :], tmp[:, :]).then_inc(turned, 1)
                dve.tensor_copy(k.odd_rows[:, :], todd[:, :]).then_inc(turned, 1)
                dve.tensor_copy(k.lane1[:, :], tcol[:, :]).then_inc(turned, 1)
                dve.tensor_copy(k.onesb[:, :], k.ones[:, :]).then_inc(turned, 1)
                dve.wait_ge(picked, 3)
                dve.tensor_copy(k.identb[:, :], k.ident[:, :]).then_inc(turned, 1)


def transpose_squares(nc, k, name, squares, small, looped=None, stream=None):
    RING = 6
    with Stage(nc, name) as s:
        load_stream, stream_sums = stream_loads(nc, k, s, *stream) if stream else (None, None)
        raw = s.sb("raw", [P, RING, KC, C])
        rawsm = s.sb("rawsm", [E, max(len(small), 1), C])
        ps = s.ps("ps", [P, RING, KC * C])
        pss = s.ps("pss", [P, BANK])
        loaded = s.sems("loaded", RING)
        sm_loaded = s.sem("sm_loaded")
        turned, out_dve, out_act, sm_turned = (s.sem(x) for x in ("turned", "odve", "oact", "smt"))
        n0 = len(squares)
        per = len(looped[1]) if looped else 0
        steps = looped[0] * per // RING if looped else 0
        assert not looped or (looped[0] * per) % RING == 0 and RING % per == 0

        def rows(src):
            return src.rearrange("(b p) c -> p b c", p=P)

        def target(i, m, n):
            if m is None:
                return squares[n][1]
            e = i * (RING // per) + m // per
            return looped[2][m % per](e)

        def walk(eng, step):
            for n in range(n0):
                step(None, None, n, n % RING, n // RING)
            if looped:
                with eng.Fori(0, steps) as i:
                    for m in range(RING):
                        n = n0 + m
                        step(i, m, n, n % RING, i + n // RING)

        with nc.Block() as block:

            @block.sync
            def _(sp):
                if stream:
                    load_stream(sp)
                for j, (src, _) in enumerate(small):
                    sp.dma_start(rawsm[:, j, :], src).then_inc(sm_loaded, 16)

                def load(i, m, n, slot, lap):
                    if m is None:
                        src = squares[n][0]
                    else:
                        src = looped[1][m % per](i * (RING // per) + m // per)
                    if m is not None or n >= RING:
                        sp.wait_ge(turned, (i * RING if m is not None else 0) + n + 1)
                    sp.dma_start(raw[:, slot, :, :], rows(src)).then_inc(loaded[slot], 16)

                walk(sp, load)

            @block.tensor
            def _(pe):
                pe.sem_inc(turned, RING)

                def turn(i, m, n, slot, lap):
                    pe.wait_ge(loaded[slot], lap * 16 + 16)
                    if m is not None or n >= RING:
                        par = out_dve if n % 2 == 0 else out_act
                        pe.wait_ge(par, (i * (RING // 2) if m is not None else 0) + n // 2 + 1)
                    for kk in range(KC):
                        for b in range(KC):
                            mm = pe.transpose(ps[:, slot, kk * C + b * P:kk * C + (b + 1) * P],
                                              raw[:, slot, b, kk * P:(kk + 1) * P], k.ident[:, :])
                    mm.then_inc(turned, 1)

                walk(pe, turn)
                if small:
                    pe.wait_ge(sm_loaded, 16 * len(small))
                    for j in range(len(small)):
                        for kk in range(KC):
                            mm = pe.transpose(pss[:, (j * KC + kk) * E:(j * KC + kk + 1) * E],
                                              rawsm[:, j, kk * P:(kk + 1) * P], k.ident[0:E, 0:E])
                    mm.then_inc(sm_turned, 1)

            def copier(which, sem):
                def copy_out(eng, copy):
                    eng.sem_inc(sem, RING // 2)

                    def out(i, m, n, slot, lap):
                        if n % 2 != which:
                            return
                        eng.wait_ge(turned, (i * RING if m is not None else 0) + n + 1 + RING)
                        copy(target(i, m, n), ps[:, slot, :].rearrange("p (k c) -> p k c", k=KC)).then_inc(sem, 1)

                    walk(eng, out)
                return copy_out

            @block.vector
            def _(dve):
                if stream:
                    stream_sums(dve)
                copier(0, out_dve)(dve, dve.tensor_copy)
                if small:
                    dve.wait_ge(sm_turned, 1)
                    for j, (_, dst) in enumerate(small):
                        dve.tensor_copy(dst, pss[:, j * KC * E:(j + 1) * KC * E].rearrange("p (k e) -> p k e", k=KC))

            @block.scalar
            def _(act):
                copier(1, out_act)(act, lambda o, i: act.activation(o, i, ACT.Copy))


def tile(ap, t):
    return ap[:, ds(t, 1), :].rearrange("p a c -> p (a c)")


class Norm:

    def __init__(self, s, k):
        self.k, self.std = k, s.sb("std", [P, NT])
        self.merged, self.rooted, self.inverted = s.sem("merged"), s.sem("rooted_var"), s.sem("inverted_std")

    def vector(self, dve):
        k = self.k
        for t in range(NT):
            dve.bn_aggr(k.mv[:, t, :], k.st6[:, t, :]).then_inc(self.merged, 1)
        dve.wait_ge(self.merged, NT)
        dve.tensor_scalar(self.std[:, :], k.mv[:, :, 1], LN_EPS, None, ALU.add).then_inc(self.merged, 1)
        dve.wait_ge(self.rooted, 1)
        dve.reciprocal(k.rstd[:, :], self.std[:, :]).then_inc(self.inverted, 1)
        dve.wait_ge(self.inverted, 1)

    def scalar(self, act):
        act.wait_ge(self.merged, NT + 1)
        act.activation(self.std[:, :], self.std[:, :], ACT.Sqrt).then_inc(self.rooted, 1)

    def apply(self, dve, out, x, t):
        return dve.tensor_scalar(out, tile(x, t), self.k.mv[:, ds(t, 1), 0], self.k.rstd[:, ds(t, 1)],
                                 ALU.subtract, ALU.mult)


def stream_loads(nc, k, s, x, bproj):
    G = 4
    in_, b_in = s.sems("xin", NT // G), s.sem("bin")

    def sync(sp):
        xd = x.rearrange("b (t p) c -> p (b t) c", p=P)
        for g in range(NT // G):
            sp.dma_start(k.x[:, g * G:(g + 1) * G, :], xd[:, g * G:(g + 1) * G, :]).then_inc(in_[g], 16)
        sp.dma_start(k.bproj[:, :], bproj.partition_broadcast(P)).then_inc(b_in, 16)

    def vector(dve):
        for g in range(NT // G):
            dve.wait_ge(in_[g], 16)
            for t in range(g * G, (g + 1) * G):
                dve.bn_stats(k.st6[:, t, :], k.x[:, t, :])
        dve.wait_ge(b_in, 16)

    return sync, vector


def linear_attention_in(nc, k):
    CH = BANK
    TC = CH // P
    NCH = T // CH
    SCH = NCH // NB
    with Stage(nc, "lai") as s:
        XR = 4
        xn = s.sb("xn", [P, XR, TC, C + 1])
        xnT = s.sb("xnT", [P, 2, KC, CH])
        low = s.sb("low", [P, 4, CH])
        phik = s.sb("phik", [P, 2, TC, C])
        kx = s.sb("kx", [P, NB, KC, C + 1])
        kxT = s.sb("kxT", [P, KC, NB * KC, P])
        psT = s.ps("psT", [P, KC, CH])
        psQ = s.ps("psQ", [P, KC, CH])
        psK = s.ps("psK", [P, 2, 2 * C])
        psG = s.ps("psG", [P, KC, BANK])
        norm = Norm(s, k)
        (start, normed, x_turned, x_out, projected, clipped, raised, phi_ready, kx_added, kx_saved, kx_turned,
         kx_out, kv_ready) = (
            s.sem(v) for v in ("start", "normed", "xturned", "xout", "projected", "clipped", "raised", "phi", "kxadded",
                               "kxsaved", "kxturned", "kxout", "kvready"))

        def unit(u):
            return psQ[:, u, :] if u < 2 else psK[:, u - 2, :]

        with nc.Block() as block:

            @block.gpsimd
            def _(pool):
                pool.memset(xn[:, :, :, C:C + 1], 1.0).then_inc(start, 1)

            @block.vector
            def _(dve):
                norm.vector(dve)

                def normalise(t):
                    c = t // TC
                    if c >= XR:
                        dve.wait_ge(kx_added, c - XR + 1)
                    norm.apply(dve, xn[:, c % XR, t % TC, 0:C], k.x, t).then_inc(normed, 1)

                def clip(n):
                    c, u = n // 4, n % 4
                    dve.wait_ge(projected, n + 1)
                    dve.tensor_scalar(low[:, u, :], unit(u), 0.0, None, ALU.min).then_inc(clipped, 1)

                def phi(n):
                    c, u = n // 4, n % 4
                    dve.wait_ge(raised, n + 1)
                    if u < 2:
                        out = k.qT[:, u, c * CH:(c + 1) * CH]
                    else:
                        if c >= 2:
                            dve.wait_ge(kx_added, c - 1)
                        out = phik[:, c % 2, (u - 2) * 2:(u - 1) * 2, :].rearrange("p t c -> p (t c)")
                    dve.scalar_tensor_tensor(out, unit(u), 0.0, low[:, u, :], ALU.max, ALU.add).then_inc(phi_ready, 1)

                def save(b):
                    dve.wait_ge(kx_added, (b + 1) * SCH)
                    dve.tensor_copy(kx[:, b, :, :], psG[:, :, 0:C + 1]).then_inc(kx_saved, 1)
                    dve.wait_ge(kx_saved, b + 1)
                    for kk in range(KC):
                        dve.tensor_scalar(k.kvd[:, b, kk, P:P + H // KC],
                                          k.blockdiag[:, :].rearrange("p (h d) -> p h d", d=D)[:, :, 0],
                                          kx[:, b, kk, C:C + 1], None, ALU.mult)

                for t in range(2 * TC):
                    normalise(t)
                for c in range(NCH):
                    for u in range(4):
                        n = c * 4 + u
                        if n:
                            phi(n - 1)
                        clip(n)
                        if c + 2 < NCH:
                            normalise((c + 2) * TC + u)
                    if c == SCH + 1:
                        save(0)
                phi(NCH * 4 - 1)
                save(1)
                dve.wait_ge(kv_ready, 1)
                dve.tensor_tensor(k.kvd[:, :, :, 0:P].rearrange("p b k c -> p (b k) c"),
                                  psQ[:, 0, :].rearrange("p (n c) -> p n c", c=P),
                                  k.blockdiag[:, :].unsqueeze(1).to_broadcast([P, NB * KC, P]), ALU.mult)

            @block.scalar
            def _(act):
                norm.scalar(act)
                for c in range(NCH + 1):
                    if c < NCH:
                        for kk in range(KC):
                            act.wait_ge(x_turned, c * 2 + kk + 1)
                            if c >= 2:
                                act.wait_ge(projected, (c - 1) * 4)
                            act.activation(xnT[:, c % 2, kk, :], psT[:, kk, :], ACT.Copy).then_inc(x_out, 1)
                    if c:
                        for u in range(4):
                            act.wait_ge(clipped, (c - 1) * 4 + u + 1)
                            act.activation(low[:, u, :], low[:, u, :], ACT.Exp).then_inc(raised, 1)
                for cc in range(KC):
                    act.wait_ge(kx_turned, 1)
                    act.activation(kxT[:, cc, :, :].rearrange("p n c -> p (n c)"), psT[:, cc, :],
                                   ACT.Copy).then_inc(kx_out, 1)

            @block.tensor
            def _(pe):
                pe.wait_ge(start, 1)

                def turn(c):
                    pe.wait_ge(normed, (c + 1) * TC)
                    for kk in range(KC):
                        if c:
                            pe.wait_ge(x_out, (c - 1) * 2 + kk + 1)
                        for q in range(TC):
                            mm = pe.transpose(psT[:, kk, q * P:(q + 1) * P], xn[:, c % XR, q, kk * P:(kk + 1) * P],
                                              k.ident[:, :])
                        mm.then_inc(x_turned, 1)

                def project(c):
                    pe.wait_ge(x_out, c * 2 + 2)
                    for u in range(4):
                        if c:
                            pe.wait_ge(phi_ready, (c - 1) * 4 + u + 1)
                        if u < 2:
                            for kk in range(KC):
                                mm = pe.matmul(psQ[:, u, :], k.wqkv[:, kk, u * P:(u + 1) * P], xnT[:, c % 2, kk, :],
                                               start=(kk == 0), stop=(kk == KC - 1))
                        else:
                            for q in range(2):
                                r = (u - 2) * 2 + q
                                for kk in range(KC):
                                    mm = pe.matmul(psK[:, u - 2, q * C:(q + 1) * C],
                                                   xnT[:, c % 2, kk, r * P:(r + 1) * P], k.wqkv[:, kk, C:2 * C],
                                                   start=(kk == 0), stop=(kk == KC - 1))
                        mm.then_inc(projected, 1)

                def add_kx(c):
                    pe.wait_ge(phi_ready, (c + 1) * 4)
                    if c == SCH:
                        pe.wait_ge(kx_saved, 1)
                    for q in range(TC):
                        for kk in range(KC):
                            mm = pe.matmul(psG[:, kk, 0:C + 1], phik[:, c % 2, q, kk * P:(kk + 1) * P],
                                           xn[:, c % XR, q, :], start=(c % SCH == 0 and q == 0),
                                           stop=(c % SCH == SCH - 1 and q == TC - 1))
                    mm.then_inc(kx_added, 1)

                for c in range(NCH + 2):
                    if c < NCH:
                        turn(c)
                    if 0 <= c - 1 < NCH:
                        project(c - 1)
                    if c - 2 >= 0:
                        add_kx(c - 2)
                pe.wait_ge(kx_saved, 2)
                for cc in range(KC):
                    for n in range(NB * KC):
                        mm = pe.transpose(psT[:, cc, n * P:(n + 1) * P],
                                          kx[:, n // KC, n % KC, cc * P:(cc + 1) * P], k.ident[:, :])
                mm.then_inc(kx_turned, 1)
                pe.wait_ge(kx_out, KC)
                for n in range(NB * KC):
                    kk = n % KC
                    for cc in range(KC):
                        mm = pe.matmul(psQ[:, 0, n * P:(n + 1) * P], kxT[:, cc, n, :],
                                       k.wqkv[:, cc, 2 * C + kk * P:2 * C + (kk + 1) * P],
                                       start=(cc == 0), stop=(cc == KC - 1))
                mm.then_inc(kv_ready, 1)


def linear_attention_out(nc, k):
    NPR = NT // 2
    HH = H // KC
    with Stage(nc, "lao") as s:
        den = s.sb("den", [P, 2, 2, KC, HH])
        inv = s.sb("inv", [P, 2, 2, KC, HH])
        o = s.sb("o", [P, 2, 2, C])
        oT = s.sb("oT", [P, 2, KC, 2, P])
        psN = s.ps("psN", [P, 2, 2, BANK])
        psT = s.ps("psT", [P, 2, BANK])
        psY = s.ps("psY", [P, 2, 2 * C])
        (biased, multiplied, guarded, inverted, divided, o_turned, o_out, y_ready, y_added) = (
            s.sem(v) for v in ("biased", "mult", "guarded", "inverted", "div", "oturned", "oout", "y", "yadd"))

        def sums(j):
            v = psN[:, j, :, 0:KC * (P + HH)].rearrange("p t (k c) -> p t k c", k=KC)
            return v[:, :, :, 0:P].rearrange("p t k (h d) -> p t k h d", d=D), v[:, :, :, P:P + HH]

        with nc.Block() as block:

            @block.gpsimd
            def _(pool):
                for n in range(NPR):
                    x = k.x[:, 2 * n:2 * n + 2, :]
                    pool.tensor_tensor(x, x, k.bproj[:, :].unsqueeze(1).to_broadcast([P, 2, C]),
                                       ALU.add).then_inc(biased, 1)

            @block.tensor
            def _(pe):
                for st in range(NPR + 2):
                    if st < NPR:
                        n = st
                        if n >= 2:
                            pe.wait_ge(divided, (n - 1) * 2)
                        for q in range(2):
                            t = 2 * n + q
                            for kk in range(KC):
                                mm = pe.matmul(psN[:, n % 2, q, kk * (P + HH):(kk + 1) * (P + HH)],
                                               k.qT[:, kk, t * P:(t + 1) * P], k.kvd[:, t // TB, kk, :],
                                               start=True, stop=True)
                        mm.then_inc(multiplied, 1)
                    if 0 <= st - 1 < NPR:
                        n = st - 1
                        pe.wait_ge(divided, n * 2 + 2)
                        if n >= 2:
                            pe.wait_ge(o_out, n - 1)
                        for kk in range(KC):
                            for q in range(2):
                                mm = pe.transpose(psT[:, n % 2, (kk * 2 + q) * P:(kk * 2 + q + 1) * P],
                                                  o[:, n % 2, q, kk * P:(kk + 1) * P], k.ident[:, :])
                        mm.then_inc(o_turned, 1)
                    if st >= 2:
                        n = st - 2
                        pe.wait_ge(o_out, n + 1)
                        if n >= 2:
                            pe.wait_ge(y_added, n - 1)
                        for q in range(2):
                            for kk in range(KC):
                                mm = pe.matmul(psY[:, n % 2, q * C:(q + 1) * C], oT[:, n % 2, kk, q, :],
                                               k.wproj[:, kk, :], start=(kk == 0), stop=(kk == KC - 1))
                        mm.then_inc(y_ready, 1)

            @block.scalar
            def _(act):
                for n in range(NPR):
                    act.wait_ge(o_turned, n + 1)
                    if n >= 2:
                        act.wait_ge(y_ready, n - 1)
                    act.activation(oT[:, n % 2, :, :, :].rearrange("p k q c -> p (k q c)"), psT[:, n % 2, :],
                                   ACT.Copy).then_inc(o_out, 1)

            @block.vector
            def _(dve):
                for st in range(NPR + 3):
                    if st < NPR:
                        n = st
                        num, d = sums(n % 2)
                        dve.wait_ge(multiplied, n + 1)
                        dve.tensor_scalar(den[:, n % 2, :, :, :], d, EPS, None, ALU.add).then_inc(guarded, 1)
                        dve.wait_ge(guarded, n + 1)
                        dve.reciprocal(inv[:, n % 2, :, :, :], den[:, n % 2, :, :, :]).then_inc(inverted, 1)
                        dve.wait_ge(inverted, n + 1)
                        if n >= 2:
                            dve.wait_ge(o_turned, n - 1)
                        for q in range(2):
                            dve.tensor_tensor(o[:, n % 2, q, :].rearrange("p (k h d) -> p k h d", k=KC, d=D),
                                              num[:, q, :, :, :],
                                              inv[:, n % 2, q, :, :].unsqueeze(3).to_broadcast([P, KC, HH, D]),
                                              ALU.mult).then_inc(divided, 1)
                    if 0 <= st - 2 < NPR:
                        n = st - 2
                        dve.wait_ge(biased, n + 1)
                        dve.wait_ge(y_ready, n + 1)
                        dve.tensor_tensor(k.x[:, 2 * n:2 * n + 2, :],
                                          psY[:, n % 2, :].rearrange("p (t c) -> p t c", c=C),
                                          k.x[:, 2 * n:2 * n + 2, :], ALU.add).then_inc(y_added, 1)
                    if st >= 3:
                        n = st - 3
                        dve.wait_ge(y_added, n + 1)
                        for t in range(2 * n, 2 * n + 2):
                            dve.bn_stats(k.st6[:, t, :], k.x[:, t, :])


def route(nc, k, name, layer, gateT, x, meanwhile=None):
    with Stage(nc, name) as s:
        G, R = 4, 8
        area = s.sb("area", [P, (R + 10) * C])
        xn = area[:, 0:R * C].rearrange("p (r c) -> p r c", c=C)
        xnT = area[:, R * C:(R + 8) * C].rearrange("p (r k c) -> p r k c", r=2, k=KC)
        junk = area[:, (R + 8) * C:(R + 10) * C].rearrange("p (r c) -> p r c", r=2)
        LT = s.sb("LT", [E, G * P])
        cT2 = s.sb("cT2", [P, KC, E])
        xsq = s.sb("xsq", [P, NT])
        csq = s.sb("csq", [P, E])
        psT = s.ps("psT", [P, 4, BANK])
        psL = s.ps("psL", [P, BANK])
        psLT = s.ps("psLT", [P, G * P])
        psSum = s.ps("psSum", [P, 2, NT * E])
        psTab = s.ps("psTab", [P, BANK])
        psC, psPre, psTot = psL[:, NT * E:NT * E + E], psSum[:, 0, :], psSum[:, 1, :]
        normed, turned, x_out, scored, scores_out, logits, squared, csq_ready = (
            s.sem(v) for v in ("normed", "turned", "xout", "scored", "scoresout", "logits", "squared", "csq"))
        stored = s.sems("stored", R // G)
        norm = Norm(s, k)
        vals, work, mask = s.sb("vals", [P, NT, E]), s.sb("work", [P, NT, E]), s.sb("mask", [P, NT, E])
        one1, one2, maskb = s.sb("one1", [P, NT, E]), s.sb("one2", [P, NT, E]), s.sb("maskb", [P, NT * E], BF16)
        tot, incl, pos = s.sb("tot", [P, NT, E]), s.sb("incl", [P, NT, E]), s.sb("pos", [P, NT, E])
        desc = s.sb("desc", [P, E])
        m1, m2, c1, row = (s.sb(v, [P, NT]) for v in ("m1", "m2", "c1", "row"))
        p12 = s.sb("p12", [P, NT, 2])
        w12 = s.sb("w12", [P, NT, 2])
        hi, lo, dstv = (s.sb(v, [P, NT, 2]) for v in ("hi", "lo", "dstv"))
        pi, pj = s.sb("pi", [P, NT * 2], I32), s.sb("pj", [P, NT * 2], I32)
        ni = s.sb("ni", [P, E], I32)
        nf, ends, first = s.sb("nf", [P, E]), s.sb("ends", [P, E]), s.sb("first", [P, E])
        zeroE, zeroT = s.sb("zeroE", [P, E]), s.sb("zeroT", [P, NT])
        tes = s.sb("tes", [P, NTILE])
        PG = 4
        NPG = 2 * NT // PG
        oneLo = area[:, 0:2 * PG * P].rearrange("p (r n c) -> p r n c", r=2, n=PG)
        at = 2 * PG * P
        oneHi = area[:, at:at + 4 * PG * NTILE].rearrange("p (r n a c) -> p r n a c", r=2, n=PG, a=2)
        at += 4 * PG * NTILE
        hiEq = area[:, at:at + 2 * PG * NTILE].rearrange("p (r n c) -> p r n c", r=2, n=PG)
        at += 2 * PG * NTILE
        te = area[:, at:at + NTILE * E].rearrange("p (t e) -> p t e", e=E)
        at += NTILE * E
        raw, pad, big = (area[:, at + n * NTILE:at + (n + 1) * NTILE] for n in range(3))
        assert at + 3 * NTILE <= (R + 10) * C
        chain, soft, softed, sums_asked, sums_ready, matched, hot, weighted, tab_added = (
            s.sem(v) for v in ("chain", "soft", "softed", "asked", "sums", "matched", "hot", "weighted", "tabadd"))
        xn_d = k.xn_d.rearrange("(t p) c -> p t c", p=P)

        def bt(ap):
            return ap.unsqueeze(2).to_broadcast([P, NT, E])

        def be(ap):
            return ap.unsqueeze(1).to_broadcast([P, NT, E])

        with nc.Block() as block:

            @block.sync
            def _(sp):
                for g in range(NT // G):
                    j = g % (R // G)
                    sp.wait_ge(normed, (g + 1) * G)
                    sp.dma_start(xn_d[:, g * G:(g + 1) * G, :], xn[:, j * G:(j + 1) * G, :]).then_inc(stored[j], 16)
                if meanwhile:
                    meanwhile(sp)
                for j in range(R // G):
                    sp.wait_ge(stored[j], 16 * (NT // R))

            @block.scalar
            def _(act):
                norm.scalar(act)
                for st in steps(act, NT // G, 2, 1):
                    if st.on(0):
                        c = st.tile()
                        st.again(act, scored, c - 1)
                        for q in range(G):
                            act.wait_ge(turned, c * G + q + 1)
                            act.activation(xnT[:, st.slot(0, 2), :, q * P:(q + 1) * P],
                                           psT[:, q, 0:C].rearrange("p (k c) -> p k c", k=KC),
                                           ACT.Copy).then_inc(x_out, 1)
                            if layer == 1:
                                st.again(act, squared, c * G + q - 1)
                                act.activation(junk[:, q % 2, :], xn[:, st.slot(0, 2) * G + q, :], ACT.Square,
                                               accum_out=xsq[:, ds(c * G + q, 1)]).then_inc(squared, 1)
                    if st.on(1):
                        c = st.tile(1)
                        act.wait_ge(scored, c + 1)
                        st.again(act, logits, c)
                        act.activation(LT[:, :], psLT[0:E, :], ACT.Copy).then_inc(scores_out, 1)
                if layer == 0:
                    act.wait_ge(soft, 1)
                    act.activation(work[:, :, :], work[:, :, :], ACT.Exp).then_inc(softed, 1)
                else:
                    act.wait_ge(soft, 1)
                    act.activation(p12[:, :, :], p12[:, :, :], ACT.Sqrt).then_inc(softed, 1)
                    act.wait_ge(soft, 2)
                    act.activation(m2[:, :], m2[:, :], ACT.Exp).then_inc(softed, 1)

                for n in range(NPG):
                    act.wait_ge(matched, n + 1)
                    if n >= 2:
                        act.wait_ge(tab_added, n - 1)
                    for m in range(PG):
                        t, j = (n * PG + m) // 2, m % 2
                        ins = act.activation(oneHi[:, n % 2, m, 1, :], hiEq[:, n % 2, m, :], ACT.Copy,
                                             scale=w12[:, t, j:j + 1])
                    ins.then_inc(weighted, 1)

            @block.tensor
            def _(pe):
                for step in range(NT // G + 2):
                    if step < NT // G:
                        c = step
                        for q in range(G):
                            pe.wait_ge(normed, c * G + q + 1)
                            if c:
                                pe.wait_ge(x_out, (c - 1) * G + q + 1)
                            for kk in range(KC):
                                mm = pe.transpose(psT[:, q, kk * P:(kk + 1) * P],
                                                  xn[:, c % 2 * G + q, kk * P:(kk + 1) * P], k.ident[:, :])
                            mm.then_inc(turned, 1)
                    if 0 <= step - 1 < NT // G:
                        c = step - 1
                        pe.wait_ge(x_out, c * G + G)
                        if c:
                            pe.wait_ge(scores_out, c)
                        for kk in range(KC):
                            mm = pe.matmul(psLT[0:E, :], gateT[:, kk, :], xnT[:, c % 2, kk, :],
                                           start=(kk == 0), stop=(kk == KC - 1))
                        mm.then_inc(scored, 1)
                    if step >= 2:
                        c = step - 2
                        pe.wait_ge(scores_out, c + 1)
                        for t in range(c * G, (c + 1) * G):
                            mm = pe.transpose(psL[:, t * E:(t + 1) * E], LT[:, t % G * P:(t % G + 1) * P],
                                              k.ident[0:E, 0:E])
                        mm.then_inc(logits, 1)
                if layer == 1:
                    pe.wait_ge(csq_ready, 1)
                    for kk in range(KC):
                        mm = pe.matmul(psC, k.ones[:, :], cT2[:, kk, :], start=(kk == 0), stop=(kk == KC - 1))
                    mm.then_inc(csq_ready, 1)
                pe.wait_ge(sums_asked, 1)
                pe.matmul(psPre, k.upperb[:, :], maskb[:, :], start=True, stop=True)
                pe.matmul(psTot, k.onesb[:, :], maskb[:, :], start=True, stop=True).then_inc(sums_ready, 1)
                for n in range(NPG):
                    pe.wait_ge(hot, n + 1)
                    pe.wait_ge(weighted, n + 1)
                    for m in range(PG):
                        mm = pe.matmul(psTab[:, 0:2 * NTILE], oneLo[:, n % 2, m, :],
                                       oneHi[:, n % 2, m, :, :].rearrange("p a c -> p (a c)"),
                                       start=(n == 0 and m == 0), stop=(n == NPG - 1 and m == PG - 1))
                    mm.then_inc(tab_added, 1)

            @block.vector
            def _(dve):
                norm.vector(dve)
                if layer == 1:
                    dve.wait_ge(k.x_in, 16)
                ser = Serial(dve, chain)
                for st in steps(dve, NT, R, 0):
                    t, j = st.tile(), st.slot(0, R)
                    st.again(dve, stored[j // G], st.lap(0, R) * 16)
                    st.again(dve, turned, t - R + 1)
                    if layer == 1:
                        st.again(dve, squared, t - R + 1)
                    norm.apply(dve, xn[:, j, :], x, t).then_inc(normed, 1)
                ser(dve.memset(zeroE[:, :], 0.0))
                ser(dve.memset(zeroT[:, :], 0.0))
                ser(dve.tensor_scalar(desc[:, :], k.lane[:, 0:E], -1.0, float(E), ALU.mult, ALU.add))
                if layer == 1:
                    dve.tensor_tensor(cT2[:, :, :], gateT[:, :, :], gateT[:, :, :], ALU.mult).then_inc(csq_ready, 1)
                    dve.wait_ge(csq_ready, 2)
                    ser(dve.tensor_copy(csq[:, :], psC))
                dve.wait_ge(logits, NT // G)
                L = psL[:, 0:NT * E].rearrange("p (t e) -> p t e", e=E)
                if layer == 0:
                    ser(dve.tensor_reduce(m1[:, :], L, AX.X, ALU.max))
                    ser(dve.tensor_tensor(work[:, :, :], L, bt(m1[:, :]), ALU.subtract))
                    dve.sem_inc(soft, 1)
                    dve.wait_ge(softed, 1)
                    ser(dve.tensor_reduce(m1[:, :], work[:, :, :], AX.X, ALU.add))
                    ser(dve.reciprocal(m2[:, :], m1[:, :]))
                    ser(dve.tensor_tensor(vals[:, :, :], work[:, :, :], bt(m2[:, :]), ALU.mult))
                else:
                    dve.wait_ge(squared, NT)
                    ser(dve.tensor_scalar(work[:, :, :], L, -2.0, None, ALU.mult))
                    ser(dve.tensor_tensor(mask[:, :, :], be(csq[:, :]), bt(xsq[:, :]), ALU.add))
                    ser(dve.tensor_tensor(vals[:, :, :], work[:, :, :], mask[:, :, :], ALU.add))
                    ser(dve.tensor_scalar(vals[:, :, :], vals[:, :, :], 1e-12, None, ALU.max))

                def largest(v, val, onehot):
                    ser(dve.tensor_reduce(val, v, AX.X, ALU.max))
                    ser(dve.tensor_tensor(mask[:, :, :], v, bt(val), ALU.is_equal))
                    ser(dve.tensor_tensor(mask[:, :, :], mask[:, :, :], be(desc[:, :]), ALU.mult))
                    ser(dve.tensor_reduce(c1[:, :], mask[:, :, :], AX.X, ALU.max))
                    ser(dve.tensor_tensor(onehot, bt(c1[:, :]), be(desc[:, :]), ALU.is_equal))

                largest(vals[:, :, :], p12[:, :, 0], one1[:, :, :])
                ser(dve.tensor_scalar(mask[:, :, :], one1[:, :, :], -1.0, 1.0, ALU.mult, ALU.add))
                ser(dve.tensor_tensor(work[:, :, :], vals[:, :, :], mask[:, :, :], ALU.mult))
                ser(dve.tensor_tensor(work[:, :, :], work[:, :, :], one1[:, :, :], ALU.subtract))
                largest(work[:, :, :], p12[:, :, 1], one2[:, :, :])
                ser(dve.tensor_tensor(maskb[:, :].rearrange("p (t e) -> p t e", e=E), one1[:, :, :], one2[:, :, :],
                                      ALU.add))
                dve.sem_inc(sums_asked, 1)
                if layer == 0:
                    ser(dve.tensor_tensor(m1[:, :], p12[:, :, 0], p12[:, :, 1], ALU.add))
                    ser(dve.reciprocal(m2[:, :], m1[:, :]))
                    ser(dve.tensor_tensor(w12[:, :, :], p12[:, :, :], m2[:, :].unsqueeze(2).to_broadcast([P, NT, 2]),
                                          ALU.mult))
                else:
                    dve.sem_inc(soft, 1)
                    dve.wait_ge(softed, 1)
                    ser(dve.tensor_tensor(m2[:, :], p12[:, :, 1], p12[:, :, 0], ALU.subtract))
                    dve.sem_inc(soft, 1)
                    dve.wait_ge(softed, 2)
                    ser(dve.tensor_scalar(m1[:, :], m2[:, :], 1.0, None, ALU.add))
                    ser(dve.reciprocal(w12[:, :, 0], m1[:, :]))
                    ser(dve.tensor_tensor(w12[:, :, 1], w12[:, :, 0], m2[:, :], ALU.mult))
                dve.wait_ge(sums_ready, 1)
                ser(dve.tensor_copy(tot[:, :, :], psTot.rearrange("p (t e) -> p t e", e=E)))
                for e in range(E):
                    ins = dve.tensor_tensor_scan(incl[:, :, e], tot[:, :, e], zeroT[:, :], 0.0, ALU.add, ALU.add)
                ser(ins)
                ser(dve.tensor_scalar(nf[:, :], incl[:, NT - 1, :], float(P - 1), None, ALU.add))
                ser(dve.tensor_copy(ni[:, :], nf[:, :]))
                ser(dve.tensor_scalar(ni[:, :], ni[:, :], 7, None, ALU.logical_shift_right))
                ser(dve.tensor_copy(nf[:, :], ni[:, :]))
                ser(dve.tensor_tensor_scan(ends[:, :], nf[:, :], zeroE[:, :], 0.0, ALU.add, ALU.add))
                ser(dve.tensor_tensor(first[:, :], ends[:, :], nf[:, :], ALU.subtract))
                ser(dve.tensor_scalar(first[:, :], first[:, :], float(P), None, ALU.mult))
                ser(dve.tensor_tensor(pos[:, :, :], incl[:, :, :], tot[:, :, :], ALU.subtract))
                ser(dve.tensor_tensor(pos[:, :, :], pos[:, :, :], be(first[:, :]), ALU.add))
                ser(dve.tensor_tensor(pos[:, :, :], psPre.rearrange("p (t e) -> p t e", e=E),
                                      pos[:, :, :], ALU.add))
                for j, one in enumerate((one1, one2)):
                    ser(dve.tensor_tensor(work[:, :, :], one[:, :, :], pos[:, :, :], ALU.mult))
                    ser(dve.tensor_reduce(dstv[:, :, j], work[:, :, :], AX.X, ALU.add))
                flat = dstv[:, :, :].rearrange("p t j -> p (t j)")
                ser(dve.tensor_copy(pi[:, :], flat))
                ser(dve.tensor_scalar(pj[:, :], pi[:, :], 7, None, ALU.logical_shift_right))
                ser(dve.tensor_copy(hi[:, :, :].rearrange("p t j -> p (t j)"), pj[:, :]))
                ser(dve.tensor_scalar(pj[:, :], pi[:, :], P - 1, None, ALU.bitwise_and))
                ser(dve.tensor_copy(lo[:, :, :].rearrange("p t j -> p (t j)"), pj[:, :]))
                ser(dve.tensor_scalar(row[:, :], k.tilebase[:, :], k.lane1[:, 0:1], 1.0, ALU.add, ALU.add))
                ser(dve.tensor_copy(dstv[:, :, 0], row[:, :]))
                ser(dve.tensor_scalar(dstv[:, :, 1], row[:, :], float(T), None, ALU.add))
                for j in range(R // G):
                    dve.wait_ge(stored[j], 16 * (NT // R))

                def wide(ap, n, width):
                    v = ap[:, n * PG // 2:(n + 1) * PG // 2, :].rearrange("p t j -> p (t j)")
                    return v.unsqueeze(2).to_broadcast([P, PG, width])

                def lanes(width):
                    return k.lane[:, 0:width].unsqueeze(1).to_broadcast([P, PG, width])

                for n in range(NPG):
                    r = n % 2
                    if n >= 2:
                        dve.wait_ge(tab_added, n - 1)
                    dve.tensor_tensor(hiEq[:, r, :, :], lanes(NTILE), wide(hi, n, NTILE),
                                      ALU.is_equal).then_inc(matched, 1)
                    dve.tensor_tensor(oneLo[:, r, :, :], lanes(P), wide(lo, n, P), ALU.is_equal)
                    dve.wait_ge(matched, n + 1)
                    dve.tensor_tensor(oneHi[:, r, :, 0, :], hiEq[:, r, :, :], wide(dstv, n, NTILE),
                                      ALU.mult).then_inc(hot, 1)
                ser(dve.tensor_tensor(te[:, :, :], k.lane[:, 0:NTILE].unsqueeze(2).to_broadcast([P, NTILE, E]),
                                      ends[:, :].unsqueeze(1).to_broadcast([P, NTILE, E]), ALU.is_ge))
                ser(dve.tensor_reduce(tes[:, :], te[:, :, :], AX.X, ALU.add))
                ser(dve.tensor_scalar(tes[:, :], tes[:, :], float(E - 1), None, ALU.min))
                ser(dve.tensor_copy(k.tile_expert[:, :], tes[0:1, :]))
                dve.wait_ge(tab_added, NPG)
                ser(dve.tensor_copy(k.wgt[:, :], psTab[:, NTILE:2 * NTILE]))
                ser(dve.tensor_copy(raw[:, :], psTab[:, 0:NTILE]))
                ser(dve.tensor_scalar(pad[:, :], raw[:, :], 0.0, None, ALU.is_equal))
                ser(dve.tensor_scalar(big[:, :], k.odd_rows[:, 0:NTILE], k.lane1[:, 0:1], None, ALU.add))
                ser(dve.tensor_tensor(big[:, :], big[:, :], pad[:, :], ALU.mult))
                ser(dve.tensor_scalar(pad[:, :], pad[:, :], float(2 * T + 1), -1.0, ALU.mult, ALU.add))
                ser(dve.tensor_tensor(raw[:, :], raw[:, :], pad[:, :], ALU.add))
                ser(dve.tensor_tensor(raw[:, :], raw[:, :], big[:, :], ALU.add))
                ser(dve.tensor_copy(k.dst[:, :], raw[:, :]))
                ser(dve.tensor_scalar(k.tok[:, :], k.dst[:, :], T - 1, None, ALU.bitwise_and))


def slot_transfers(pool, k, idx, odx, xg, y, got, put, x_turned, y_done, indexed, passed):
    LAG = GR + 2
    for st in steps(pool, NTILE, 8, LAG):
        if st.on(0):
            t, g = st.tile(0), st.slot(0, GR)
            st.again(pool, got[g], st.lap(0, GR) * 16)
            st.again(pool, x_turned, t - GR + 1)
            pool.tensor_copy(idx[:, g, :], k.tok[:, ds(t, 1)]).then_inc(indexed, 1)
        if st.on(LAG):
            t, j = st.tile(LAG), st.slot(LAG, 2)
            st.again(pool, put[j], st.lap(LAG, 2) * 16)
            pool.tensor_copy(odx[:, j, :], k.dst[:, ds(t, 1)]).then_inc(indexed, 1)
        if isinstance(st.i, int):
            count = min(st.tile() + 1, NTILE) + max(st.tile() - LAG + 1, 0)
        else:
            count = st.i * 16 + 2 * st.m + 2 - LAG
        if st.on(0):
            pool.wait_ge(indexed, count)
            pool.sem_inc(passed, 1)
            pool.indirect_dma_start(xg[:, g, :], None, k.xn_d,
                                    bass.IndirectOffsetOnAxis(idx[:, g, :], 0)).then_inc(got[g], 16)
        if st.on(LAG):
            pool.wait_ge(indexed, count)
            pool.wait_ge(y_done, t + 1)
            pool.sem_inc(passed, 1)
            pool.indirect_dma_start(k.y_d, bass.IndirectOffsetOnAxis(odx[:, j, :], 0), y[:, j, :],
                                    None).then_inc(put[j], 16)
    for j in range(2):
        pool.wait_ge(put[j], 16 * ((NTILE + 1 - j) // 2))


def experts0(nc, k):
    with Stage(nc, "ex0") as s:
        idx, odx = s.sb("idx", [P, GR, 1], U32), s.sb("odx", [P, 2, 1], U32)
        xg = s.sb("xg", [P, GR, C])
        xT = s.sb("xT", [P, 2, KC, P])
        sg = s.sb("sg", [P, 2, F0])
        h = s.sb("h", [P, 2, F0])
        hT = s.sb("hT", [P, 2, KC, P])
        y = s.sb("y", [P, 2, C])
        psX = s.ps("psX", [P, 2, BANK])
        psH = s.ps("psH", [P, 2, BANK])
        psG = s.ps("psG", [P, 2, BANK])
        psY = s.ps("psY", [P, 2, BANK])
        (x_turned, x_out, h_ready, gated, h_done, h_turned, h_out, y_ready, y_done) = (
            s.sem(v) for v in ("xturned", "xout", "hready", "gated", "hdone", "hturned", "hout", "yready",
                               "ydone"))
        got, put = s.sems("got", GR), s.sems("put", 2)
        indexed, passed = s.sem("indexed"), s.sem("passed")
        with nc.Block() as block:

            @block.gpsimd
            def _(pool):
                slot_transfers(pool, k, idx, odx, xg, y, got, put, x_turned, y_done, indexed, passed)

            @block.tensor
            def _(pe):
                for st in steps(pe, NTILE, 8, 3):
                    if st.on(0):
                        t, g, j = st.tile(0), st.slot(0, GR), st.slot(0, 2)
                        pe.wait_ge(got[g], st.lap(0, GR) * 16 + 16)
                        st.again(pe, x_out, t - 1)
                        for kk in range(KC):
                            mm = pe.transpose(psX[:, j, kk * P:(kk + 1) * P], xg[:, g, kk * P:(kk + 1) * P],
                                              k.ident[:, :])
                        mm.then_inc(x_turned, 1)
                    if st.on(1):
                        t, j = st.tile(1), st.slot(1, 2)
                        e = pe.value_load(k.tile_expert[0:1, ds(t, 1)], min_val=0, max_val=E - 1)
                        pe.wait_ge(x_out, t + 1)
                        st.again(pe, h_done, t - 1)
                        for kk in range(KC):
                            mm = pe.matmul(psH[:, j, :], xT[:, j, kk, :],
                                           k.w13[:, ds(e, 1), kk, :].rearrange("p a c -> p (a c)"),
                                           start=(kk == 0), stop=(kk == KC - 1))
                        mm.then_inc(h_ready, 1)
                    if st.on(2):
                        t, j = st.tile(2), st.slot(2, 2)
                        pe.wait_ge(h_done, t + 1)
                        st.again(pe, h_out, t - 1)
                        for kk in range(KC):
                            mm = pe.transpose(psG[:, j, kk * P:(kk + 1) * P], h[:, j, kk * P:(kk + 1) * P],
                                              k.ident[:, :])
                        mm.then_inc(h_turned, 1)
                    if st.on(3):
                        t, j = st.tile(3), st.slot(3, 2)
                        e = pe.value_load(k.tile_expert[0:1, ds(t, 1)], min_val=0, max_val=E - 1)
                        pe.wait_ge(h_out, t + 1)
                        st.again(pe, y_done, t - 1)
                        for kk in range(KC):
                            mm = pe.matmul(psY[:, j, 0:C], hT[:, j, kk, :],
                                           k.w2[:, ds(e, 1), kk, :].rearrange("p a c -> p (a c)"),
                                           start=(kk == 0), stop=(kk == KC - 1))
                        mm.then_inc(y_ready, 1)

            @block.scalar
            def _(act):
                for st in steps(act, NTILE, 8, 2):
                    if st.on(0):
                        t, j = st.tile(0), st.slot(0, 2)
                        act.wait_ge(x_turned, t + 1)
                        st.again(act, h_ready, t - 1)
                        act.activation(xT[:, j, :, :], psX[:, j, 0:C].rearrange("p (k c) -> p k c", k=KC),
                                       ACT.Copy).then_inc(x_out, 1)
                    if st.on(2):
                        t, j = st.tile(2), st.slot(2, 2)
                        act.wait_ge(h_turned, t + 1)
                        st.again(act, y_ready, t - 1)
                        act.activation(hT[:, j, :, :], psG[:, j, 0:C].rearrange("p (k c) -> p k c", k=KC),
                                       ACT.Copy).then_inc(h_out, 1)
                    if st.on(1):
                        t, j = st.tile(1), st.slot(1, 2)
                        act.wait_ge(h_ready, t + 1)
                        st.again(act, h_done, t - 1)
                        act.activation(sg[:, j, :], psH[:, j, 0:F0], ACT.Silu).then_inc(gated, 1)

            @block.vector
            def _(dve):
                for st in steps(dve, NTILE, 4, 1):
                    if st.on(0):
                        t, j = st.tile(0), st.slot(0, 2)
                        dve.wait_ge(gated, t + 1)
                        st.again(dve, h_turned, t - 1)
                        dve.tensor_tensor(h[:, j, :], psH[:, j, F0:2 * F0], sg[:, j, :], ALU.mult).then_inc(h_done, 1)
                    if st.on(1):
                        t, j = st.tile(1), st.slot(1, 2)
                        dve.wait_ge(y_ready, t + 1)
                        st.again(dve, put[j], st.lap(1, 2) * 16)
                        dve.tensor_scalar(y[:, j, :], psY[:, j, 0:C], k.wgt[:, ds(t, 1)], None,
                                          ALU.mult).then_inc(y_done, 1)


def combine(nc, k, name, x_out_dram):
    G = 4
    R = 4
    with Stage(nc, name) as s:
        y = s.sb("y", [P, R, 2, G, C])
        got, paired, added, out_sem = s.sems("got", R), s.sem("paired"), s.sem("added"), s.sem("out")
        y0 = k.y_d[0:2 * T, :].rearrange("(n t p) c -> p n t c", p=P, n=2)
        with nc.Block() as block:

            @block.sync
            def _(sp):
                for g in range(NT // G):
                    if g >= R:
                        sp.wait_ge(added, g - R + 1)
                    for n in range(2):
                        sp.dma_start(y[:, g % R, n, :, :], y0[:, n, g * G:(g + 1) * G, :]).then_inc(got[g % R], 16)

            @block.vector
            def _(dve):
                for g in range(NT // G):
                    x = k.x[:, g * G:(g + 1) * G, :]
                    dve.wait_ge(got[g % R], (g // R + 1) * 32)
                    dve.tensor_tensor(y[:, g % R, 0, :, :], y[:, g % R, 0, :, :], y[:, g % R, 1, :, :],
                                      ALU.add).then_inc(paired, 1)
                    dve.wait_ge(paired, g + 1)
                    dve.tensor_tensor(x, x, y[:, g % R, 0, :, :], ALU.add).then_inc(added, 1)

            @block.scalar
            def _(act):
                for g in range(NT // G):
                    act.wait_ge(added, g + 1)
                    act.dma_start(x_out_dram[:, g * G:(g + 1) * G, :],
                                  k.x[:, g * G:(g + 1) * G, :]).then_inc(out_sem, 16)
                act.wait_ge(out_sem, 16 * (NT // G))


def combine_and_log_map(nc, k):
    with Stage(nc, "lm") as s:
        sp_ = s.sb("sp", [P, NT, C])
        junk = s.sb("junk", [P, 2, C])
        R = 4
        y = s.sb("y", [P, R, 2, 4, C])
        std = s.sb("std", [P, NT])
        got, paired, added, x_stored, merged, rooted_var, inverted = (
            s.sems("got", R), s.sem("paired"), s.sem("added"), s.sem("xstored"), s.sem("merged"), s.sem("rootedvar"),
            s.sem("inverted"))
        rows = k.y_d[0:2 * T, :].rearrange("(n t p) c -> p n t c", p=P, n=2)
        s2, y0, a, am, b, d, f = (s.sb(v, [P, NT]) for v in ("s2", "y0", "a", "am", "b", "d", "f"))
        clipped, squared, chain, asked, rooted, grouped = (
            s.sem(v) for v in ("clipped", "squared", "chain", "asked", "rooted", "grouped"))
        G = 4
        stored, grouped_act = s.sem("stored"), s.sem("groupeda")
        with nc.Block() as block:

            @block.vector
            def _(dve):
                ser = Serial(dve, chain)

                def group(ap, g):
                    return ap[:, g * G:(g + 1) * G]

                for g in range(NT // G + 1):
                    if g < NT // G:
                        dve.wait_ge(paired, g + 1)
                        ser(dve.tensor_tensor(group(k.x, g), group(k.x, g), y[:, g % R, 0, :, :], ALU.add))
                        dve.sem_inc(added, 1)
                        for t in range(g * G, (g + 1) * G):
                            ins = dve.bn_stats(k.st6[:, t, :], k.x[:, t, :])
                        ser(ins)
                        for t in range(g * G, (g + 1) * G):
                            ins = dve.bn_aggr(k.mv[:, t, :], k.st6[:, t, :])
                        ser(ins)
                        dve.tensor_scalar(group(std, g), group(k.mv, g)[:, :, 1], LN_EPS, None,
                                          ALU.add).then_inc(merged, 1)
                    if g:
                        dve.wait_ge(rooted_var, g)
                        dve.reciprocal(group(k.rstd, g - 1), group(std, g - 1)).then_inc(inverted, 1)
                        dve.wait_ge(inverted, g)
                        for t in range((g - 1) * G, g * G):
                            ins = dve.tensor_scalar(sp_[:, t, :], k.x[:, t, :], k.mv[:, t, 0:1], k.rstd[:, t:t + 1],
                                                    ALU.subtract, ALU.mult)
                        ser(ins)
                        dve.tensor_scalar(group(sp_, g - 1), group(sp_, g - 1), -8.0, 8.0,
                                          ALU.max, ALU.min).then_inc(clipped, 1)
                dve.wait_ge(squared, NT)
                ser(dve.tensor_scalar(y0[:, :], s2[:, :], 1.0, EPS, ALU.add, ALU.add))
                dve.sem_inc(asked, 1)
                dve.wait_ge(rooted, 1)
                ser(dve.tensor_scalar(a[:, :], y0[:, :], 1.0 + EPS, None, ALU.max))
                ser(dve.tensor_scalar(am[:, :], a[:, :], 1.0, None, ALU.subtract))
                ser(dve.scalar_tensor_tensor(b[:, :], a[:, :], 1.0, am[:, :], ALU.add, ALU.mult))
                ser(dve.tensor_tensor(y0[:, :], y0[:, :], a[:, :], ALU.subtract))
                ser(dve.tensor_tensor(d[:, :], y0[:, :], y0[:, :], ALU.mult))
                ser(dve.tensor_tensor(d[:, :], s2[:, :], d[:, :], ALU.subtract))
                ser(dve.tensor_scalar(d[:, :], d[:, :], EPS, None, ALU.max))
                dve.sem_inc(asked, 1)
                dve.wait_ge(rooted, 3)
                ser(dve.tensor_tensor(a[:, :], a[:, :], b[:, :], ALU.add))
                dve.sem_inc(asked, 1)
                dve.wait_ge(rooted, 4)
                ser(dve.tensor_scalar(a[:, :], a[:, :], 1e-3, None, ALU.max))
                ser(dve.tensor_scalar(d[:, :], d[:, :], EPS, None, ALU.add))
                ser(dve.reciprocal(b[:, :], d[:, :]))
                ser(dve.tensor_tensor(f[:, :], a[:, :], b[:, :], ALU.mult))
                ser(dve.tensor_copy(sp_[:, :, 0], y0[:, :]))
                dve.sem_inc(asked, 1)
                for g in range(NT // G):
                    for t in range(g * G, g * G + G // 2):
                        ins = dve.tensor_scalar(sp_[:, t, :], sp_[:, t, :], f[:, t:t + 1], None, ALU.mult)
                    ins.then_inc(grouped, 1)

            @block.scalar
            def _(act):
                for g in range(NT // G + 1):
                    if g < NT // G:
                        act.wait_ge(merged, g + 1)
                        act.activation(std[:, g * G:(g + 1) * G], std[:, g * G:(g + 1) * G],
                                       ACT.Sqrt).then_inc(rooted_var, 1)
                    if g:
                        act.wait_ge(clipped, g)
                        for t in range((g - 1) * G, g * G):
                            if t >= 2:
                                act.wait_ge(squared, t - 1)
                            act.activation(junk[:, t % 2, 1:C], sp_[:, t, 1:C], ACT.Square,
                                           accum_out=s2[:, t:t + 1]).then_inc(squared, 1)
                act.wait_ge(asked, 1)
                act.activation(y0[:, :], y0[:, :], ACT.Sqrt).then_inc(rooted, 1)
                act.wait_ge(asked, 2)
                act.activation(b[:, :], b[:, :], ACT.Sqrt).then_inc(rooted, 1)
                act.activation(d[:, :], d[:, :], ACT.Sqrt).then_inc(rooted, 1)
                act.wait_ge(asked, 3)
                act.activation(a[:, :], a[:, :], ACT.Ln).then_inc(rooted, 1)
                act.wait_ge(asked, 4)
                for g in range(NT // G):
                    for t in range(g * G + G // 2, (g + 1) * G):
                        ins = act.activation(sp_[:, t, :], sp_[:, t, :], ACT.Copy, scale=f[:, t:t + 1])
                    ins.then_inc(grouped_act, 1)

            @block.gpsimd
            def _(pool):
                for g in range(NT // G):
                    pool.wait_ge(got[g % R], (g // R + 1) * 32)
                    pool.tensor_tensor(y[:, g % R, 0, :, :], y[:, g % R, 0, :, :], y[:, g % R, 1, :, :],
                                       ALU.add).then_inc(paired, 1)

            @block.sync
            def _(sp):
                for g in range(NT // G + 2):
                    if g < NT // G:
                        if g >= R:
                            sp.wait_ge(added, g - R + 1)
                        for n in range(2):
                            sp.dma_start(y[:, g % R, n, :, :],
                                         rows[:, n, g * G:(g + 1) * G, :]).then_inc(got[g % R], 16)
                    if g >= 2:
                        sp.wait_ge(added, g - 1)
                        sp.dma_start(k.x2_t[:, (g - 2) * G:(g - 1) * G, :],
                                     k.x[:, (g - 2) * G:(g - 1) * G, :]).then_inc(x_stored, 16)
                sp.wait_ge(x_stored, 16 * (NT // G))
                for g in range(NT // G):
                    sp.wait_ge(grouped, g + 1)
                    sp.wait_ge(grouped_act, g + 1)
                    sp.dma_start(k.v_t[:, g * G:(g + 1) * G, :], sp_[:, g * G:(g + 1) * G, :]).then_inc(stored, 16)
                sp.wait_ge(stored, 16 * (NT // G))


def stacked_heads(nc, k, b):
    S2 = 6 * D
    HB = H // 2
    R = 4
    with Stage(nc, f"sh{b}") as s:
        v = s.sb("v", [P, R, C])
        vT = s.sb("vT", [P, 2, KC, P])
        qk = s.sb("qk", [P, 2, 2 * H, D])
        sq = s.sb("sq", [P, 2 * H, D])
        root = s.sb("root", [P, 2, 2 * H])
        rest = s.sb("rest", [P, 2, 2 * H, D])
        hm = s.sb("hm", [P, 2, 2 * H, 2, D], BF16)
        stq, stk = s.sb("stq", [P, 2, H, P], BF16), s.sb("stk", [P, 2, H, P], BF16)
        psT = s.ps("psT", [P, BANK])
        psQK = s.ps("psQK", [P, 2, BANK])
        psV = s.ps("psV", [P, BANK])
        psS = s.ps("psS", [P, 4, 2 * BANK], BF16)
        (start, turned, vT_out, qk_ready, v_ready, v_out, clipped, squared, summed, rooted, led, high, left, middle,
         low, stacked, pool_stacked, st_turned, evac_dve, evac_act) = (
            s.sem(n) for n in ("start", "turned", "vTout", "qk", "vr", "vout", "clipped", "squared", "summed", "rooted",
                               "led", "high", "left", "middle", "low", "stacked", "pstacked", "stturned", "evacd",
                               "evaca"))
        got = s.sems("got", R)
        passed = s.sem("passed")

        def section(buf, j, a):
            return buf[:, j, :, a * D:(a + 1) * D]

        def evacuate(eng, copy, st, n, half, sem):
            t, dst = st.tile(4), (k.QT, k.KT)[n]
            eng.wait_ge(st_turned, t * 4 + n * 2 + half + 2)
            copy(dst[:, half * HB:(half + 1) * HB, ds(t * P, P)],
                 psS[:, n * 2 + half, :].rearrange("p (h t) -> p h t", h=HB)).then_inc(sem, 1)

        with nc.Block() as block:

            @block.sync
            def _(sp):
                for st in steps(sp, TB, R, 0):
                    t, j = st.tile(), st.slot(0, R)
                    st.again(sp, turned, t - R + 1)
                    sp.dma_start(v[:, j, :], tile(k.v_t, b * TB + t)).then_inc(got[j], 16)

            @block.gpsimd
            def _(pool):
                pool.memset(stq[:, :, :, S2:P], 0.0).then_inc(start, 1)
                pool.memset(stk[:, :, :, S2 + 3:P], 0.0).then_inc(start, 1)
                pool.memset(stk[:, :, :, S2:S2 + 3], 1.0).then_inc(start, 1)
                for st in steps(pool, TB, 4, 3):
                    if st.on(3):
                        t, j = st.tile(3), st.slot(3, 2)
                        pool.wait_ge(high, t + 1)
                        st.again(pool, st_turned, t * 4 - 3)
                        pool.sem_inc(passed, 1)
                        pool.tensor_copy(section(stk, j, 5), hm[:, j, H:2 * H, 0, :]).then_inc(pool_stacked, 1)

            @block.tensor
            def _(pe):
                pe.wait_ge(start, 3)
                pe.sem_inc(st_turned, 1)
                for st in steps(pe, TB, 4, 4):
                    if st.on(0):
                        t, j = st.tile(), st.slot(0, R)
                        pe.wait_ge(got[j], st.lap(0, R) * 16 + 16)
                        st.again(pe, vT_out, t)
                        for kk in range(KC):
                            mm = pe.transpose(psT[:, kk * P:(kk + 1) * P], v[:, j, kk * P:(kk + 1) * P], k.ident[:, :])
                        mm.then_inc(turned, 1)
                    if st.on(1):
                        t, j = st.tile(1), st.slot(1, 2)
                        pe.wait_ge(vT_out, t + 1)
                        st.again(pe, clipped, t - 1)
                        for kk in range(KC):
                            mm = pe.matmul(psQK[:, j, :], vT[:, j, kk, :], k.w1qkv[:, kk, 0:2 * C],
                                           start=(kk == 0), stop=(kk == KC - 1))
                        mm.then_inc(qk_ready, 1)
                        st.again(pe, v_out, t)
                        for kk in range(KC):
                            mm = pe.matmul(psV[:, 0:C], vT[:, j, kk, :], k.w1qkv[:, kk, 2 * C:3 * C],
                                           start=(kk == 0), stop=(kk == KC - 1))
                        mm.then_inc(v_ready, 1)
                    if st.on(4):
                        t, j = st.tile(4), st.slot(4, 2)
                        pe.wait_ge(stacked, t + 1)
                        pe.wait_ge(low, t + 1)
                        pe.wait_ge(pool_stacked, t + 1)
                        for n, stk_ in enumerate((stq, stk)):
                            for half in range(2):
                                pe.wait_ge(evac_dve if half == 0 else evac_act, t * 2 + 1 + n)
                                for hh in range(HB):
                                    mm = pe.transpose(psS[:, n * 2 + half, hh * P:(hh + 1) * P],
                                                      stk_[:, j, half * HB + hh, :], k.identb[:, :])
                                mm.then_inc(st_turned, 1)

            @block.vector
            def _(dve):
                dve.sem_inc(evac_dve, 2)
                for st in steps(dve, TB, 4, 4):
                    if st.on(1):
                        t, j = st.tile(1), st.slot(1, 2)
                        dve.wait_ge(qk_ready, t + 1)
                        dve.tensor_scalar(qk[:, j, :, :].rearrange("p h d -> p (h d)"), psQK[:, j, :], -5.0, 5.0,
                                          ALU.max, ALU.min).then_inc(clipped, 1)
                    if st.on(2):
                        t, j = st.tile(2), st.slot(2, 2)
                        dve.wait_ge(rooted, t + 1)
                        dve.tensor_scalar(qk[:, j, 0:H, 0], root[:, j, 0:H], -1.0, None, ALU.mult)
                        dve.tensor_copy(qk[:, j, H:2 * H, 0], root[:, j, H:2 * H]).then_inc(led, 1)
                    if st.on(4):
                        evacuate(dve, dve.tensor_copy, st, 0, 0, evac_dve)
                    if st.on(3):
                        t, j = st.tile(3), st.slot(3, 2)
                        dve.wait_ge(middle, t + 1)
                        st.again(dve, st_turned, t * 4 - 3)
                        dve.tensor_tensor(section(stq, j, 5), rest[:, j, 0:H, :], hm[:, j, 0:H, 1, :], ALU.subtract)
                        dve.tensor_tensor(section(stk, j, 2), rest[:, j, H:2 * H, :], hm[:, j, H:2 * H, 1, :],
                                          ALU.subtract).then_inc(low, 1)
                    if st.on(2):
                        t, j = st.tile(2), st.slot(2, 2)
                        dve.wait_ge(led, t + 1)
                        st.again(dve, stacked, t - 1)
                        st.again(dve, pool_stacked, t - 1)
                        dve.tensor_copy(hm[:, j, :, 0, :], qk[:, j, :, :]).then_inc(high, 1)
                    if st.on(4):
                        evacuate(dve, dve.tensor_copy, st, 1, 0, evac_dve)
                    if st.on(2):
                        dve.wait_ge(high, t + 1)
                        dve.tensor_tensor(rest[:, j, :, :], qk[:, j, :, :], hm[:, j, :, 0, :],
                                          ALU.subtract).then_inc(left, 1)
                    if st.on(1):
                        u, i = st.tile(1), st.slot(1, 2)
                        dve.wait_ge(squared, u + 1)
                        dve.tensor_reduce(root[:, i, :], sq[:, :, 1:D], AX.X, ALU.add).then_inc(summed, 1)
                    if st.on(2):
                        dve.wait_ge(left, t + 1)
                        dve.tensor_copy(hm[:, j, :, 1, :], rest[:, j, :, :]).then_inc(middle, 1)
                    if st.on(1):
                        dve.wait_ge(summed, u * 2 + 1)
                        dve.tensor_scalar(root[:, i, :], root[:, i, :], 1.0, EPS, ALU.add, ALU.add).then_inc(summed, 1)

            @block.scalar
            def _(act):
                def copy(o, i):
                    return act.activation(o, i, ACT.Copy)

                act.wait_ge(start, 3)
                act.sem_inc(evac_act, 2)
                for st in steps(act, TB, 4, 4):
                    if st.on(0):
                        t, j = st.tile(), st.slot(0, 2)
                        act.wait_ge(turned, t + 1)
                        st.again(act, v_ready, t - 1)
                        copy(vT[:, j, :, :], psT[:, 0:C].rearrange("p (k c) -> p k c", k=KC)).then_inc(vT_out, 1)
                    if st.on(2):
                        t, j = st.tile(2), st.slot(2, 2)
                        act.wait_ge(summed, t * 2 + 2)
                        act.activation(root[:, j, :], root[:, j, :], ACT.Sqrt).then_inc(rooted, 1)
                    if st.on(1):
                        t, j = st.tile(1), st.slot(1, 2)
                        act.wait_ge(clipped, t + 1)
                        st.again(act, summed, t * 2)
                        act.activation(sq[:, :, :], qk[:, j, :, :], ACT.Square).then_inc(squared, 1)
                    if st.on(4):
                        evacuate(act, copy, st, 0, 1, evac_act)
                    if st.on(1):
                        act.wait_ge(v_ready, t + 1)
                        copy(tile(k.V, t), psV[:, 0:C]).then_inc(v_out, 1)
                    if st.on(3):
                        t, j = st.tile(3), st.slot(3, 2)
                        act.wait_ge(middle, t + 1)
                        st.again(act, st_turned, t * 4 - 3)
                        q, kk = hm[:, j, 0:H, :, :], hm[:, j, H:2 * H, :, :]
                        copy(stq[:, j, :, 0:3 * D].rearrange("p h (s d) -> p h s d", d=D),
                             q[:, :, 0:1, :].to_broadcast([P, H, 3, D]))
                        copy(stq[:, j, :, 3 * D:5 * D].rearrange("p h (s d) -> p h s d", d=D),
                             q[:, :, 1:2, :].to_broadcast([P, H, 2, D]))
                        copy(stk[:, j, :, 0:6 * D].rearrange("p h (r s) -> p h r s", r=2)[:, :, :, 0:2 * D],
                             kk.rearrange("p h s d -> p h (s d)").unsqueeze(2).to_broadcast([P, H, 2, 2 * D])
                             ).then_inc(stacked, 1)
                    if st.on(4):
                        evacuate(act, copy, st, 1, 1, evac_act)


def attention(nc, k, b):
    KT16 = TB
    QC = TS // BANK
    GM = 4
    UN = 2 * BANK
    VW = 32
    SPREAD = 12
    with Stage(nc, f"at{b}") as s:
        pexp = s.sb("pexp", [P, 4, UN])
        vst = s.sb("vst", [P, 2, KT16, VW])
        ksumT = s.sb("ksumT", [P, 2, TS // GM], BF16)
        mx = s.sb("mx", [P, KT16])
        sa, sb_ = s.sb("sa", [P, KT16]), s.sb("sb", [P, KT16])
        shift = s.sb("shift", [P, KT16, 3], BF16)
        oT = s.sb("oT", [P, BANK])
        inv = s.sb("inv", [P, QC, QC])
        psS = s.ps("psS", [P, 2, UN])
        psO = s.ps("psO", [P, BANK])
        psM = s.ps("psM", [P, 2, BANK])
        psX = s.ps("psX", [P, BANK])
        (scored, raised, weighed, v_ready, o_out, maxed, reduced, k_ready, q_ready, shifted, x_turned, x_free,
         chain, divided, start) = (
            s.sem(n) for n in ("scored", "raised", "weighed", "vready", "oout", "maxed", "reduced", "kready",
                               "qready", "shifted", "xturned", "xfree", "chain", "divided", "start"))

        def shift_use(h, half):
            return 1 + half if isinstance(h, int) and h == 0 else h * 3 + half

        with nc.Block() as block:

            def head_of(ap, h):
                return ap[:, ds(h, 1), :].rearrange("p a t -> p (a t)")

            @block.gpsimd
            def _(pool):
                def take_v(h, j):
                    pool.tensor_copy(vst[:, j, :, 0:D], k.V[:, :, ds(h * D, D)]).then_inc(v_ready, 1)

                pool.memset(vst[:, :, :, :], 0.0).then_inc(start, 1)
                pool.wait_ge(start, 1)
                pool.memset(vst[:, :, :, D:D + 1], 1.0).then_inc(start, 1)
                pool.wait_ge(start, 2)
                take_v(0, 0)
                take_v(1, 1)
                with pool.Fori(0, H // 2 - 1) as i:
                    for j in range(2):
                        pool.wait_ge(weighed, (i * 2 + j + 1) * KT16 * 2 + 4)
                        take_v(i * 2 + j + 2, j)

            @block.tensor
            def _(pe):
                def scores(h, kt, u2):
                    u = h * 2 * KT16 + kt * 2 + u2
                    pe.wait_ge(raised, u + 1)
                    for c in range(2):
                        mm = pe.matmul(psS[:, u2, c * BANK:(c + 1) * BANK],
                                       k.KT[:, ds(h, 1), kt * P:(kt + 1) * P].rearrange("p a t -> p (a t)"),
                                       k.QT[:, ds(h, 1), u2 * UN + c * BANK:u2 * UN + (c + 1) * BANK].rearrange(
                                           "p a t -> p (a t)"), start=True, stop=True)
                    mm.then_inc(scored, 1)

                def weigh(h, j, kt, u2):
                    pe.wait_ge(raised, h * 2 * KT16 + kt * 2 + u2 + 3)
                    if kt == 0 and u2 == 0:
                        if not isinstance(h, int) or h:
                            pe.wait_ge(o_out, h)
                        pe.wait_ge(v_ready, h + 1)
                    for c in range(2 * u2, 2 * u2 + 2):
                        mm = pe.matmul(psO[c * VW:(c + 1) * VW, :], vst[:, j, kt, :],
                                       pexp[:, (kt % 2) * 2 + u2, (c % 2) * BANK:(c % 2 + 1) * BANK],
                                       start=(kt == 0), stop=(kt == KT16 - 1))
                    mm.then_inc(weighed, 1)

                def means(h, j, n):
                    if n == 0:
                        pe.wait_ge(k_ready, h + 1)
                    pe.wait_ge(reduced, h * KT16 + n + 1)
                    pe.matmul(psM[:, n % 2, :],
                              k.QT[:, ds(h, 1), n * P:(n + 1) * P].rearrange("p a t -> p (a t)"),
                              ksumT[:, j, :], start=True, stop=True).then_inc(maxed, 1)

                def turn_shift(h, half):
                    if half == 0:
                        pe.wait_ge(shifted, h + 1)
                    pe.wait_ge(x_free, shift_use(h, half) - 1)
                    view = psX[:, :].bitcast(BF16)
                    for n in range(KT16 // 2):
                        mm = pe.transpose(view[6 * D:6 * D + 3, n * P:(n + 1) * P],
                                          shift[:, half * (KT16 // 2) + n, :], k.identb[:, :])
                    mm.then_inc(x_turned, 1)

                def turn_out(h):
                    pe.wait_ge(o_out, h + 1)
                    pe.wait_ge(x_free, h * 3 + 4)
                    for c in range(QC):
                        mm = pe.transpose(psX[:, c * P:(c + 1) * P], oT[:, c * P:(c + 1) * P], k.ident[:, :])
                    mm.then_inc(x_turned, 1)

                def head(h, j, first=False, last=False):
                    pe.wait_ge(q_ready, h + 1)
                    n = 0
                    for kt in range(KT16):
                        for u2 in range(2):
                            scores(h, kt, u2)
                            if kt:
                                weigh(h, j, kt - 1, u2)
                            elif not first:
                                weigh(h - 1, 1 - j, KT16 - 1, u2)
                        if kt < SPREAD and not last:
                            for _ in range(2 if kt % 3 == 0 else 1):
                                means(h + 1, 1 - j, n)
                                n += 1
                        if kt == 2 and not first:
                            turn_out(h - 1)
                        if kt in (SPREAD + 1, SPREAD + 2) and not last:
                            turn_shift(h + 1, kt - SPREAD - 1)
                    assert last or n == KT16

                pe.wait_ge(start, 2)
                for n in range(KT16):
                    means(0, 0, n)
                for half in range(2):
                    turn_shift(0, half)
                head(0, 0, first=True)
                with pe.Fori(0, H // 2 - 1) as i:
                    head(i * 2 + 1, 1)
                    head(i * 2 + 2, 0)
                head(H - 1, 1, last=True)
                for u2 in range(2):
                    weigh(H - 1, 1, KT16 - 1, u2)
                pe.wait_ge(o_out, H)
                pe.wait_ge(x_free, 3 * H - 1)
                for c in range(QC):
                    mm = pe.transpose(psX[:, c * P:(c + 1) * P], oT[:, c * P:(c + 1) * P], k.ident[:, :])
                mm.then_inc(x_turned, 1)

            @block.scalar
            def _(act):
                act.sem_inc(raised, 2)
                with act.Fori(0, H // 2) as i:
                    for n in range(4 * KT16):
                        h, u = i * 2 + n // (2 * KT16), n % (2 * KT16)
                        act.wait_ge(scored, h * 2 * KT16 + u + 1)
                        act.wait_ge(weighed, h * 2 * KT16 + u + 1)
                        act.activation(pexp[:, u % 4, :], psS[:, u % 2, :], ACT.Exp,
                                       scale=D ** -0.5).then_inc(raised, 1)

            @block.vector
            def _(dve):
                dve.sem_inc(weighed, 4)
                dve.sem_inc(reduced, 2)

                def sum_keys(h, j):
                    with nc.allow_low_precision(reason="the shift need not be exact"):
                        dve.tensor_reduce(ksumT[:, j, :], head_of(k.KT, h).rearrange("p (g m) -> p g m", m=GM),
                                          AX.X, ALU.add).then_inc(k_ready, 1)

                def reduce(h, n):
                    dve.wait_ge(maxed, h * KT16 + n + 1)
                    dve.tensor_reduce(mx[:, n:n + 1], psM[:, n % 2, :], AX.X, ALU.max).then_inc(reduced, 1)

                def step(h, n, ins):
                    ins.then_inc(chain, 1)
                    dve.wait_ge(chain, h * 7 + n + 1)

                def make_shift(h):
                    dve.wait_ge(reduced, h * KT16 + KT16 + 2)
                    step(h, 0, dve.tensor_scalar(sa[:, :], mx[:, :], 0.25, 280.0, ALU.mult, ALU.add))
                    step(h, 1, dve.tensor_scalar(sa[:, :], sa[:, :], -280.0, None, ALU.min))
                    step(h, 2, dve.scalar_tensor_tensor(sb_[:, :], mx[:, :], 0.25, sa[:, :], ALU.mult, ALU.max))
                    step(h, 3, dve.tensor_scalar(sb_[:, :], sb_[:, :], -1.0, None, ALU.mult))
                    step(h, 4, dve.tensor_copy(shift[:, :, 0], sb_[:, :]))
                    step(h, 5, dve.tensor_tensor(sa[:, :], sb_[:, :], shift[:, :, 0], ALU.subtract))
                    step(h, 6, dve.tensor_copy(shift[:, :, 1], sa[:, :]))
                    dve.tensor_tensor(shift[:, :, 2], sa[:, :], shift[:, :, 1], ALU.subtract).then_inc(shifted, 1)

                def put_shift(h, half):
                    dve.wait_ge(x_turned, shift_use(h, half))
                    ins = dve.tensor_copy(
                        k.QT[6 * D:6 * D + 3, ds(h, 1), half * UN:(half + 1) * UN].rearrange("p a t -> p (a t)"),
                        psX[:, :].bitcast(BF16)[6 * D:6 * D + 3, :])
                    ins.then_inc(x_free, 1)
                    if half == 1:
                        dve.wait_ge(x_free, shift_use(h, 1))
                        dve.sem_inc(q_ready, 1)

                def take_out(h):
                    dve.wait_ge(weighed, (h + 1) * KT16 * 2 + 4)
                    dve.wait_ge(x_turned, h * 3 + 2)
                    dve.tensor_copy(oT[:, :], psO[:, :]).then_inc(o_out, 1)

                def divide(h, count):
                    dve.wait_ge(x_turned, count)
                    o = psX[:, :].rearrange("p (c j d) -> p c j d", c=QC, j=QC)
                    dve.reciprocal(inv[:, :, :], o[:, :, :, D]).then_inc(divided, 1)
                    dve.wait_ge(divided, h + 1)
                    dve.tensor_tensor(k.O[:, :, ds(h * D, D)].rearrange("p (j c) d -> p c j d", j=QC),
                                      o[:, :, :, 0:D], inv[:, :, :].unsqueeze(3).to_broadcast([P, QC, QC, D]),
                                      ALU.mult).then_inc(x_free, 1)

                def head(h, first=False, last=False):
                    if not first:
                        take_out(h - 1)
                    for n in range(6):
                        if not last:
                            reduce(h + 1, n)
                    if not first:
                        divide(h - 1, h * 3 + 2)
                    if last:
                        return
                    for n in range(6, KT16):
                        reduce(h + 1, n)
                    make_shift(h + 1)
                    put_shift(h + 1, 0)
                    put_shift(h + 1, 1)

                sum_keys(0, 0)
                for n in range(KT16):
                    reduce(0, n)
                make_shift(0)
                put_shift(0, 0)
                put_shift(0, 1)
                sum_keys(1, 1)
                head(0, first=True)
                sum_keys(2, 0)
                with dve.Fori(0, H // 2 - 2) as i:
                    head(i * 2 + 1)
                    sum_keys(i * 2 + 3, 1)
                    head(i * 2 + 2)
                    sum_keys(i * 2 + 4, 0)
                head(H - 3)
                sum_keys(H - 1, 1)
                head(H - 2)
                head(H - 1, last=True)
                take_out(H - 1)
                divide(H - 1, 3 * H)


def attention_out(nc, k, b, u, x3_out, meanwhile=None):
    G = 4
    NG, NPR = TB // G, TB // 2
    with Stage(nc, f"ao{b}") as s:
        x2 = s.sb("x2", [P, 2, G, C])
        oT = s.sb("oT", [P, 2, KC, 2, P])
        junk = s.sb("junk", [P, C])
        s2, vn, e1, e2, t2, pl, sm, g = (s.sb(v, [P, TB]) for v in ("s2", "vn", "e1", "e2", "t2", "pl", "sm", "g"))
        psT = s.ps("psT", [P, 2, BANK])
        psU = s.ps("psU", [P, 3, 2 * C])
        (turned, oT_out, u_ready, u_out, squared, chain, asked, done_act, scaled, clipped, led, added, x3_stored) = (
            s.sem(v) for v in ("turned", "oTout", "uready", "uout", "squared", "chain", "asked", "doneact", "scaled",
                               "clipped", "led", "added", "x3stored"))
        x2_in = s.sems("x2in", 2)
        with nc.Block() as block:

            @block.sync
            def _(sp):
                for n in range(NG):
                    if n == 2 and meanwhile:
                        meanwhile(sp)
                    if n >= 2:
                        sp.wait_ge(added, n - 1)
                    sp.dma_start(x2[:, n % 2, :, :], k.x2_t[:, b * TB + n * G:b * TB + (n + 1) * G, :]).then_inc(
                        x2_in[n % 2], 16)
                if x3_out is not None:
                    for n in range(NG):
                        sp.wait_ge(added, n + 1)
                        sp.dma_start(x3_out[:, n * G:(n + 1) * G, :],
                                     u[:, n * G:(n + 1) * G, :]).then_inc(x3_stored, 16)
                    sp.wait_ge(x3_stored, 16 * NG)

            @block.tensor
            def _(pe):
                for n in range(NPR + 1):
                    if n < NPR:
                        if n >= 2:
                            pe.wait_ge(oT_out, n - 1)
                        for kk in range(KC):
                            for q in range(2):
                                mm = pe.transpose(psT[:, n % 2, (kk * 2 + q) * P:(kk * 2 + q + 1) * P],
                                                  k.O[:, 2 * n + q, kk * P:(kk + 1) * P], k.ident[:, :])
                        mm.then_inc(turned, 1)
                    if n:
                        m = n - 1
                        pe.wait_ge(oT_out, m + 1)
                        if m >= 3:
                            pe.wait_ge(u_out, m - 2)
                        for q in range(2):
                            for kk in range(KC):
                                mm = pe.matmul(psU[:, m % 3, q * C:(q + 1) * C], oT[:, m % 2, kk, q, :],
                                               k.w1o[:, kk, :], start=(kk == 0), stop=(kk == KC - 1))
                        mm.then_inc(u_ready, 1)

            @block.vector
            def _(dve):
                ser = Serial(dve, chain)
                for n in range(NPR):
                    dve.wait_ge(u_ready, n + 1)
                    dve.tensor_copy(u[:, 2 * n:2 * n + 2, :],
                                    psU[:, n % 3, :].rearrange("p (t c) -> p t c", c=C)).then_inc(u_out, 1)
                dve.wait_ge(squared, TB)
                ser(dve.tensor_scalar(vn[:, :], s2[:, :], 0.0, EPS, ALU.max, ALU.add))
                dve.sem_inc(asked, 1)
                dve.wait_ge(done_act, 1)
                ser(dve.tensor_scalar(vn[:, :], vn[:, :], 5.0, None, ALU.min))
                dve.sem_inc(asked, 1)
                ser(dve.tensor_tensor(t2[:, :], vn[:, :], vn[:, :], ALU.mult))
                ser(dve.tensor_scalar(pl[:, :], t2[:, :], 1.0 / 42.0, 1.0, ALU.mult, ALU.add))
                ser(dve.scalar_tensor_tensor(pl[:, :], t2[:, :], 1.0 / 20.0, pl[:, :], ALU.mult, ALU.mult))
                ser(dve.tensor_scalar(pl[:, :], pl[:, :], 1.0, None, ALU.add))
                ser(dve.scalar_tensor_tensor(pl[:, :], t2[:, :], 1.0 / 6.0, pl[:, :], ALU.mult, ALU.mult))
                ser(dve.tensor_scalar(pl[:, :], pl[:, :], 1.0, None, ALU.add))
                ser(dve.tensor_tensor(pl[:, :], pl[:, :], vn[:, :], ALU.mult))
                ser(dve.tensor_scalar(sm[:, :], vn[:, :], 0.5, None, ALU.is_lt))
                dve.wait_ge(done_act, 3)
                ser(dve.tensor_tensor(e1[:, :], e1[:, :], e2[:, :], ALU.subtract))
                ser(dve.tensor_scalar(e1[:, :], e1[:, :], 0.5, None, ALU.mult))
                ser(dve.tensor_tensor(pl[:, :], pl[:, :], e1[:, :], ALU.subtract))
                ser(dve.tensor_tensor(pl[:, :], pl[:, :], sm[:, :], ALU.mult))
                ser(dve.tensor_tensor(e1[:, :], e1[:, :], pl[:, :], ALU.add))
                ser(dve.tensor_scalar(t2[:, :], vn[:, :], EPS, None, ALU.add))
                ser(dve.reciprocal(e2[:, :], t2[:, :]))
                ser(dve.tensor_tensor(g[:, :], e1[:, :], e2[:, :], ALU.mult))
                dve.sem_inc(asked, 1)
                for n in range(NG):
                    part = u[:, n * G:(n + 1) * G, :]
                    dve.wait_ge(scaled, (n + 1) * G)
                    dve.tensor_scalar(part, part, -8.0, 8.0, ALU.max, ALU.min).then_inc(clipped, 1)
                dve.wait_ge(squared, 2 * TB)
                ser(dve.tensor_scalar(s2[:, :], s2[:, :], 1.0, EPS, ALU.add, ALU.add))
                dve.sem_inc(asked, 1)
                dve.wait_ge(done_act, 4)
                dve.tensor_copy(u[:, :, 0], s2[:, :]).then_inc(led, 1)
                dve.wait_ge(led, 1)
                for n in range(NG):
                    part = u[:, n * G:(n + 1) * G, :]
                    dve.wait_ge(x2_in[n % 2], (n // 2 + 1) * 16)
                    dve.tensor_tensor(part, part, x2[:, n % 2, :, :], ALU.add).then_inc(added, 1)
                    dve.wait_ge(added, n + 1)
                    for t in range(n * G, (n + 1) * G):
                        dve.bn_stats(k.st6[:, b * TB + t, :], u[:, t, :])

            @block.scalar
            def _(act):
                for n in range(NPR + 1):
                    if n < NPR:
                        act.wait_ge(turned, n + 1)
                        if n >= 2:
                            act.wait_ge(u_ready, n - 1)
                        act.activation(oT[:, n % 2, :, :, :].rearrange("p k q c -> p (k q c)"), psT[:, n % 2, :],
                                       ACT.Copy).then_inc(oT_out, 1)
                    if n:
                        m = n - 1
                        act.wait_ge(u_out, m + 1)
                        for q in range(2):
                            if m or q:
                                act.wait_ge(squared, 2 * m + q)
                            act.activation(junk[:, 1:C], u[:, 2 * m + q, 1:C], ACT.Square,
                                           accum_out=s2[:, 2 * m + q:2 * m + q + 1]).then_inc(squared, 1)
                act.wait_ge(asked, 1)
                act.activation(vn[:, :], vn[:, :], ACT.Sqrt).then_inc(done_act, 1)
                act.wait_ge(asked, 2)
                act.activation(e1[:, :], vn[:, :], ACT.Exp).then_inc(done_act, 1)
                act.activation(e2[:, :], vn[:, :], ACT.Exp, scale=-1.0).then_inc(done_act, 1)
                act.wait_ge(asked, 3)
                act.wait_ge(u_out, NPR)

                def scale(n):
                    for t in range(n * G, (n + 1) * G):
                        act.activation(u[:, t, :], u[:, t, :], ACT.Copy, scale=g[:, t:t + 1]).then_inc(scaled, 1)

                scale(0)
                for n in range(NG):
                    if n + 1 < NG:
                        scale(n + 1)
                    act.wait_ge(clipped, n + 1)
                    for t in range(n * G, (n + 1) * G):
                        act.wait_ge(squared, TB + t)
                        act.activation(junk[:, 1:C], u[:, t, 1:C], ACT.Square,
                                       accum_out=s2[:, t:t + 1]).then_inc(squared, 1)
                act.wait_ge(asked, 4)
                act.activation(s2[:, :], s2[:, :], ACT.Sqrt).then_inc(done_act, 1)


def load_experts(sp, k, a, experts):
    for e in experts:
        for n, w in enumerate(("L1_ffn_Wg", "L1_ffn_W1")):
            sp.dma_start(k.wgu[:, e, :, n, :], a[w][e, :, :].rearrange("(k p) c -> p k c", p=P)).then_inc(k.w_in[e], 16)
        sp.dma_start(k.w2b[0:HP, e, :, :],
                     a["L1_ffn_W2"][e, :, :].rearrange("(n p) c -> p n c", p=HP)).then_inc(k.w_in[e], 16)
        sp.dma_start(k.w2b[HP:HP + 1, e, HK - 1, :], a["L1_ffn_b2"][e:e + 1, :]).then_inc(k.w_in[e], 16)


def prepare_biases(nc, k, a):
    with Stage(nc, "lw") as s:
        cleared, b_in = s.sem("cleared"), s.sem("bin")
        picked, chain = s.sem("picked"), s.sem("chain")
        raw = s.sb("raw", [P, HG, 2, HW])
        part = s.sb("part", [P, 2, HG * 2 * HW], BF16)
        with nc.Block() as block:

            @block.sync
            def _(sp):
                sp.wait_ge(cleared, 1)
                for q in range(3):
                    for n, w in enumerate(("L1_ffn_bg", "L1_ffn_b1")):
                        sp.dma_start(raw[32 * q:32 * q + E, :, n, :],
                                     a[w].rearrange("e (g c) -> e g c", g=HG)).then_inc(b_in, 16)

            @block.gpsimd
            def _(pool):
                pool.memset(k.pick[:, :, :], 0.0).then_inc(picked, 1)
                pool.wait_ge(picked, 1)
                for q in range(3):
                    pool.affine_select(out=k.pick[32 * q:32 * (q + 1), :, :], in_=k.pick[32 * q:32 * (q + 1), :, :],
                                       compare_op=ALU.not_equal, fill=1.0, base=0, pattern=[[-1, E], [0, P]],
                                       channel_multiplier=1).then_inc(picked, 1)

            @block.vector
            def _(dve):
                ser = Serial(dve, chain)
                dve.memset(raw[:, :, :, :], 0.0).then_inc(cleared, 1)
                ser(dve.memset(k.bias[:, :], 0.0))
                dve.wait_ge(b_in, 16 * 6)
                flat = raw[:, :, :, :].rearrange("p g n c -> p (g n c)")
                ser(dve.tensor_copy(part[:, 0, :], flat))
                ser(dve.tensor_copy(k.bias[0:32, :], part[0:32, 0, :]))
                ser(dve.tensor_tensor(flat, flat, part[:, 0, :], ALU.subtract))
                ser(dve.tensor_copy(part[:, 1, :], flat))
                ser(dve.tensor_copy(k.bias[32:64, :], part[32:64, 1, :]))
                ser(dve.tensor_tensor(k.bias[64:96, :], flat[64:96, :], part[64:96, 1, :], ALU.subtract))


def experts1(nc, k):
    G2 = 2 * HW
    with Stage(nc, "ex1") as s:
        idx, odx = s.sb("idx", [P, GR, 1], U32), s.sb("odx", [P, 2, 1], U32)
        xg = s.sb("xg", [P, GR, C])
        xT = s.sb("xT", [P, 2, KC, P])
        sg = s.sb("sg", [P, HG, HW])
        h = s.sb("h", [P, 2, HG, HW])
        hT = s.sb("hT", [P, 2, HK, P])
        y = s.sb("y", [P, 2, C])
        psX = s.ps("psX", [P, 2, BANK])
        psH = s.ps("psH", [P, HG, BANK])
        psG = s.ps("psG", [P, 2, BANK])
        psY = s.ps("psY", [P, BANK])
        HB = HK // 2
        (x_turned, x_out, h_ready, gated, h_done, h_turned, hl_out, hr_out, y_ready,
         y_done, start) = (
            s.sem(v) for v in ("xturned", "xout", "hready", "gated", "hdone", "hturned", "hlout", "hrout", "yready",
                               "ydone", "start"))
        got, put = s.sems("got", GR), s.sems("put", 2)
        indexed, passed = s.sem("indexed"), s.sem("passed")
        with nc.Block() as block:

            @block.gpsimd
            def _(pool):
                slot_transfers(pool, k, idx, odx, xg, y, got, put, x_turned, y_done, indexed, passed)

            @block.tensor
            def _(pe):
                for e in range(E):
                    pe.wait_ge(k.w_in[e], 16 * 4)
                pe.wait_ge(start, 2)
                for st in steps(pe, NTILE, 4, 3):
                    if st.on(0):
                        t, g, j = st.tile(0), st.slot(0, GR), st.slot(0, 2)
                        pe.wait_ge(got[g], st.lap(0, GR) * 16 + 16)
                        st.again(pe, x_out, t - 1)
                        for kk in range(KC):
                            mm = pe.transpose(psX[:, j, kk * P:(kk + 1) * P], xg[:, g, kk * P:(kk + 1) * P],
                                              k.ident[:, :])
                        mm.then_inc(x_turned, 1)
                    if st.on(1):
                        t, j = st.tile(1), st.slot(1, 2)
                        e = pe.value_load(k.tile_expert[0:1, ds(t, 1)], min_val=0, max_val=E - 1)
                        pe.wait_ge(x_out, t + 1)
                        for n in range(HG):
                            st.again(pe, h_done, t * HG - HG + n + 1)
                            pe.matmul(psH[:, n, 0:G2], k.pick[:, ds(e, 1), :].rearrange("p a c -> p (a c)"),
                                      k.bias[:, n * G2:(n + 1) * G2], start=True, stop=False)
                            for kk in range(KC):
                                mm = pe.matmul(psH[:, n, 0:G2].rearrange("p (n c) -> p n c", n=2), xT[:, j, kk, :],
                                               k.wgu[:, ds(e, 1), kk, :, n * HW:(n + 1) * HW].rearrange(
                                                   "p a n c -> p (a n) c"), start=False, stop=(kk == KC - 1))
                            mm.then_inc(h_ready, 1)
                    if st.on(2):
                        t, j = st.tile(2), st.slot(2, 2)
                        pe.wait_ge(h_done, t * HG + HG)
                        for n, out in enumerate((hl_out, hr_out)):
                            st.again(pe, out, t)
                            for m in range(HB):
                                g = n * HB + m
                                mm = pe.transpose(psG[0:HP, n, m * P:(m + 1) * P],
                                                  h[:, j, g // 2, (g % 2) * HP:(g % 2 + 1) * HP], k.ident[:, :])
                            mm.then_inc(h_turned, 1)
                    if st.on(3):
                        t, j = st.tile(3), st.slot(3, 2)
                        e = pe.value_load(k.tile_expert[0:1, ds(t, 1)], min_val=0, max_val=E - 1)
                        st.again(pe, y_done, t)
                        for g in range(HK):
                            if g % HB == 0:
                                pe.wait_ge((hl_out, hr_out)[g // HB], t + 1)
                            rows = HP + (g == HK - 1)
                            mm = pe.matmul(psY[:, 0:C], hT[0:rows, j, g, :],
                                           k.w2b[0:rows, ds(e, 1), g, :].rearrange("p a c -> p (a c)"),
                                           start=(g == 0), stop=(g == HK - 1))
                        mm.then_inc(y_ready, 1)

            @block.scalar
            def _(act):
                for st in steps(act, NTILE, 8, 2):
                    if st.on(0):
                        t, j = st.tile(0), st.slot(0, 2)
                        act.wait_ge(x_turned, t + 1)
                        st.again(act, h_ready, (t - 1) * HG)
                        act.activation(xT[:, j, :, :], psX[:, j, 0:C].rearrange("p (k c) -> p k c", k=KC),
                                       ACT.Copy).then_inc(x_out, 1)
                    if st.on(1):
                        t = st.tile(1)
                        for n in range(HG):
                            act.wait_ge(h_ready, t * HG + n + 1)
                            st.again(act, h_done, t * HG - HG + n + 1)
                            act.activation(sg[:, n, :], psH[:, n, 0:HW], ACT.Silu).then_inc(gated, 1)
                    if st.on(2):
                        t, j = st.tile(2), st.slot(2, 2)
                        act.wait_ge(h_turned, t * 2 + 2)
                        st.again(act, y_ready, t - 1)
                        act.activation(hT[0:HP, j, HB:HK, :],
                                       psG[0:HP, 1, 0:HB * P].rearrange("p (k c) -> p k c", k=HB),
                                       ACT.Copy).then_inc(hr_out, 1)

            @block.vector
            def _(dve):
                dve.memset(hT[:, 0, HK - 1, :], 1.0).then_inc(start, 1)
                dve.memset(hT[:, 1, HK - 1, :], 1.0).then_inc(start, 1)
                dve.wait_ge(start, 2)
                for st in steps(dve, NTILE, 4, 2):
                    if st.on(0):
                        t, j = st.tile(0), st.slot(0, 2)
                        st.again(dve, h_turned, t * 2 - 2)
                        for n in range(HG):
                            dve.wait_ge(gated, t * HG + n + 1)
                            dve.tensor_tensor(h[:, j, n, :], psH[:, n, HW:2 * HW], sg[:, n, :],
                                              ALU.mult).then_inc(h_done, 1)
                    if st.on(1):
                        t, j = st.tile(1), st.slot(1, 2)
                        dve.wait_ge(h_turned, t * 2 + 1)
                        st.again(dve, y_ready, t - 1)
                        dve.tensor_copy(hT[0:HP, j, 0:HB, :],
                                        psG[0:HP, 0, 0:HB * P].rearrange("p (k c) -> p k c", k=HB)).then_inc(hl_out, 1)
                    if st.on(2):
                        t, j = st.tile(2), st.slot(2, 2)
                        dve.wait_ge(y_ready, t + 1)
                        st.again(dve, put[j], st.lap(2, 2) * 16)
                        dve.tensor_scalar(y[:, j, :], psY[:, 0:C], k.wgt[:, ds(t, 1)], None,
                                          ALU.mult).then_inc(y_done, 1)


def program(nc, a, out):
    k = Consts()
    top = Stage(nc, "top")
    with top:
        constants(nc, top, k)
        k.st6 = top.sb("st6", [P, NT, 6])
        k.mv = top.sb("mv", [P, NT, 2])
        k.rstd = top.sb("rstd", [P, NT])
        k.cent = top.sb("cent", [P, KC, E])
        k.tok = top.sb("tok", [P, NTILE], I32)
        k.dst = top.sb("dst", [P, NTILE], I32)
        k.wgt = top.sb("wgt", [P, NTILE])
        k.tile_expert = top.sb("tile_expert", [1, NTILE], I32)
        k.tilebase = top.sb("tilebase", [P, NT])
        tile_bases(nc, k)
        k.xn_d = nc.dram_tensor("normed", [T, C], F32).ap()
        k.y_d = nc.dram_tensor("expert_rows", [2 * T + 2 * P, C], F32).ap()
        k.x2_d = nc.dram_tensor("stream", [T, C], F32).ap()
        k.x2_t = k.x2_d.rearrange("(t p) c -> p t c", p=P)
        k.x3_t = nc.dram_tensor("stream3", [TS, C], F32).ap().rearrange("(t p) c -> p t c", p=P)
        k.v_t = nc.dram_tensor("tangents", [T, C], F32).ap().rearrange("(t p) c -> p t c", p=P)
        res = Stage(nc, "res")
        with res:
            k.x = res.sb("x", [P, NT, C])
            l0 = Stage(nc, "l0")
            with l0:
                k.wqkv = l0.sb("wqkv", [P, KC, 3 * C])
                k.wproj = l0.sb("wproj", [P, KC, C])
                k.gate = l0.sb("gate", [P, KC, E])
                k.w13 = l0.sb("w13", [P, E, KC, 2 * F0])
                k.w2 = l0.sb("w2", [P, E, KC, C])
                k.bproj = l0.sb("bproj", [P, C])
                squares = [(a["L0_attn_Wqkv"][i * C:(i + 1) * C, :], k.wqkv[:, :, i * C:(i + 1) * C]) for i in range(3)]
                squares.append((a["L0_attn_Wproj"], k.wproj[:, :, :]))

                def expert(w):
                    return lambda e: w[ds(e, 1), :, :].rearrange("a r c -> (a r) c")

                def into(w, c0):
                    return lambda e: w[:, ds(e, 1), :, c0:c0 + C].rearrange("p a k c -> p (a k) c")

                transpose_squares(nc, k, "w0", squares, [(a["L0_ffn_gate_w"], k.gate[:, :, :])],
                                  (E, [expert(a[w]) for w in ("L0_ffn_w1", "L0_ffn_w3", "L0_ffn_w2")],
                                   [into(k.w13, 0), into(k.w13, C), into(k.w2, 0)]),
                                  (a["L0_attn_x"], a["L0_attn_bproj"]))
                with Stage(nc, "la") as la:
                    k.qT = la.sb("qT", [P, KC, T])
                    k.kvd = la.sb("kvd", [P, NB, KC, P + H // KC])
                    linear_attention_in(nc, k)
                    linear_attention_out(nc, k)
                route(nc, k, "rt0", 0, k.gate, k.x)
                experts0(nc, k)
            combine_and_log_map(nc, k)
        wide, stacks = Stage(nc, "wide"), Stage(nc, "l1w")
        stacks.__enter__()
        with Stage(nc, "l1") as l1:
            k.w1o = l1.sb("wo", [P, KC, C])
            k.w1qkv = stacks.sb("wqkv", [P, KC, 3 * C], side="right")
            squares = [(a[f"L1_attn_W{n}"], k.w1qkv[:, :, i * C:(i + 1) * C]) for i, n in enumerate("qkv")]
            squares.append((a["L1_attn_Wo"], k.w1o[:, :, :]))
            transpose_squares(nc, k, "w1", squares, [(a["L1_ffn_centroid"], k.cent[:, :, :])])
            for b in range(NB):
                with Stage(nc, f"l1b{b}") as lb:
                    with Stage(nc, f"l1c{b}") as lc:
                        k.V = lc.sb("V", [P, TB, C], side="right")
                        k.QT = lc.sb("QT", [P, H, TS], BF16, side="right")
                        k.KT = lc.sb("KT", [P, H, TS], BF16, side="right")
                        stacked_heads(nc, k, b)
                        k.O = lb.sb("O", [P, TB, C])
                        attention(nc, k, b)
                    if b < NB - 1:
                        u = lb.sb("u", [P, TB, C])
                        attention_out(nc, k, b, u, k.x3_t)
                    else:
                        stacks.close()
                        wide.__enter__()
                        k.wgu = wide.sb("wgu", [P, E, KC, 2, F1], side="right")
                        k.w2b = wide.sb("w2b", [P, E, HK, C], side="right")
                        k.bias = wide.sb("bias", [P, HG * 2 * HW], BF16, side="right")
                        k.pick = wide.sb("pick", [P, E, P], BF16, side="right")
                        k.x = wide.sb("x", [P, NT, C], side="right")
                        k.w_in, k.x_in = wide.sems("win", E), wide.sem("xin")
                        prepare_biases(nc, k, a)

                        def loads(sp):
                            sp.dma_start(k.x[:, 0:TB, :], k.x3_t).then_inc(k.x_in, 16)
                            load_experts(sp, k, a, range(E // 2))

                        attention_out(nc, k, b, k.x[:, TB:NT, :], None, loads)
        route(nc, k, "rt1", 1, k.cent, k.x, lambda sp: load_experts(sp, k, a, range(E // 2, E)))
        experts1(nc, k)
        combine(nc, k, "cb1", out.rearrange("b (t p) c -> p (b t) c", p=P))
        wide.close()


def tile_bases(nc, k):
    with nc.Block() as block:

        @block.vector
        def _(dve):
            dve.tensor_scalar(k.tilebase[:, :], k.lane[:, 0:NT], float(P), None, ALU.mult)


INPUTS = ("L0_attn_x", "L0_attn_Wqkv", "L0_attn_Wproj", "L0_attn_bproj", "L0_ffn_gate_w", "L0_ffn_w1", "L0_ffn_w3",
          "L0_ffn_w2", "L1_attn_Wq", "L1_attn_Wk", "L1_attn_Wv", "L1_attn_Wo", "L1_ffn_centroid", "L1_ffn_Wg",
          "L1_ffn_bg", "L1_ffn_W1", "L1_ffn_b1", "L1_ffn_W2", "L1_ffn_b2")


def kernel(**inputs):
    import concourse.bacc as bacc
    import numpy as np
    from concourse.bass_utils import run_bass_kernel_spmd

    nc = bacc.Bacc("TRN2", target_bir_lowering=False, num_devices=1)
    arrays, args = {}, {}
    for name in INPUTS:
        array = np.ascontiguousarray(inputs[name])
        arrays["in_" + name] = array
        args[name] = nc.dram_tensor("in_" + name, array.shape, mybir.dt.from_np(array.dtype), kind="ExternalInput").ap()
    out = nc.dram_tensor("out", (NB, TS, C), F32, kind="ExternalOutput").ap()
    program(nc, args, out)
    result = run_bass_kernel_spmd(nc, [arrays], core_ids=[0])
    return result.results[0]["out"]
```
